# Optimizing a Trainium2 kernel written in Bass

```python
import numpy as np
import jax
import jax.numpy as jnp

def _softmax(x, axis=-1):
    return jax.nn.softmax(x, axis=axis)

def _gelu(x):
    return jax.nn.gelu(x, approximate=True)

def _silu(x):
    return jax.nn.silu(x)

def _sigmoid(x):
    return jax.nn.sigmoid(x)

def _layernorm(x, axis=-1, eps=1e-05):
    m = jnp.mean(x, axis=axis, keepdims=True)
    v = jnp.var(x, axis=axis, keepdims=True)
    return (x - m) / jnp.sqrt(v + eps)

def _scatter_add(tgt, idx, src, axis=0):
    return tgt.at[idx].add(src)

def _segment_sum(src, seg, n):
    return jax.ops.segment_sum(src, seg, n)
kernel_name = 'mk_adaln_attn_ffn_d1_seqx_r4_dcddb8'

def setup_inputs(seed: int=0):
    np.random.seed(seed)
    _w = jnp.asarray

    def _rec_inputs():
        import jax
        import jax.numpy as jnp
        _rk = jax.random.key(seed)
        x = -0.0001538 + 1 * jax.random.normal(jax.random.fold_in(_rk, 1), (8, 512, 256), jnp.float32)
        _lenS = 512 - jax.random.randint(jax.random.fold_in(_rk, 7), (8,), 0, max(1, 512 // 4) + 1, jnp.int32)
        _lenS2 = 512 - jax.random.randint(jax.random.fold_in(_rk, 8), (8,), 0, max(1, 512 // 4) + 1, jnp.int32)
        cond_1024 = 0.00782532 + 1.00527 * jax.random.normal(jax.random.fold_in(_rk, 11), (8, 256), jnp.float32)
        return (x, cond_1024)
    x, cond_1024 = _rec_inputs()

    def _L0_cond_setup():
        import jax, jax.numpy as jnp
        import numpy as np
        NUM_EXPERTS = 4
        TOP_K = 2
        key = jax.random.key(seed)
        ks = jax.random.split(key, 16)
        B, L, D, E, H = (8, 192, 256, NUM_EXPERTS, 1024)
        s = 0.02
        return {'context_c': jax.random.normal(ks[0], (B, L, D), jnp.float32), 'time_cond': jax.random.normal(ks[1], (B, D), jnp.float32), 'gate_w': jax.random.normal(ks[2], (3 * D, E), jnp.float32) * s, 'gate_b': jnp.zeros((E,), jnp.float32), 'time_w': jax.random.normal(ks[3], (D, 2 * E), jnp.float32) * s, 'time_b': jnp.zeros((2 * E,), jnp.float32), 'ew1': jax.random.normal(ks[4], (E, D, H), jnp.float32) * s, 'eb1': jnp.zeros((E, H), jnp.float32), 'ew2': jax.random.normal(ks[5], (E, H, D), jnp.float32) * s, 'eb2': jnp.zeros((E, D), jnp.float32), 'sw1': jax.random.normal(ks[6], (D, H), jnp.float32) * s, 'sb1': jnp.zeros((H,), jnp.float32), 'sw2': jax.random.normal(ks[7], (H, D), jnp.float32) * s, 'sb2': jnp.zeros((D,), jnp.float32)}
    _L0_cond_all = _L0_cond_setup()
    _L0_cond_in = {k: v for k, v in _L0_cond_all.items() if k in ('gate_w', 'gate_b', 'time_w', 'time_b', 'ew1', 'eb1', 'ew2', 'eb2', 'sw1', 'sb1', 'sw2', 'sb2')}
    del _L0_cond_all

    def _L0_attn_setup():
        import math
        import jax, jax.numpy as jnp
        import numpy as np
        from jax.scipy.special import xlogy, gammaln

        def get_positional_embed(seq_len, feature_size):
            distances = jnp.arange(-seq_len + 1, seq_len, dtype=jnp.float32)
            n = feature_size // 6
            absd = jnp.abs(distances)[:, None]
            max_range = math.log(seq_len) / math.log(2.0)
            half_life = 2.0 ** jnp.linspace(3.0, max_range, n)
            feat_exp = jnp.exp(-math.log(2.0) / half_life[None, :] * absd)
            center_widths = 2.0 ** jnp.arange(1, n + 1, dtype=jnp.float32) - 1.0
            feat_cm = (center_widths[None, :] > absd).astype(jnp.float32)
            stddev = seq_len / (2.0 * n)
            start_mean = seq_len / n
            mean = jnp.linspace(start_mean, float(seq_len), n)[None, :]
            conc = (mean / stddev) ** 2
            rate = mean / stddev ** 2
            log_unnorm = xlogy(conc - 1.0, absd) - rate * absd
            log_norm = gammaln(conc) - conc * jnp.log(rate)
            probs = jnp.exp(log_unnorm - log_norm) + 1e-08
            feat_gamma = probs / jnp.max(probs, axis=-1, keepdims=True)
            emb = jnp.concatenate([feat_exp, feat_cm, feat_gamma], axis=-1)
            emb = jnp.concatenate([emb, jnp.sign(distances)[:, None] * emb], axis=-1)
            return emb

        def relative_shift(x):
            b, h, t1, t2m1 = x.shape
            x = jnp.pad(x, ((0, 0), (0, 0), (0, 0), (1, 0)))
            t2 = t2m1 + 1
            x = x.reshape(b, h, t2, t1)
            x = x[:, :, 1:, :]
            x = x.reshape(b, h, t1, t2 - 1)
            return x[..., :(t2 + 1) // 2]
        key = jax.random.key(seed)
        ks = jax.random.split(key, 9)
        B, L, D = (2, 256, 256)
        H, Dk, Dv = (8, 128, 128)
        R = 192
        sq = math.sqrt(2.0 / (D + Dk))
        sv = math.sqrt(2.0 / (D + Dv))
        return {'q': jax.random.normal(ks[0], (B, L, D), jnp.float32), 'w_qs': jax.random.normal(ks[1], (D, H * Dk), jnp.float32) * sq, 'w_ks': jax.random.normal(ks[2], (D, H * Dk), jnp.float32) * sq, 'w_vs': jax.random.normal(ks[3], (D, H * Dv), jnp.float32) * sv, 'w_rel_pos_k': jax.random.normal(ks[4], (R, H * Dk), jnp.float32) * 0.05, 'rel_embed_bias': jax.random.normal(ks[5], (1, H, 1, Dk), jnp.float32), 'rel_pos_bias': jax.random.normal(ks[6], (1, H, 1, Dk), jnp.float32), 'w_out': jax.random.normal(ks[7], (H * Dv, D), jnp.float32) * 0.02, 'b_out': jax.random.normal(ks[8], (D,), jnp.float32) * 0.02}
    _L0_attn_all = _L0_attn_setup()
    _L0_attn_in = {k: v for k, v in _L0_attn_all.items() if k in ('w_qs', 'w_ks', 'w_vs', 'w_rel_pos_k', 'rel_embed_bias', 'rel_pos_bias', 'w_out', 'b_out')}
    del _L0_attn_all

    def _L0_cond2_setup():
        import jax, jax.numpy as jnp
        import numpy as np
        import math
        N, T, D, H = (64, 128, 256, 256)
        key = jax.random.key(seed)
        k1, k2, k3, k4 = jax.random.split(key, 4)
        x = jax.random.normal(k1, (N, T, D), dtype=jnp.float32)
        h0 = jax.random.normal(k2, (N, H), dtype=jnp.float32)
        Wx = jax.random.normal(k3, (D, 4 * H), dtype=jnp.float32) / math.sqrt(D)
        Wh = jax.random.normal(k4, (H, 4 * H), dtype=jnp.float32) / math.sqrt(H)
        b = jnp.zeros((4 * H,), dtype=jnp.float32)
        return {'x': x, 'h0': h0, 'Wx': Wx, 'Wh': Wh, 'b': b}
    _L0_cond2_all = _L0_cond2_setup()
    _L0_cond2_in = {k: v for k, v in _L0_cond2_all.items() if k in ('Wx', 'Wh', 'b')}
    del _L0_cond2_all

    def _L0_ffn_setup():
        import jax, jax.numpy as jnp
        import numpy as np
        B, S, H, E = (4, 512, 256, 8)
        key = jax.random.key(seed)
        k1, k2, k3 = jax.random.split(key, 3)
        scale = 1.0 / np.sqrt(H)
        return {'x': jax.random.normal(k1, (B, S, H), dtype=jnp.float32), 'router_w': jax.random.normal(k2, (H, E), dtype=jnp.float32) * scale, 'router_b': jnp.zeros((E,), dtype=jnp.float32), 'expert_w': jax.random.normal(k3, (E, H, H), dtype=jnp.float32) * scale, 'expert_b': jnp.zeros((E, H), dtype=jnp.float32)}
    _L0_ffn_all = _L0_ffn_setup()
    _L0_ffn_in = {k: v for k, v in _L0_ffn_all.items() if k in ('router_w', 'router_b', 'expert_w', 'expert_b')}
    del _L0_ffn_all
    return {'x': x, 'cond_1024': cond_1024, 'L0_cond_gate_w': _L0_cond_in['gate_w'], 'L0_cond_gate_b': _L0_cond_in['gate_b'], 'L0_cond_time_w': _L0_cond_in['time_w'], 'L0_cond_time_b': _L0_cond_in['time_b'], 'L0_cond_ew1': _L0_cond_in['ew1'], 'L0_cond_eb1': _L0_cond_in['eb1'], 'L0_cond_ew2': _L0_cond_in['ew2'], 'L0_cond_eb2': _L0_cond_in['eb2'], 'L0_cond_sw1': _L0_cond_in['sw1'], 'L0_cond_sb1': _L0_cond_in['sb1'], 'L0_cond_sw2': _L0_cond_in['sw2'], 'L0_cond_sb2': _L0_cond_in['sb2'], 'L0_attn_w_qs': _L0_attn_in['w_qs'], 'L0_attn_w_ks': _L0_attn_in['w_ks'], 'L0_attn_w_vs': _L0_attn_in['w_vs'], 'L0_attn_w_rel_pos_k': _L0_attn_in['w_rel_pos_k'], 'L0_attn_rel_embed_bias': _L0_attn_in['rel_embed_bias'], 'L0_attn_rel_pos_bias': _L0_attn_in['rel_pos_bias'], 'L0_attn_w_out': _L0_attn_in['w_out'], 'L0_attn_b_out': _L0_attn_in['b_out'], 'L0_cond2_Wx': _L0_cond2_in['Wx'], 'L0_cond2_Wh': _L0_cond2_in['Wh'], 'L0_cond2_b': _L0_cond2_in['b'], 'L0_ffn_router_w': _L0_ffn_in['router_w'], 'L0_ffn_router_b': _L0_ffn_in['router_b'], 'L0_ffn_expert_w': _L0_ffn_in['expert_w'], 'L0_ffn_expert_b': _L0_ffn_in['expert_b']}

def reference(x, cond_1024, L0_cond_gate_w, L0_cond_gate_b, L0_cond_time_w, L0_cond_time_b, L0_cond_ew1, L0_cond_eb1, L0_cond_ew2, L0_cond_eb2, L0_cond_sw1, L0_cond_sb1, L0_cond_sw2, L0_cond_sb2, L0_attn_w_qs, L0_attn_w_ks, L0_attn_w_vs, L0_attn_w_rel_pos_k, L0_attn_rel_embed_bias, L0_attn_rel_pos_bias, L0_attn_w_out, L0_attn_b_out, L0_cond2_Wx, L0_cond2_Wh, L0_cond2_b, L0_ffn_router_w, L0_ffn_router_b, L0_ffn_expert_w, L0_ffn_expert_b):
    import jax
    import jax.numpy as jnp

    def _L0_cond_ref(context_c, time_cond, gate_w, gate_b, time_w, time_b, ew1, eb1, ew2, eb2, sw1, sb1, sw2, sb2):
        import jax, jax.numpy as jnp
        import numpy as np
        NUM_EXPERTS = 4
        TOP_K = 2
        B, L, D = context_c.shape
        E, K = (NUM_EXPERTS, TOP_K)
        L_head = L_wrist = L // 3
        head = context_c[:, :L_head]
        wrist = context_c[:, L_head:L_head + L_wrist]
        proprio = context_c[:, L_head + L_wrist:]
        full_agg = context_c.mean(axis=1)
        hp_agg = jnp.concatenate([head, proprio], axis=1).mean(axis=1)
        wp_agg = jnp.concatenate([wrist, proprio], axis=1).mean(axis=1)
        gate_in = jnp.concatenate([full_agg, hp_agg, wp_agg], axis=-1)
        gate_logits = gate_in @ gate_w + gate_b
        mod = jax.nn.silu(time_cond) @ time_w + time_b
        scale, shift = jnp.split(mod, 2, axis=-1)
        gate_logits = gate_logits * (1.0 + scale) + shift
        gate_scores = jax.nn.softmax(gate_logits, axis=-1)
        topk_w, topk_i = jax.lax.top_k(gate_scores, K)
        topk_w = topk_w / (topk_w.sum(axis=-1, keepdims=True) + 1e-08)
        onehot = (topk_i[..., None] == jnp.arange(E)[None, None, :]).astype(context_c.dtype)
        w_be = jnp.sum(topk_w[..., None] * onehot, axis=1)
        mask = np.ones((E, L), dtype=np.float32)
        mask[1, L_head:L_head + L_wrist] = 0.0
        mask[2, :L_head] = 0.0
        mask = jnp.asarray(mask)
        out = jnp.zeros_like(context_c)
        for e in range(E):
            h = jax.nn.gelu(context_c @ ew1[e] + eb1[e], approximate=True)
            y = h @ ew2[e] + eb2[e]
            out = out + w_be[:, e][:, None, None] * mask[e][None, :, None] * y
        shared = jax.nn.gelu(context_c @ sw1 + sb1, approximate=True) @ sw2 + sb2
        return out + shared

    def _L0_attn_ref(q, w_qs, w_ks, w_vs, w_rel_pos_k, rel_embed_bias, rel_pos_bias, w_out, b_out):
        import math
        import jax, jax.numpy as jnp
        import numpy as np
        from jax.scipy.special import xlogy, gammaln

        def get_positional_embed(seq_len, feature_size):
            distances = jnp.arange(-seq_len + 1, seq_len, dtype=jnp.float32)
            n = feature_size // 6
            absd = jnp.abs(distances)[:, None]
            max_range = math.log(seq_len) / math.log(2.0)
            half_life = 2.0 ** jnp.linspace(3.0, max_range, n)
            feat_exp = jnp.exp(-math.log(2.0) / half_life[None, :] * absd)
            center_widths = 2.0 ** jnp.arange(1, n + 1, dtype=jnp.float32) - 1.0
            feat_cm = (center_widths[None, :] > absd).astype(jnp.float32)
            stddev = seq_len / (2.0 * n)
            start_mean = seq_len / n
            mean = jnp.linspace(start_mean, float(seq_len), n)[None, :]
            conc = (mean / stddev) ** 2
            rate = mean / stddev ** 2
            log_unnorm = xlogy(conc - 1.0, absd) - rate * absd
            log_norm = gammaln(conc) - conc * jnp.log(rate)
            probs = jnp.exp(log_unnorm - log_norm) + 1e-08
            feat_gamma = probs / jnp.max(probs, axis=-1, keepdims=True)
            emb = jnp.concatenate([feat_exp, feat_cm, feat_gamma], axis=-1)
            emb = jnp.concatenate([emb, jnp.sign(distances)[:, None] * emb], axis=-1)
            return emb

        def relative_shift(x):
            b, h, t1, t2m1 = x.shape
            x = jnp.pad(x, ((0, 0), (0, 0), (0, 0), (1, 0)))
            t2 = t2m1 + 1
            x = x.reshape(b, h, t2, t1)
            x = x[:, :, 1:, :]
            x = x.reshape(b, h, t1, t2 - 1)
            return x[..., :(t2 + 1) // 2]
        B, L, _ = q.shape
        H, Dk = (rel_embed_bias.shape[1], rel_embed_bias.shape[3])
        Dv = w_vs.shape[1] // H
        scale = Dk ** (-0.5)
        Q = (q @ w_qs).reshape(B, L, H, Dk).transpose(0, 2, 1, 3) * scale
        K = (q @ w_ks).reshape(B, L, H, Dk).transpose(0, 2, 1, 3)
        V = (q @ w_vs).reshape(B, L, H, Dv).transpose(0, 2, 1, 3)
        attn = jnp.einsum('bnqd,bnkd->bnqk', Q + rel_embed_bias, K)
        positions = get_positional_embed(L, w_rel_pos_k.shape[0])
        rel_k = (positions @ w_rel_pos_k).reshape(-1, H, Dk).transpose(1, 0, 2)
        attn_pos = jnp.einsum('bnqd,nkd->bnqk', Q + rel_pos_bias, rel_k)
        attn_pos = relative_shift(attn_pos)
        a = jax.nn.softmax(attn + attn_pos, axis=-1)
        out = jnp.einsum('bnqk,bnkd->bnqd', a, V)
        out = out.transpose(0, 2, 1, 3).reshape(B, L, H * Dv)
        return out @ w_out + b_out

    def _L0_cond2_ref(x, h0, Wx, Wh, b):
        import jax, jax.numpy as jnp
        import numpy as np
        import math
        N, T, D, H = (64, 128, 256, 256)
        Hdim = h0.shape[1]
        xW = jnp.einsum('ntd,dg->ntg', x, Wx) + b

        def step(carry, xw_t):
            prev_h, prev_c = carry
            a = xw_t + prev_h @ Wh
            i = jax.nn.sigmoid(a[:, :Hdim])
            f = jax.nn.sigmoid(a[:, Hdim:2 * Hdim])
            o = jax.nn.sigmoid(a[:, 2 * Hdim:3 * Hdim])
            g = jnp.tanh(a[:, 3 * Hdim:])
            next_c = f * prev_c + i * g
            next_h = o * jnp.tanh(next_c)
            return ((next_h, next_c), next_h)
        c0 = jnp.zeros_like(h0)
        _, hs = jax.lax.scan(step, (h0, c0), jnp.swapaxes(xW, 0, 1))
        return jnp.swapaxes(hs, 0, 1)

    def _L0_ffn_ref(x, router_w, router_b, expert_w, expert_b):
        import jax, jax.numpy as jnp
        import numpy as np
        B, S, H, E = (4, 512, 256, 8)
        b, s, h = x.shape
        hs = x.reshape(-1, h)
        logits = hs @ router_w + router_b
        probs = jax.nn.softmax(logits, axis=-1)
        idx = jnp.argmax(probs, axis=-1)
        gate = jnp.take_along_axis(probs, idx[:, None], axis=-1)
        expert_out = jnp.einsum('th,ehd->ted', hs, expert_w) + expert_b
        dispatch = jax.nn.one_hot(idx, expert_w.shape[0], dtype=hs.dtype) * gate
        out = jnp.einsum('te,ted->td', dispatch, expert_out)
        return out.reshape(b, s, h)
    x = x + _L0_attn_ref(_L0_cond_ref(x, cond_1024, L0_cond_gate_w, L0_cond_gate_b, L0_cond_time_w, L0_cond_time_b, L0_cond_ew1, L0_cond_eb1, L0_cond_ew2, L0_cond_eb2, L0_cond_sw1, L0_cond_sb1, L0_cond_sw2, L0_cond_sb2), L0_attn_w_qs, L0_attn_w_ks, L0_attn_w_vs, L0_attn_w_rel_pos_k, L0_attn_rel_embed_bias, L0_attn_rel_pos_bias, L0_attn_w_out, L0_attn_b_out)
    x = x + _L0_ffn_ref(_L0_cond2_ref(x, cond_1024, L0_cond2_Wx, L0_cond2_Wh, L0_cond2_b), L0_ffn_router_w, L0_ffn_router_b, L0_ffn_expert_w, L0_ffn_expert_b)
    return x

_drawn_inputs = setup_inputs


def setup_inputs(seed=0):
    import zlib

    import numpy as np

    out = dict(_drawn_inputs(seed))
    spreads = {'L0_cond_gate_b': (0.0, 0.42),
     'L0_cond_time_b': (0.0, 0.288),
     'L0_cond_eb1': (0.0, 0.418),
     'L0_cond_eb2': (0.0, 0.1),
     'L0_cond_sb1': (0.0, 0.334),
     'L0_cond_sb2': (0.0, 0.1),
     'L0_cond2_b': (0.0, 0.411),
     'L0_ffn_router_b': (0.0, 0.309),
     'L0_ffn_expert_b': (0.0, 0.473)}
    factors = {'L0_cond_gate_w': 8.0,
     'L0_attn_w_qs': 25.881,
     'L0_attn_b_out': 2.814,
     'L0_cond2_Wh': 2.837}
    for name, (base, spread) in spreads.items():
        noise = np.random.default_rng([zlib.crc32(name.encode()), seed]).standard_normal(out[name].shape)
        drawn = base * np.exp(spread * noise) if base else spread * noise
        out[name] = jnp.asarray(drawn.astype(out[name].dtype))
    for name, factor in factors.items():
        out[name] = (out[name] * factor).astype(out[name].dtype)
    return out
```

```python
from contextlib import ExitStack

import concourse.bass as bass
from concourse import mybir

F32 = mybir.dt.float32
F32R = mybir.dt.float32r
F16 = mybir.dt.float16
I32 = mybir.dt.int32
ALU = mybir.AluOpType
ACT = mybir.ActivationFunctionType
AX = mybir.AxisListType

P = 128
B, L, D = 8, 512, 256
KD = D // P
EXPERTS, TOP_K, HID = 4, 2, 1024
SHARED = EXPERTS
SLOTS = TOP_K + 1
KH = HID // P
THIRD = L // 3
RANGES = [(0, THIRD), (THIRD, 2 * THIRD), (2 * THIRD, L)]


class Scope:

    def __init__(self, nc, ctx):
        self.nc, self.ctx = nc, ctx

    def sb(self, name, shape, dt=F32):
        return self.ctx.enter_context(self.nc.sbuf_tensor(name, shape, dt))

    def ps(self, name):
        return self.ctx.enter_context(self.nc.psum_tensor(name, [P, 512], F32))

    def sem(self, name):
        return self.ctx.enter_context(self.nc.semaphore(name))


def gating(nc, xT, condT, gate_w, gate_b, time_w, time_b, steps, table_i, table_w):
    with ExitStack() as ctx:
        s = Scope(nc, ctx)
        x_all = s.sb("x_all", [P, KD, B, L])
        gw = s.sb("gw", [P, 3 * KD, EXPERTS])
        tw = s.sb("tw", [P, KD, 2 * EXPERTS])
        gb = s.sb("gb", [1, EXPERTS])
        tb = s.sb("tb", [1, 2 * EXPERTS])
        stp = s.sb("stp", [B, EXPERTS + B])
        cond = s.sb("cond", [P, KD, B])
        csig = s.sb("csig", [P, KD, B])
        csilu = s.sb("csilu", [P, KD, B])
        sums = s.sb("sums", [P, 3, KD, B])
        agg = s.sb("agg", [P, 3, KD, B])
        tmp = s.sb("tmp", [P, KD, B])
        ones = s.sb("ones", [8, P])
        g = s.sb("g", [B, 24, EXPERTS])
        one = s.sb("one", [B, 16])
        vals = s.sb("vals", [B, SLOTS * 4])
        spread = s.sb("spread", [B, B, SLOTS * 4])
        logit_ps, mod_ps, table_ps = s.ps("logit_ps"), s.ps("mod_ps"), s.ps("table_ps")
        small_in, x_in = s.sem("small_in"), s.sem("x_in")
        sig_done, vec, aggs_done, logits_done, spread_done, table_done, exp_done = (
            s.sem(n) for n in ("sig_done", "vec", "aggs_done", "logits_done", "spread_done", "table_done", "exp_done"))
        block = ctx.enter_context(nc.Block())

        @block.sync
        def _(sp):
            sp.dma_start(x_all[:, :, :, :], xT.rearrange("(k p) b l -> p k b l", p=P)).then_inc(x_in, 16)
            sp.dma_start(cond[:, :, :], condT.rearrange("(k p) b -> p k b", p=P)).then_inc(small_in, 16)
            sp.dma_start(gw[:, :, :], gate_w.rearrange("(k p) e -> p k e", p=P)).then_inc(small_in, 16)
            sp.dma_start(tw[:, :, :], time_w.rearrange("(k p) e -> p k e", p=P)).then_inc(small_in, 16)
            sp.dma_start(gb[:, :], gate_b.rearrange("(a e) -> a e", a=1)).then_inc(small_in, 16)
            sp.dma_start(tb[:, :], time_b.rearrange("(a e) -> a e", a=1)).then_inc(small_in, 16)
            sp.dma_start(stp[:, :], steps).then_inc(small_in, 16)

        @block.scalar
        def _(act):
            act.wait_ge(small_in, 96)
            act.activation(csig[:, :, :], cond[:, :, :], ACT.Sigmoid).then_inc(sig_done, 1)
            act.wait_ge(vec, 17)
            act.activation(g[:, 5, :], g[:, 4, :], ACT.Exp, bias=one[:, 0:1],
                           accum_out=one[:, 1:2]).then_inc(exp_done, 1)

        @block.tensor
        def _(pe):
            pe.wait_ge(small_in, 96)
            pe.wait_ge(vec, 2)
            for k in range(KD):
                pe.matmul(mod_ps[0:B, 0:2 * EXPERTS], csilu[:, k, :], tw[:, k, :], start=(k == 0), stop=False)
            pe.matmul(mod_ps[0:B, 0:2 * EXPERTS], ones[0:1, 0:B], tb[:, :], start=False, stop=True)
            pe.wait_ge(aggs_done, 1)
            for j in range(3 * KD):
                pe.matmul(logit_ps[0:B, 0:EXPERTS], agg[:, j // KD, j % KD, :], gw[:, j, :],
                          start=(j == 0), stop=False)
            pe.matmul(logit_ps[0:B, 0:EXPERTS], ones[0:1, 0:B], gb[:, :], start=False,
                      stop=True).then_inc(logits_done, 1)
            pe.wait_ge(spread_done, 1)
            pe.matmul(table_ps[:, 0:B * SLOTS * 4], ones[0:B, :], spread[:, :, :].rearrange("p b n -> p (b n)"),
                      start=True, stop=True).then_inc(table_done, 1)

        @block.vector
        def _(dve):
            done = [0]

            def then(ins):
                done[0] += 1
                ins.then_inc(vec, 1)
                dve.wait_ge(vec, done[0])

            then(dve.memset(ones[:, :], 1.0))
            dve.wait_ge(sig_done, 1)
            then(dve.tensor_tensor(csilu[:, :, :], cond[:, :, :], csig[:, :, :], ALU.mult))
            dve.wait_ge(x_in, 16)
            for r, (a, z) in enumerate(RANGES):
                then(dve.tensor_reduce(sums[:, r, :, :], x_all[:, :, :, a:z], AX.X, ALU.add))
            n_pair = L - THIRD
            then(dve.tensor_tensor(tmp[:, :, :], sums[:, 0, :, :], sums[:, 2, :, :], ALU.add))
            then(dve.tensor_scalar(agg[:, 1, :, :], tmp[:, :, :], 1.0 / n_pair, None, ALU.mult))
            then(dve.tensor_tensor(agg[:, 0, :, :], tmp[:, :, :], sums[:, 1, :, :], ALU.add))
            then(dve.tensor_scalar(agg[:, 0, :, :], agg[:, 0, :, :], 1.0 / L, None, ALU.mult))
            then(dve.tensor_tensor(tmp[:, :, :], sums[:, 1, :, :], sums[:, 2, :, :], ALU.add))
            dve.tensor_scalar(agg[:, 2, :, :], tmp[:, :, :], 1.0 / n_pair, None, ALU.mult).then_inc(aggs_done, 1)
            dve.wait_ge(logits_done, 1)
            then(dve.tensor_scalar(g[:, 0, :], mod_ps[0:B, 0:EXPERTS], 1.0, None, ALU.add))
            then(dve.tensor_copy(g[:, 1, :], mod_ps[0:B, EXPERTS:2 * EXPERTS]))
            then(dve.tensor_tensor(g[:, 2, :], logit_ps[0:B, 0:EXPERTS], g[:, 0, :], ALU.mult))
            then(dve.tensor_tensor(g[:, 4, :], g[:, 2, :], g[:, 1, :], ALU.add))
            then(dve.tensor_reduce(one[:, 2:3], g[:, 4, :], AX.X, ALU.max))
            then(dve.tensor_scalar(one[:, 0:1], one[:, 2:3], -1.0, None, ALU.mult))
            then(dve.memset(vals[:, :], 1.0))
            assert done[0] == 17
            dve.wait_ge(exp_done, 1)
            then(dve.reciprocal(one[:, 3:4], one[:, 1:2]))
            then(dve.tensor_scalar(g[:, 6, :], g[:, 5, :], one[:, 3:4], None, ALU.mult))
            for j in range(TOP_K):
                score = g[:, 6 + j, :]
                top, eq, cand, hot = one[:, 4 + j:5 + j], g[:, 8 + 3 * j, :], g[:, 9 + 3 * j, :], g[:, 10 + 3 * j, :]
                then(dve.tensor_reduce(top, score, AX.X, ALU.max))
                then(dve.tensor_scalar(eq, score, top, None, ALU.is_lt))
                then(dve.scalar_tensor_tensor(out=cand, in0=eq, scalar=8.0, in1=stp[:, 0:EXPERTS],
                                              op0=ALU.mult, op1=ALU.add))
                then(dve.tensor_reduce(vals[:, 4 * j + 3:4 * j + 4], cand, AX.X, ALU.min))
                then(dve.tensor_scalar(hot, stp[:, 0:EXPERTS], vals[:, 4 * j + 3:4 * j + 4], None, ALU.is_equal))
                then(dve.scalar_tensor_tensor(out=g[:, 7 + j, :], in0=hot, scalar=-2.0, in1=score,
                                              op0=ALU.mult, op1=ALU.add) if j == 0 else
                     dve.tensor_tensor(one[:, 6:7], one[:, 4:5], one[:, 5:6], ALU.add))
            then(dve.tensor_scalar(one[:, 7:8], one[:, 6:7], 1e-8, None, ALU.add))
            then(dve.reciprocal(one[:, 8:9], one[:, 7:8]))
            for j in range(TOP_K):
                hot, w = g[:, 10 + 3 * j, :], one[:, 9 + j:10 + j]
                then(dve.tensor_tensor(w, one[:, 4 + j:5 + j], one[:, 8:9], ALU.mult))
                then(dve.tensor_scalar(g[:, 16 + j, :], hot, -1.0, 1.0, ALU.mult, ALU.add))
                then(dve.tensor_tensor(vals[:, 4 * j:4 * j + 1], g[:, 16 + j, 2:3], w, ALU.mult))
                then(dve.tensor_tensor(vals[:, 4 * j + 1:4 * j + 2], g[:, 16 + j, 1:2], w, ALU.mult))
                then(dve.tensor_copy(vals[:, 4 * j + 2:4 * j + 3], w))
            then(dve.memset(vals[:, 4 * TOP_K + 3:4 * TOP_K + 4], float(SHARED)))
            for b in range(B):
                then(dve.tensor_scalar(spread[:, b, :], vals[:, :], stp[:, EXPERTS + b:EXPERTS + b + 1], None,
                                       ALU.mult))
            dve.nop().then_inc(spread_done, 1)
            dve.wait_ge(table_done, 1)
            t = table_ps[:, 0:B * SLOTS * 4].rearrange("p (n c) -> p n c", c=4)
            then(dve.tensor_copy(table_w[:, :].rearrange("p (n c) -> p n c", c=3), t[:, :, 0:3]))
            then(dve.tensor_copy(table_i[0:1, :], t[0:1, :, 3]))


def mixture(nc, xT, w1, w2, biases, table_i, table_w, context):
    GELUS = 4
    with ExitStack() as ctx:
        s = Scope(nc, ctx)
        raw1, raw2 = s.sb("raw1", [P, KD, HID]), s.sb("raw2", [P, KH, D])
        w1h, w1l = s.sb("w1h", [P, KD, HID], F32R), s.sb("w1l", [P, KD, HID], F32R)
        w2h, w2l = s.sb("w2h", [P, KH, D], F32R), s.sb("w2l", [P, KH, D], F32R)
        bias = s.sb("bias", [P, SLOTS, KH + KD])
        weight = s.sb("weight", [P, 3 * SLOTS])
        x_raw = s.sb("x_raw", [P, KD, L])
        x_hi, x_lo = s.sb("x_hi", [P, KD, L], F32R), s.sb("x_lo", [P, KD, L], F32R)
        g = s.sb("gelu", [P, GELUS, L])
        h_hi, h_lo = s.sb("h_hi", [P, KH, L], F32R), s.sb("h_lo", [P, KH, L], F32R)
        y, acc = s.sb("y", [P, KD, L]), s.sb("acc", [P, KD, L])
        split = s.sb("split", [P, 2, KD, L], F32R)
        h_ps = [s.ps(f"h_ps{i}") for i in range(GELUS)]
        y_ps = [s.ps(f"y_ps{i}") for i in range(KD)]
        raw1_in, raw2_in, x_in = s.sem("raw1_in"), s.sem("raw2_in"), s.sem("mix_x_in")
        bias_in = [s.sem(f"bias_in{i}") for i in range(SLOTS)]
        w1_hi_done, w1_done, w2_hi_done, w2_done = (
            s.sem(n) for n in ("w1_hi_done", "w1_done", "w2_hi_done", "w2_done"))
        x_hi_done, x_done = s.sem("x_hi_done"), s.sem("x_done")
        h_full, gelu_done, hi_done, lo_done = (s.sem(n) for n in ("h_full", "gelu_done", "hi_done", "lo_done"))
        y_full, y_out, y_used, acc_done = (s.sem(n) for n in ("y_full", "y_out", "y_used", "acc_done"))
        split_hi_done, split_done, context_out, context_free = (
            s.sem(n) for n in ("split_hi_done", "split_done", "context_out", "context_free"))
        block = ctx.enter_context(nc.Block())

        @block.sync
        def _(sp):
            with sp.Fori(0, B) as b:
                sp.wait_ge(x_done, b + 1)
                sp.dma_start(x_raw[:, :, :],
                             xT[:, bass.ds(b, 1), :].rearrange("(k p) b l -> p k (b l)", p=P)).then_inc(x_in, 16)
                for slot in range(SLOTS):
                    k = SLOTS * b + slot
                    e = sp.value_load(table_i[0:1, bass.ds(k, 1)], min_val=0, max_val=SHARED)
                    sp.wait_ge(w1_done, k + 1)
                    sp.dma_start(raw1[:, :, :], w1[bass.ds(e, 1)].rearrange("e (k p) n -> p (e k) n", p=P)
                                 ).then_inc(raw1_in, 16)
                    sp.dma_start(bias[:, slot, :], biases[bass.ds(e, 1)].rearrange("e p n -> p (e n)")
                                 ).then_inc(bias_in[slot], 16)
                    sp.wait_ge(w2_done, k + 1)
                    sp.dma_start(raw2[:, :, :], w2[bass.ds(e, 1)].rearrange("e (k p) n -> p (e k) n", p=P)
                                 ).then_inc(raw2_in, 16)
            sp.wait_ge(context_out, 16 * B)

        @block.tensor
        def _(pe):
            with pe.Fori(0, B) as b:
                for slot in range(SLOTS):
                    k = SLOTS * b + slot
                    pe.wait_ge(w1_done, k + 2)
                    if slot == 0:
                        pe.wait_ge(x_done, b + 2)
                    for oc in range(KH):
                        pe.wait_ge(gelu_done, KH * k + oc + 1)
                        for n, (w, x) in enumerate(((w1h, x_hi), (w1h, x_lo), (w1l, x_hi))):
                            for c in range(KD):
                                mm = pe.matmul(h_ps[oc % GELUS][:, :], w[:, c, oc * P:(oc + 1) * P], x[:, c, :],
                                               start=(n == 0 and c == 0), stop=(n == 2 and c == KD - 1))
                        mm.then_inc(h_full, 1)
                    pe.wait_ge(w2_done, k + 2)
                    pe.wait_ge(y_out, KD * k + KD)
                    for c in range(KH):
                        pe.wait_ge(lo_done, KH * k + c + 1 + GELUS)
                        for oc in range(KD):
                            for n, (w, h) in enumerate(((w2h, h_hi), (w2h, h_lo), (w2l, h_hi))):
                                mm = pe.matmul(y_ps[oc][:, :], w[:, c, oc * P:(oc + 1) * P], h[:, c, :],
                                               start=(c == 0 and n == 0), stop=(c == KH - 1 and n == 2))
                            if c == KH - 1:
                                mm.then_inc(y_full, 1)

        @block.scalar
        def _(act):
            act.nop().then_inc(gelu_done, GELUS)
            act.nop().then_inc(y_out, KD)
            with act.Fori(0, B) as b:
                for slot in range(SLOTS):
                    k = SLOTS * b + slot
                    act.wait_ge(bias_in[slot], 16 * b + 16)
                    for oc in range(KH):
                        n = KH * k + oc
                        act.wait_ge(h_full, n + 1)
                        act.wait_ge(lo_done, n + 1)
                        act.activation(g[:, oc % GELUS, :], h_ps[oc % GELUS][:, :], ACT.Gelu_apprx_tanh,
                                       bias=bias[:, slot, oc:oc + 1]).then_inc(gelu_done, 1)
                        act.wait_ge(gelu_done, n + 1 + GELUS)
                        act.copy(h_hi[:, oc, :], g[:, oc % GELUS, :]).then_inc(hi_done, 1)
                    act.wait_ge(y_used, k + 1)
                    for oc in range(KD):
                        act.wait_ge(y_full, KD * k + oc + 1)
                        act.activation(y[:, oc, :], y_ps[oc][:, :], ACT.Identity,
                                       bias=bias[:, slot, KH + oc:KH + oc + 1]).then_inc(y_out, 1)

        @block.gpsimd
        def _(pool):
            pool.nop().then_inc(context_free, 1)
            with pool.Fori(0, B) as b:
                pool.wait_ge(split_done, b + 1)
                pool.dma_start(context[bass.ds(b, 1)].rearrange("b p s k l -> p (b s k l)"),
                               split[:, :, :, :].rearrange("p s k l -> p (s k l)").bitcast(F32)
                               ).then_inc(context_out, 16)
                pool.wait_ge(context_out, 16 * b + 16)
                pool.nop().then_inc(context_free, 1)

        @block.vector
        def _(dve):
            dve.nop().then_inc(lo_done, GELUS)
            for free in (y_used, w1_done, w2_done, x_done):
                dve.nop().then_inc(free, 1)

            def split_x(b):
                dve.wait_ge(x_in, 16 * b + 16)
                dve.tensor_copy(x_hi[:, :, :], x_raw[:, :, :]).then_inc(x_hi_done, 1)
                dve.wait_ge(x_hi_done, b + 1)
                dve.tensor_tensor(x_lo[:, :, :], x_raw[:, :, :], x_hi[:, :, :].bitcast(F32),
                                  ALU.subtract).then_inc(x_done, 1)

            def split_w(k, raw, hi, lo, came, hi_split, done):
                dve.wait_ge(came, 16 * k + 16)
                dve.tensor_copy(hi[:, :, :], raw[:, :, :]).then_inc(hi_split, 1)
                dve.wait_ge(hi_split, k + 1)
                dve.tensor_tensor(lo[:, :, :], raw[:, :, :], hi[:, :, :].bitcast(F32),
                                  ALU.subtract).then_inc(done, 1)

            def batch(b, last):
                dve.tensor_copy(weight[:, :], table_w[:, bass.ds(9 * b, 9)]).then_inc(acc_done, 1)
                for slot in range(SLOTS):
                    k = SLOTS * b + slot
                    split_w(k, raw2, w2h, w2l, raw2_in, w2_hi_done, w2_done)
                    for oc in range(KH):
                        dve.wait_ge(hi_done, KH * k + oc + 1)
                        dve.tensor_tensor(h_lo[:, oc, :], g[:, oc % GELUS, :], h_hi[:, oc, :].bitcast(F32),
                                          ALU.subtract).then_inc(lo_done, 1)
                    if not last or slot < SLOTS - 1:
                        if slot == SLOTS - 1:
                            split_x(b + 1)
                        split_w(k + 1, raw1, w1h, w1l, raw1_in, w1_hi_done, w1_done)
                    dve.wait_ge(y_out, KD * k + 2 * KD)
                    dve.wait_ge(acc_done, 6 * b + 1 + 2 * slot)
                    dve.wait_ge(y_used, k + 1)
                    if slot < TOP_K:
                        for r, (a, z) in enumerate(RANGES):
                            w = weight[:, 3 * slot + r:3 * slot + r + 1]
                            if slot == 0:
                                ins = dve.tensor_scalar(acc[:, :, a:z], y[:, :, a:z], w, None, ALU.mult)
                            else:
                                ins = dve.scalar_tensor_tensor(out=acc[:, :, a:z], in0=y[:, :, a:z], scalar=w,
                                                               in1=acc[:, :, a:z], op0=ALU.mult, op1=ALU.add)
                            ins.then_inc(y_used if r == 2 else acc_done, 1)
                        continue
                    dve.tensor_tensor(acc[:, :, :], y[:, :, :], acc[:, :, :], ALU.add).then_inc(y_used, 1)
                    dve.wait_ge(y_used, k + 2)
                    dve.wait_ge(context_free, b + 1)
                    dve.tensor_copy(split[:, 0, :, :], acc[:, :, :]).then_inc(split_hi_done, 1)
                    dve.wait_ge(split_hi_done, b + 1)
                    dve.tensor_tensor(split[:, 1, :, :], acc[:, :, :], split[:, 0, :, :].bitcast(F32),
                                      ALU.subtract).then_inc(split_done, 1)
                    dve.wait_ge(split_done, b + 1)
                    dve.nop().then_inc(acc_done, 1)

            split_x(0)
            split_w(0, raw1, w1h, w1l, raw1_in, w1_hi_done, w1_done)
            with dve.Fori(0, B - 1) as b:
                batch(b, False)
            batch(B - 1, True)


HEADS, DK = 8, 128
PAIRS = HEADS // 2
QT = L // P
KT = L // P
FEATS = 192
FP = FEATS // 2
DIST = 2 * L
WIN = L + P
HALF_WIN = WIN // 2
SCALE = float(DK) ** -0.5

REL = ["rel0", "rel1", "rel2", "rel3"]
EVEN = ["q0", "k0", "out0", "out1", "s0.0", "s0.1", "s0.2", "s0.3", "val0", "t0.0", "t0.1", "t0.2", "t0.3"]
ODD = ["q1", "k1", "val1", "s1.0", "s1.1", "s1.2", "s1.3", "v0", "v1", "t1.0", "t1.1", "t1.2", "t1.3"]
RING = [4, 5, 3, 2, 1, 0, 4, 5, 2, 3, 1, 0, 4, 2, 5, 1, 3, 0, 4, 2, 1, 5, 3, 0, 2, 1]
BANK = dict(zip(EVEN + ODD, RING), rel0=4, rel1=5, rel2=3, rel3=0, last0=4, last1=5)


class Step:

    def __init__(self, hp, bb, odd, leave_out=(), before=None):
        self.pair_start = isinstance(bb, int)
        rel = REL if self.pair_start and odd == 0 else []
        names = rel + EVEN + ODD
        self.items = [n for n in names if n not in leave_out]
        self.hp, self.bb, self.odd = hp, bb, odd
        self.g, self.m = B * hp + 2 * bb + odd, B // 2 * hp + bb
        self.b = 2 * bb + odd
        self.before = before if before is not None else EVEN + ODD

    def number(self, base, name):
        return base + self.items.index(name)


def takes_high(name):
    return name[0] != "s" and not name.startswith(("out", "last"))


def attention(nc, xT, wqkvo, wrel, positions, qbias, b_out, identity, context, skew, x1):
    with ExitStack() as ctx:
        s = Scope(nc, ctx)
        part = s.sb("part", [P, 2, 2, KD, L], F32R)
        raw_w, raw_rel = s.sb("raw_w", [P, 4, L]), s.sb("raw_rel", [FP, 2, 2 * DK])
        raw_qb = s.sb("raw_qb", [P, 4])
        pos = s.sb("pos", [FP, 4, L])
        wh, wl = s.sb("wh", [P, 4, L], F32R), s.sb("wl", [P, 4, L], F32R)
        rel_h, rel_l = s.sb("rel_h", [P, 2, DIST], F32R), s.sb("rel_l", [P, 2, DIST], F32R)
        qb = s.sb("qb", [P, 4])
        bo = s.sb("bo", [P, KD])
        ident = s.sb("ident", [P, P])
        prob = s.sb("prob", [P, 8, L])
        qe_h, qe_l = s.sb("qe_h", [P, 2, L], F32R), s.sb("qe_l", [P, 2, L], F32R)
        qp_h, qp_l = s.sb("qp_h", [P, L], F32R), s.sb("qp_l", [P, L], F32R)
        k_h, k_l = s.sb("k_h", [P, 2, L], F32R), s.sb("k_l", [P, 2, L], F32R)
        v_h, v_l = s.sb("v_h", [P, KT, 2 * DK], F32R), s.sb("v_l", [P, KT, 2 * DK], F32R)
        pt_h, pt_l = s.sb("pt_h", [P, KT, L], F32R), s.sb("pt_l", [P, KT, L], F32R)
        o_h, o_l = s.sb("o_h", [P, 2, L], F32R), s.sb("o_l", [P, 2, L], F32R)
        dist = s.sb("dist", [P, QT, WIN])
        nmax, total, rinv = s.sb("nmax", [P, 8]), s.sb("total", [P, 8]), s.sb("rinv", [P, 8])
        banks = [s.ps(f"bank{i}") for i in range(6)]
        dist_ps = [s.ps(f"dist_ps{i}") for i in range(2)]

        x1_in, x1_ready, const_in, pair_in = s.sem("x1_in"), s.sem("x1_ready"), s.sem("const2_in"), s.sem("pair_in")
        w_hi_done, w_done, wo_hi_done, wo_done, bias_ready = (
            s.sem(n) for n in ("w_hi_done", "w_done", "wo_hi_done", "wo_done", "bias_ready"))
        part_in = [s.sem(f"part_in{i}") for i in range(2)]
        item_full, high_done, freed = s.sem("item_full"), s.sem("high_done"), s.sem("freed")
        dist_full, dist_left, dist_right = s.sem("dist_full"), s.sem("dist_left"), s.sem("dist_right")
        stored = [s.sem(f"stored{i}") for i in range(QT)]
        skewed = [s.sem(f"skewed{i}") for i in range(8)]
        scores_seen, exp_done, rinv_done, prob_done = (
            s.sem(n) for n in ("scores_seen", "exp_done", "rinv_done", "prob_done"))
        block = ctx.enter_context(nc.Block())

        start = [n for n in EVEN if n not in ("q0", "k0")] + ["val1"]
        step0 = Step(0, 0, 0, leave_out=start, before=[])
        step1 = Step(0, 0, 1, leave_out=("out0", "out1"), before=step0.items)
        after = Step(PAIRS, 0, 0)
        after.items = ["out0", "out1"] + EVEN[4:] + ["val1", "last0", "last1"]

        def bases(keep):
            size = [sum(map(keep, x.items)) for x in (step0, step1)]
            full, rel = sum(map(keep, EVEN + ODD)), sum(map(keep, REL))

            def base(step):
                if step is step0:
                    return 0
                if step is step1:
                    return size[0]
                rest = size[0] + size[1] + full * (step.g - 2) + rel * step.hp
                return rest - rel if step.items[0] in (REL[0], "out0") else rest
            return base

        item_base, high_base = bases(lambda n: True), bases(takes_high)

        def item(step, name):
            return item_base(step) + step.items.index(name)

        def high(step, name):
            return high_base(step) + [n for n in step.items if takes_high(n)].index(name)

        def user_before(step, name):
            i = step.items.index(name)
            order = step.before + step.items[:i]
            for back, other in enumerate(reversed(order)):
                if BANK[other] == BANK[name]:
                    return item(step, name) - 1 - back
            return None

        def steps(eng, step, finish):
            step(step0)
            step(step1)
            with eng.Fori(1, B // 2) as bb:
                step(Step(0, bb, 0))
                step(Step(0, bb, 1))
            with eng.Fori(1, PAIRS) as hp:
                step(Step(hp, 0, 0))
                step(Step(hp, 0, 1))
                with eng.Fori(1, B // 2) as bb:
                    step(Step(hp, bb, 0))
                    step(Step(hp, bb, 1))
            finish(after)

        @block.sync
        def _(sp):
            def load_pair(hp):
                sp.dma_start(raw_rel[:, :, :], wrel[bass.ds(hp, 1)].rearrange("h p m n -> p (h m) n")
                             ).then_inc(pair_in, 16)
                sp.dma_start(raw_qb[:, :], qbias[bass.ds(hp, 1)].rearrange("h p n -> p (h n)")).then_inc(pair_in, 16)
                sp.dma_start(raw_w[:, :, :], wqkvo[bass.ds(hp, 1)].rearrange("h p m n -> p (h m) n")
                             ).then_inc(pair_in, 16)

            def load_part(b, odd):
                sp.dma_start(part[:, odd, :, :, :].rearrange("p s k l -> p (s k l)").bitcast(F32),
                             context[bass.ds(b, 1)].rearrange("b p s k l -> p (b s k l)")).then_inc(part_in[odd], 16)

            def skew_unit(at, h):
                n = 2 * at.g + h

                def load(q):
                    sp.wait_ge(stored[q], 16 * n + 16)
                    src = bass.AP(tensor=skew.tensor, offset=(4 * h + q) * P * WIN + P - 1,
                                  ap=[[WIN - 1, P], [1, L]])
                    sp.dma_start(prob[:, 4 * h + q, :], src).then_inc(skewed[4 * h + q], 16)

                for q in range(QT):
                    sp.wait_ge(dist_left, QT * n + q + 1)
                    sp.wait_ge(dist_right, QT * n + q + 1)
                    dst = bass.AP(tensor=skew.tensor, offset=(4 * h + q) * P * WIN, ap=[[WIN, P], [1, WIN]])
                    sp.dma_start(dst, dist[:, q, :]).then_inc(stored[q], 16)
                    if q:
                        load(q - 1)
                load(QT - 1)

            def step(at):
                skew_unit(at, 0)
                skew_unit(at, 1)
                sp.wait_ge(item_full, item(at, "v1") + 1)
                load_part((at.b + 2) % B, at.odd)
                if at.pair_start and at.odd == 1:
                    sp.wait_ge(wo_done, at.hp + 1)
                    load_pair((at.hp + 1) % PAIRS)

            sp.dma_start(pos[:, :, :], positions).then_inc(const_in, 16)
            load_pair(0)
            load_part(0, 0)
            sp.dma_start(ident[:, :], identity).then_inc(const_in, 16)
            load_part(1, 1)
            sp.dma_start(bo[:, :], b_out).then_inc(const_in, 16)
            sp.dma_start(x1[:, :, :, :], xT.rearrange("(k p) b l -> p k b l", p=P)).then_inc(x1_in, 16)
            steps(sp, step, lambda at: None)
            for i in range(2):
                sp.wait_ge(part_in[i], 16 * (PAIRS * B // 2 + 1))
            sp.wait_ge(pair_in, 48 * (PAIRS + 1))

        @block.tensor
        def _(pe):
            def product(out, terms, start=True, stop=True):
                for i, (a, x) in enumerate(terms):
                    mm = pe.matmul(out, a, x, start=start and i == 0, stop=stop and i == len(terms) - 1)
                return mm

            def passes(ah, al, mh, ml):
                return ((ah, mh), (ah, ml), (al, mh))

            def take_bank(at, name):
                free = user_before(at, name)
                if free is not None:
                    pe.wait_ge(freed, free + 1)
                return banks[BANK[name]]

            def distance_keys(at):
                pe.wait_ge(pair_in, 48 * at.hp + 48)
                if at is step0:
                    pe.wait_ge(const_in, 48)
                for h in range(2):
                    for half in range(2):
                        bank = take_bank(at, f"rel{2 * h + half}")
                        terms = [(raw_rel[:, k, h * DK:(h + 1) * DK], pos[:, 2 * k + half, :]) for k in range(2)]
                        product(bank[:, :], terms).then_inc(item_full, 1)

            def w(m, k, a, z):
                return wh[:, m, 2 * DK * k + a:2 * DK * k + z], wl[:, m, 2 * DK * k + a:2 * DK * k + z]

            def project_qk(at, h):
                if h == 0:
                    pe.wait_ge(part_in[at.odd], 16 * at.m + 16)
                for m, name in enumerate((f"q{h}", f"k{h}")):
                    bank = take_bank(at, name)
                    terms = []
                    for k in range(KD):
                        terms += passes(*w(m, k, h * DK, (h + 1) * DK), part[:, at.odd, 0, k, :],
                                        part[:, at.odd, 1, k, :])
                    product(bank[:, :], terms).then_inc(item_full, 1)

            def v_tile(at, t):
                bank = take_bank(at, f"v{t // 2}") if t % 2 == 0 else banks[BANK[f"v{t // 2}"]]
                rows = slice(t * P, (t + 1) * P)
                terms = []
                for k in range(KD):
                    wkh, wkl = w(2, k, 0, 2 * DK)
                    ch, cl = part[:, at.odd, 0, k, rows], part[:, at.odd, 1, k, rows]
                    terms += ((ch, wkh), (ch, wkl), (cl, wkh))
                mm = product(bank[:, (t % 2) * 2 * DK:(t % 2 + 1) * 2 * DK], terms)
                if t % 2:
                    mm.then_inc(item_full, 1)

            def values_part(at, h, k):
                name = f"val{h}"
                bank = take_bank(at, name) if k == 0 else banks[BANK[name]]
                cols = slice(h * DK, (h + 1) * DK)
                mm = product(bank[:, :], passes(v_h[:, k, cols], v_l[:, k, cols], pt_h[:, k, :], pt_l[:, k, :]),
                             start=(k == 0), stop=(k == KT - 1))
                if k == KT - 1:
                    mm.then_inc(item_full, 1)

            def values(at, h):
                for k in range(KT):
                    values_part(at, h, k)

            def scores(at, slot):
                h = 1 - slot
                for q in range(QT):
                    bank = take_bank(at, f"s{slot}.{q}")
                    cols = slice(q * P, (q + 1) * P)
                    product(bank[:, :], passes(qe_h[:, h, cols], qe_l[:, h, cols], k_h[:, h, :], k_l[:, h, :])
                            ).then_inc(item_full, 1)

            def distances(at, h, between):
                n = 2 * at.g + h
                pe.wait_ge(freed, item(at, f"q{h}") + 1)
                for q in range(QT):
                    cols = slice(q * P, (q + 1) * P)
                    for half, left in enumerate((dist_left, dist_right)):
                        if at is not step0 or 2 * n + q > 0:
                            pe.wait_ge(left, QT * n + q)
                        a = L - P - q * P + half * HALF_WIN
                        product(dist_ps[half][:, 0:HALF_WIN],
                                passes(qp_h[:, cols], qp_l[:, cols], rel_h[:, h, a:a + HALF_WIN],
                                       rel_l[:, h, a:a + HALF_WIN])).then_inc(dist_full, 1)
                    between(q)

            def transposes(at, slot):
                h, n = 1 - slot, 2 * at.g + slot - 1
                for q in range(QT):
                    bank = take_bank(at, f"t{slot}.{q}")
                    pe.wait_ge(prob_done, QT * n + q + 1)
                    for k in range(KT):
                        mm = pe.transpose(bank[:, k * P:(k + 1) * P], prob[:, 4 * h + q, k * P:(k + 1) * P],
                                          ident[:, :])
                    mm.then_inc(item_full, 1)

            def project_out(at, names):
                for oc, name in enumerate(names):
                    bank = take_bank(at, name)
                    terms = []
                    for h in range(2):
                        cols = slice(2 * DK * h + oc * P, 2 * DK * h + (oc + 1) * P)
                        terms += passes(wh[:, 3, cols], wl[:, 3, cols], o_h[:, h, :], o_l[:, h, :])
                    product(bank[:, :], terms).then_inc(item_full, 1)

            def split_before(at, name):
                pe.wait_ge(freed, item_base(at) - len(at.before) + at.before.index(name) + 1)

            def step(at):
                if "rel0" in at.items:
                    distance_keys(at)
                    pe.wait_ge(w_done, 2 * at.hp + 2)
                project_qk(at, 0)
                if "out0" in at.items:
                    if not at.pair_start:
                        pe.wait_ge(wo_done, at.hp + 1)
                    split_before(at, "val1")
                    project_out(at, ("out0", "out1"))
                if "s0.0" in at.items:
                    split_before(at, "k1")
                    scores(at, 0)
                    split_before(at, "t1.3")
                    distances(at, 0, lambda q: values_part(at, 0, q))
                    transposes(at, 0)
                else:
                    pe.wait_ge(freed, item(at, "rel3") + 1)
                    distances(at, 0, lambda q: None)
                project_qk(at, 1)
                if "val1" in at.items:
                    pe.wait_ge(freed, item(at, "t0.3") + 1)
                    values(at, 1)
                pe.wait_ge(freed, item(at, "k0") + 1)
                scores(at, 1)
                distances(at, 1, lambda q: v_tile(at, q))
                transposes(at, 1)

            def finish(at):
                split_before(at, "val1")
                project_out(at, ("out0", "out1"))
                scores(at, 0)
                split_before(at, "t1.3")
                values(at, 0)
                transposes(at, 0)
                pe.wait_ge(freed, item(at, "t0.3") + 1)
                values(at, 1)
                pe.wait_ge(freed, item(at, "val1") + 1)
                project_out(at, ("last0", "last1"))

            steps(pe, step, finish)

        @block.scalar
        def _(act):
            def split_weights(hp):
                act.wait_ge(pair_in, 48 * hp + 48)
                act.activation(wh[:, 0, :], raw_w[:, 0, :], ACT.Copy, scale=SCALE).then_inc(w_hi_done, 1)
                act.activation(wh[:, 1:3, :].rearrange("p m n -> p (m n)"),
                               raw_w[:, 1:3, :].rearrange("p m n -> p (m n)"), ACT.Copy).then_inc(w_hi_done, 1)

            def take(at, name, dst, view=lambda a: a):
                act.wait_ge(item_full, item(at, name) + 1)
                act.copy(dst, view(banks[BANK[name]][:, :])).then_inc(high_done, 1)

            def take_qk(at, h):
                act.wait_ge(item_full, item(at, f"q{h}") + 1)
                if "rel0" in at.items and h == 0:
                    act.wait_ge(bias_ready, at.hp + 1)
                bank = banks[BANK[f"q{h}"]]
                act.activation(qe_h[:, h, :], bank[:, :], ACT.Identity, bias=qb[:, h:h + 1])
                act.activation(qp_h[:, :], bank[:, :], ACT.Identity, bias=qb[:, 2 + h:3 + h]).then_inc(high_done, 1)
                take(at, f"k{h}", k_h[:, h, :])

            def exponentials(at, slot, q):
                h, n = 1 - slot, 2 * at.g + slot - 1
                i = 4 * h + q
                act.wait_ge(freed, item(at, f"s{slot}.{q}") + 1)
                act.activation(prob[:, i, :], prob[:, i, :], ACT.Exp, scale=-1.0, bias=nmax[:, i:i + 1],
                               accum_out=total[:, i:i + 1]).then_inc(exp_done, 1)

            def left_half(at, h, q):
                n = 2 * at.g + h
                if at is not step0 or n > 0:
                    act.wait_ge(stored[q], 16 * n)
                act.wait_ge(dist_full, 2 * QT * n + 2 * q + 1)
                act.copy(dist[:, q, 0:HALF_WIN], dist_ps[0][:, 0:HALF_WIN]).then_inc(dist_left, 1)

            def take_v(at, i):
                take(at, f"v{i}", v_h[:, 2 * i:2 * i + 2, :], lambda a: a.rearrange("p (t n) -> p t n", t=2))

            def take_transposed(at, slot):
                for q in range(QT):
                    take(at, f"t{slot}.{q}", pt_h[:, :, q * P:(q + 1) * P],
                         lambda a: a.rearrange("p (k n) -> p k n", k=KT))

            def slot(at, h, has_scores, after_tile):
                for q in range(QT):
                    if has_scores:
                        for e in {0: (0, 1), 1: (2,), 2: (3,), 3: ()}[q]:
                            exponentials(at, h, e)
                    if q == 2:
                        after_tile(0)
                    left_half(at, h, q)
                after_tile(1)

            def step(at):
                if "rel0" in at.items:
                    split_weights(at.hp)
                    for i, name in enumerate(REL):
                        take(at, name, rel_h[:, i // 2, (i % 2) * L:(i % 2 + 1) * L])
                take_qk(at, 0)
                before = "s0.0" in at.items
                slot(at, 0, before, lambda i: None)
                if before:
                    take(at, "val0", o_h[:, 0, :])
                    take_transposed(at, 0)
                take_qk(at, 1)
                if "val1" in at.items:
                    take(at, "val1", o_h[:, 1, :])
                slot(at, 1, True, lambda i: take_v(at, i))
                take_transposed(at, 1)
                if at.pair_start and at.odd == 1:
                    act.copy(wh[:, 3, :], raw_w[:, 3, :]).then_inc(wo_hi_done, 1)

            def finish(at):
                for q in range(QT):
                    exponentials(at, 0, q)
                take(at, "val0", o_h[:, 0, :])
                take_transposed(at, 0)
                take(at, "val1", o_h[:, 1, :])

            steps(act, step, finish)

        @block.gpsimd
        def _(pool):
            with pool.Fori(0, PAIRS * B) as g:
                for h in range(2):
                    for q in range(QT):
                        i = 4 * h + q
                        pool.wait_ge(rinv_done, QT * (2 * g + h) + q + 1)
                        pool.tensor_tensor(prob[:, i, :], prob[:, i, :], rinv[:, i:i + 1].to_broadcast([P, L]),
                                           ALU.mult).then_inc(prob_done, 1)

        @block.vector
        def _(dve):
            def split_weights(hp):
                dve.wait_ge(pair_in, 48 * hp + 48)
                dve.tensor_copy(qb[:, :], raw_qb[:, :]).then_inc(bias_ready, 1)
                dve.wait_ge(w_hi_done, 2 * hp + 1)
                dve.scalar_tensor_tensor(out=wl[:, 0, :], in0=raw_w[:, 0, :], scalar=SCALE,
                                         in1=wh[:, 0, :].bitcast(F32), op0=ALU.mult, op1=ALU.subtract
                                         ).then_inc(w_done, 1)
                dve.wait_ge(w_hi_done, 2 * hp + 2)
                dve.tensor_tensor(wl[:, 1:3, :], raw_w[:, 1:3, :], wh[:, 1:3, :].bitcast(F32), ALU.subtract
                                  ).then_inc(w_done, 1)
                dve.wait_ge(bias_ready, hp + 1)

            def take(at, name, lo, hi, view=lambda a: a):
                dve.wait_ge(high_done, high(at, name) + 1)
                dve.tensor_tensor(lo, view(banks[BANK[name]][:, :]), hi.bitcast(F32), ALU.subtract).then_inc(freed, 1)

            def take_qk(at, h):
                dve.wait_ge(high_done, high(at, f"q{h}") + 1)
                bank = banks[BANK[f"q{h}"]]
                dve.scalar_tensor_tensor(out=qe_l[:, h, :], in0=bank[:, :], scalar=qb[:, h:h + 1],
                                         in1=qe_h[:, h, :].bitcast(F32), op0=ALU.add, op1=ALU.subtract)
                dve.scalar_tensor_tensor(out=qp_l[:, :], in0=bank[:, :], scalar=qb[:, 2 + h:3 + h],
                                         in1=qp_h[:, :].bitcast(F32), op0=ALU.add, op1=ALU.subtract
                                         ).then_inc(freed, 1)
                take(at, f"k{h}", k_l[:, h, :], k_h[:, h, :])

            def logits(at, slot, q):
                h, m = 1 - slot, at.g + slot - 1
                i = 4 * h + q
                dve.wait_ge(skewed[i], 16 * m + 16 if slot == 0 else 16 * at.g + 16)
                dve.wait_ge(item_full, item(at, f"s{slot}.{q}") + 1)
                dve.nop().then_inc(scores_seen, 1)
                dve.tensor_tensor_reduce(out=prob[:, i, :], in0=banks[BANK[f"s{slot}.{q}"]][:, :],
                                         in1=prob[:, i, :], scale=-1.0, scalar=3.0e38, op0=ALU.add, op1=ALU.min,
                                         accum_out=nmax[:, i:i + 1]).then_inc(freed, 1)

            def inverse(at, slot, q):
                h, n = 1 - slot, 2 * at.g + slot - 1
                i = 4 * h + q
                dve.wait_ge(exp_done, QT * n + q + 1)
                dve.reciprocal(rinv[:, i:i + 1], total[:, i:i + 1]).then_inc(rinv_done, 1)

            def right_half(at, h, q):
                n = 2 * at.g + h
                if at is not step0 or n > 0:
                    dve.wait_ge(stored[q], 16 * n)
                dve.wait_ge(dist_full, 2 * QT * n + 2 * q + 2)
                dve.tensor_copy(dist[:, q, HALF_WIN:WIN], dist_ps[1][:, 0:HALF_WIN]).then_inc(dist_right, 1)

            def take_v(at, i):
                take(at, f"v{i}", v_l[:, 2 * i:2 * i + 2, :], v_h[:, 2 * i:2 * i + 2, :],
                     lambda a: a.rearrange("p (t n) -> p t n", t=2))

            def take_transposed(at, slot):
                for q in range(QT):
                    cols = slice(q * P, (q + 1) * P)
                    take(at, f"t{slot}.{q}", pt_l[:, :, cols], pt_h[:, :, cols],
                         lambda a: a.rearrange("p (k n) -> p k n", k=KT))

            def add_out(at, names, b):
                for oc, name in enumerate(names):
                    dve.wait_ge(item_full, item(at, name) + 1)
                    acc = x1[:, oc, bass.ds(b, 1), :].rearrange("p b l -> p (b l)")
                    dve.tensor_tensor(acc, banks[BANK[name]][:, :], acc, ALU.add).then_inc(freed, 1)

            def slot(at, h, has_scores, after_tile):
                if has_scores:
                    logits(at, h, 0)
                    logits(at, h, 1)
                    logits(at, h, 2)
                    inverse(at, h, 0)
                    logits(at, h, 3)
                    inverse(at, h, 1)
                for q in range(QT):
                    right_half(at, h, q)
                    if has_scores and q < 2:
                        inverse(at, h, q + 2)
                    if q == 1:
                        after_tile(0)
                after_tile(1)

            def step(at):
                if "rel0" in at.items:
                    split_weights(at.hp)
                    for i, name in enumerate(REL):
                        cols = slice((i % 2) * L, (i % 2 + 1) * L)
                        take(at, name, rel_l[:, i // 2, cols], rel_h[:, i // 2, cols])
                take_qk(at, 0)
                if "out0" in at.items:
                    add_out(at, ("out0", "out1"), B - 2 + at.odd if at.pair_start else 2 * at.bb + at.odd - 2)
                before = "s0.0" in at.items
                slot(at, 0, before, lambda i: None)
                if before:
                    take(at, "val0", o_l[:, 0, :], o_h[:, 0, :])
                    take_transposed(at, 0)
                take_qk(at, 1)
                if "val1" in at.items:
                    take(at, "val1", o_l[:, 1, :], o_h[:, 1, :])
                slot(at, 1, True, lambda i: take_v(at, i))
                take_transposed(at, 1)
                if at.pair_start and at.odd == 1:
                    dve.wait_ge(wo_hi_done, at.hp + 1)
                    dve.tensor_tensor(wl[:, 3, :], raw_w[:, 3, :], wh[:, 3, :].bitcast(F32), ALU.subtract
                                      ).then_inc(wo_done, 1)

            def finish(at):
                add_out(at, ("out0", "out1"), B - 2)
                for q in range(QT):
                    logits(at, 0, q)
                for q in range(QT):
                    inverse(at, 0, q)
                take(at, "val0", o_l[:, 0, :], o_h[:, 0, :])
                take_transposed(at, 0)
                take(at, "val1", o_l[:, 1, :], o_h[:, 1, :])
                add_out(at, ("last0", "last1"), B - 1)

            dve.wait_ge(const_in, 48)
            dve.wait_ge(x1_in, 16)
            for k in range(KD):
                dve.tensor_scalar(x1[:, k, :, :], x1[:, k, :, :], bo[:, k:k + 1], None, ALU.add
                                  ).then_inc(x1_ready, 1)
            dve.wait_ge(x1_ready, KD)
            steps(dve, step, finish)


GATES = 4
GC = GATES * D // P
FFN_EXPERTS = 8
TB = 64
BLOCKS = L // TB
SUB = TB // 4
UP = 16.0


CONSTANTS = 8
MADE = 13 + 3 + 3


def recurrence(nc, condT, wx, wh, gate_bias, router_w, router_b, expert_w, expert_b, row_mask, count8,
               identity, x1, out):
    GK = GC * P
    EK = FFN_EXPERTS * D
    with ExitStack() as ctx:
        s = Scope(nc, ctx)
        raw = s.sb("raw_split", [P, KD, EK])
        wxh, wxl = s.sb("wxh", [P, KD * GK], F16), s.sb("wxl", [P, KD * GK], F16)
        whh, whl = s.sb("whh", [P, KD, GK], F16), s.sb("whl", [P, KD, GK], F16)
        weh, wel = s.sb("weh", [P, KD, EK], F16), s.sb("wel", [P, KD, EK], F16)
        rraw, wrh, wrl = s.sb("rraw", [P, KD, 8]), s.sb("wrh", [P, KD, 8], F16), s.sb("wrl", [P, KD, 8], F16)
        gbias, rbias = s.sb("gbias", [P, GC]), s.sb("rbias", [P, 8])
        eb, ebh, ebl = s.sb("eb", [2, EK]), s.sb("ebh", [2, EK], F16), s.sb("ebl", [2, EK], F16)
        ebm, rows = s.sb("ebm", [2, EK], F16), s.sb("rows", [2, EK], F16)
        mask, count = s.sb("mask", [2, 2]), s.sb("count", [P, 8])
        ones2 = s.sb("ones2", [2, P], F16)
        ident, ident16 = s.sb("ident3", [P, P]), s.sb("ident16", [P, P], F16)
        h0 = s.sb("h0", [P, KD, B])
        xs_h, xs_l = s.sb("xs_h", [P, KD, B, TB], F16), s.sb("xs_l", [P, KD, B, TB], F16)
        share_h = s.sb("share_h", [P, 2 * TB * GC * B], F16)
        share_l = s.sb("share_l", [P, 2 * TB * GC * B], F16)
        xstage = s.sb("xstage", [P, 2, B, TB])
        hs = s.sb("hs", [P, 4, KD, 2 * B], F16)
        hist = s.sb("hist", [P, 2 * 2 * KD * B * TB], F16)
        f, gi, o = s.sb("forget", [P, 2, 2 * B]), s.sb("cand_in", [P, 2, 4 * B]), s.sb("out_gate", [P, 2, 2 * B])
        cell, fc, ig = s.sb("cell", [P, 2, 2 * B]), s.sb("fc", [P, 2, 2 * B]), s.sb("ig", [P, 2, 2 * B])
        tc, h = s.sb("tc", [P, 2, 2 * B]), s.sb("hidden", [P, 2, 2 * B])
        xt = s.sb("xt", [P, KD, P])
        acc = s.sb("acc3", [P, D])
        logit, zexp, sig_p, sig_n, inv_n, cand, pick = (
            s.sb(n, [P, 8]) for n in ("logit", "zexp", "sig_p", "sig_n", "inv_n", "cand", "pick"))
        top, ztop, zsum, gate, first_top = (s.sb(n, [P, 1]) for n in ("top", "ztop", "zsum", "gate", "first_top"))
        f_ps, gi_ps, o_ps, share_ps, route_ps, xt_ps = (
            s.ps(n) for n in ("f_ps", "gi_ps", "o_ps", "share_ps", "route_ps", "xt_ps"))
        ffn_ps = [s.ps(f"ffn_ps{i}") for i in range(2)]

        const_in, wx_in, wh_in, we_in = (s.sem(n) for n in ("const_in", "wx_in", "wh_in", "we_in"))
        made, gates_split, experts_split = s.sem("made"), s.sem("gates_split"), s.sem("experts_split")
        hi_ready, h_ready, lo_ready = s.sem("hi_ready"), s.sem("h_ready"), s.sem("lo_ready")
        f_full, gi_full, o_full = s.sem("f_full"), s.sem("gi_full"), s.sem("o_full")
        f_done, gi_done, o_done = s.sem("f_done"), s.sem("gi_done"), s.sem("o_done")
        fc_done, ig_done, cell_done, tanh_done = (s.sem(n) for n in ("fc_done", "ig_done", "cell_done", "tanh_done"))
        hist_done = s.sem("hist_done")
        xs_hi_done, xs_done = s.sem("xs_hi_done"), s.sem("xs_done")
        share_full, share_staged, share_hi_done, share_done = (
            s.sem(n) for n in ("share_full", "share_staged", "share_hi_done", "share_done"))
        routed, xt_done, xt_full, acc_init = (s.sem(n) for n in ("routed", "xt_done", "xt_full", "acc_init"))
        logit_done, zmax_done, sig_done, gate_step, pick_done = (
            s.sem(n) for n in ("logit_done", "zmax_done", "sig_done", "gate_step", "pick_done"))
        ffn_full, acc_step, out_sent = s.sem("ffn_full"), s.sem("acc_step"), s.sem("out_sent")
        block = ctx.enter_context(nc.Block())

        def blocks(eng, body):
            with eng.Fori(0, 4) as q:
                body(0, q, False, True)
            with eng.Fori(1, BLOCKS - 1) as j:
                with eng.Fori(0, 4) as q:
                    body(j, q, True, True)
            with eng.Fori(0, 4) as q:
                body(BLOCKS - 1, q, True, False)

        def after(eng, side):
            with eng.Fori(0, 4) as q:
                for i in range(SUB):
                    side(BLOCKS, q, i, True, False)

        @block.sync
        def _(sp):
            constants = ((ident[:, :], identity), (h0[:, :, :], condT.rearrange("(k p) b -> p k b", p=P)),
                         (gbias[:, :], gate_bias), (rbias[:, :], router_b), (count[:, :], count8),
                         (rraw[:, :, :], router_w.rearrange("(k p) e -> p k e", p=P)),
                         (eb[:, :], expert_b), (mask[:, :], row_mask))
            assert len(constants) == CONSTANTS
            for dst, src in constants:
                sp.dma_start(dst, src).then_inc(const_in, 16)
            sp.dma_start(raw[:, :, 0:GK], wx.rearrange("(k p) n -> p k n", p=P)).then_inc(wx_in, 16)
            sp.dma_start(raw[:, :, GK:2 * GK], wh.rearrange("(k p) n -> p k n", p=P)).then_inc(wh_in, 16)
            sp.wait_ge(gates_split, 2)
            sp.dma_start(raw[:, :, :], expert_w.rearrange("(k p) n -> p k n", p=P)).then_inc(we_in, 16)
            sp.nop().then_inc(out_sent, 32)
            with sp.Fori(1, BLOCKS + 1) as j:
                with sp.Fori(0, 4) as q:
                    sp.wait_ge(acc_step, FFN_EXPERTS * (4 * (j - 1) + q + 1) + 4)
                    for i in range(2):
                        dst = out[bass.ds(2 * q + i, 1), bass.ds(TB * (j - 1), TB), :]
                        sp.dma_start(dst.rearrange("b t d -> (b t) d"), acc[TB * i:TB * (i + 1), :]
                                     ).then_inc(out_sent, 16)
            sp.wait_ge(out_sent, 32 * 4 * BLOCKS + 32)

        @block.tensor
        def _(pe):
            def state_products(bank, T, slot, g0, g1, terms):
                for g in range(g0, g1):
                    for k in range(KD):
                        for w, c in terms:
                            mm = pe.matmul(bank[:, (g - g0) * B:(g - g0 + 1) * B], w[:, k, g * P:(g + 1) * P],
                                           hs[:, slot, k, c:c + B], start=False, stop=True, skip_group_check=True)
                return mm

            def put_share(j, q, i):
                T = TB * j + SUB * q + i
                step = GC * B * (TB * (j % 2) + SUB * q + i)
                for bank, a, z, done in ((f_ps, 0, 2, f_done), (gi_ps, 2, 6, gi_done), (o_ps, 6, 8, o_done)):
                    pe.wait_ge(done, T + 1)
                    n = (z - a) * B
                    pe.matmul(bank[:, 0:n], ident16[:, :], share_h[:, bass.ds(step + a * B, n)], start=True,
                              stop=False, skip_group_check=True)
                    pe.matmul(bank[:, 0:n], ident16[:, :], share_l[:, bass.ds(step + a * B, n)], start=False,
                              stop=False, skip_group_check=True)

            def share_terms(jb, c, lo, hi):
                if lo == 0:
                    pe.wait_ge(share_staged, GC * jb + c + 1)
                    pe.wait_ge(xs_done, jb + 1)
                terms = [(w, x, k) for w, x in ((wxh, xs_h), (wxh, xs_l), (wxl, xs_h)) for k in range(KD)]
                for n in range(lo, hi):
                    w, x, k = terms[n]
                    mm = pe.matmul(share_ps[:, :], w[:, bass.ds(P * c + GK * k, P)],
                                   x[:, k, :, :].rearrange("p b t -> p (b t)"), start=(n == 0), stop=(n == 5))
                if hi == 6:
                    mm.then_inc(share_full, 1)

            def hidden(j, part, k, q):
                return hist[:, bass.ds(2048 * ((j + 1) % 2) + 1024 * part + 512 * k + P * q, P)]

            def route(j, q):
                m = 4 * (j - 1) + q
                pe.wait_ge(hist_done, TB * j + 4)
                pe.wait_ge(logit_done, m + 1)
                n = 0
                for part, w in ((0, wrh), (1, wrh), (0, wrl)):
                    for k in range(KD):
                        mm = pe.matmul(route_ps[:, 0:8], hidden(j, part, k, q), w[:, k, :], start=(n == 0),
                                       stop=(n == 5))
                        n += 1
                mm.then_inc(routed, 1)

            def turn_x1(j, q):
                m = 4 * (j - 1) + q
                pe.wait_ge(xt_done, m + 1)
                pe.wait_ge(acc_init, m + 1)
                for k in range(KD):
                    mm = pe.transpose(xt_ps[:, k * P:(k + 1) * P], xt[:, k, :], ident[:, :])
                mm.then_inc(xt_full, 1)

            def expert_pair(j, q, e, half):
                m = 4 * (j - 1) + q
                bank = ffn_ps[e % 2]
                cols = slice(2 * D * e, 2 * D * (e + 1))
                if half == 0:
                    pe.wait_ge(acc_step, FFN_EXPERTS * m + 2 * e + 2)
                    pe.matmul(bank[:, :], ones2[:, :], rows[:, cols], start=True, stop=False)
                    for k in range(KD):
                        pe.matmul(bank[:, :], hidden(j, 0, k, q), weh[:, k, cols], start=False, stop=False)
                    return
                for part, w in ((1, weh), (0, wel)):
                    for k in range(KD):
                        mm = pe.matmul(bank[:, :], hidden(j, part, k, q), w[:, k, cols], start=False,
                                       stop=(part == 0 and k == KD - 1))
                mm.then_inc(ffn_full, 1)

            def side(j, q, i, routing, sharing):
                if routing and i == 0:
                    route(j, q)
                if sharing and 1 <= i <= 4:
                    share_terms(j + 1, 2 * q + (i - 1) // 2, 3 * ((i - 1) % 2), 3 * ((i - 1) % 2) + 3)
                if routing and i == 3:
                    turn_x1(j, q)
                if routing and 5 <= i <= 12:
                    expert_pair(j, q, (i - 5) // 2, (i - 5) % 2)

            def body(j, q, routing, sharing):
                high, low = ((whh, 0), (whl, 0)), ((whh, B),)
                for i in range(SUB):
                    T, slot = TB * j + SUB * q + i, i % 4
                    if i == 0:
                        pe.wait_ge(share_done, GC * (j + 1) + 2)
                    put_share(j, q, i)
                    pe.wait_ge(hi_ready, T + 1)
                    state_products(f_ps, T, slot, 0, 2, high)
                    state_products(gi_ps, T, slot, 2, 6, high)
                    pe.wait_ge(lo_ready, T + 1)
                    state_products(f_ps, T, slot, 0, 2, low).then_inc(f_full, 1)
                    state_products(gi_ps, T, slot, 2, 6, low).then_inc(gi_full, 1)
                    state_products(o_ps, T, slot, 6, 8, high)
                    state_products(o_ps, T, slot, 6, 8, low).then_inc(o_full, 1)
                    side(j, q, i, routing, sharing)

            pe.wait_ge(gates_split, 2)
            pe.wait_ge(made, MADE)
            with pe.Fori(0, GC) as c:
                share_terms(0, c, 0, 6)
            pe.wait_ge(experts_split, 1)
            blocks(pe, body)
            after(pe, side)

        @block.scalar
        def _(act):
            act.nop().then_inc(share_staged, 1)
            for free in (f_done, gi_done, o_done, acc_init):
                act.nop().then_inc(free, 1)

            def stage_share(jb, c, b):
                q = GC * jb + c
                act.wait_ge(share_full, q + 1)
                act.wait_ge(share_done, q + 1)
                act.activation(xstage[:, b, :, :].rearrange("p b t -> p (b t)"), share_ps[:, :], ACT.Identity,
                               bias=gbias[:, bass.ds(c, 1)]).then_inc(share_staged, 1)

            def side(j, q, i, routing, sharing):
                m = 4 * (j - 1) + q
                if routing and i == 2:
                    act.wait_ge(zmax_done, m + 1)
                    act.activation(sig_p[:, :], zexp[:, :], ACT.Sigmoid).then_inc(sig_done, 1)
                    act.activation(sig_n[:, :], zexp[:, :], ACT.Sigmoid, scale=-1.0).then_inc(sig_done, 1)
                if routing and i == 5:
                    act.wait_ge(xt_full, m + 1)
                    act.wait_ge(out_sent, 32 * m + 32)
                    act.copy(acc[:, :], xt_ps[:, 0:D]).then_inc(acc_init, 1)
                if sharing and i in (2, 4):
                    stage_share(j + 1, 2 * q + (i - 2) // 2, (i - 2) // 2)

            def body(j, q, routing, sharing):
                for i in range(SUB):
                    T, p = TB * j + SUB * q + i, i % 2
                    act.wait_ge(f_full, T + 1)
                    act.activation(f[:, p, :], f_ps[:, 0:2 * B], ACT.Sigmoid, scale=1.0 / UP).then_inc(f_done, 1)
                    act.wait_ge(gi_full, T + 1)
                    act.activation(gi[:, p, :], gi_ps[:, 0:4 * B], ACT.Sigmoid, scale=1.0 / UP).then_inc(gi_done, 1)
                    act.wait_ge(o_full, T + 1)
                    act.activation(o[:, p, :], o_ps[:, 0:2 * B], ACT.Sigmoid, scale=1.0 / UP).then_inc(o_done, 1)
                    act.wait_ge(cell_done, T + 1)
                    act.activation(tc[:, p, :], cell[:, p, :], ACT.Tanh, scale=2.0).then_inc(tanh_done, 1)
                    side(j, q, i, routing, sharing)

            act.wait_ge(made, MADE)
            with act.Fori(0, GC // 2) as c:
                for b in range(2):
                    stage_share(0, 2 * c + b, b)
            blocks(act, body)
            after(act, side)

        @block.gpsimd
        def _(pool):
            pool.nop().then_inc(hist_done, 4)

            def tile_x1(j, q):
                src = x1[:, :, bass.ds(2 * q, 2), bass.ds(TB * (j - 1), TB)]
                pool.tensor_copy(xt[:, :, :].rearrange("p k (b t) -> p k b t", b=2), src).then_inc(xt_done, 1)

            def body(j, q, routing, sharing):
                for i in range(SUB):
                    T = TB * j + SUB * q + i
                    pool.wait_ge(lo_ready, T + 2)
                    if routing and i == 0:
                        tile_x1(j, q)
                    rows_t = hist[:, :].rearrange("p (n t) -> p n t", t=TB)
                    dst = rows_t[:, bass.ds(2 * KD * B * (j % 2), 2 * KD * B), bass.ds(SUB * q + i, 1)]
                    pool.tensor_copy(dst.rearrange("p (s k b) t -> p s k (b t)", s=2, k=KD),
                                     hs[:, (i + 1) % 4, :, :].rearrange("p k (s b) -> p s k b", s=2)
                                     ).then_inc(hist_done, 1)

            blocks(pool, body)
            with pool.Fori(0, 4) as q:
                pool.wait_ge(xt_full, 4 * (BLOCKS - 1) + q)
                tile_x1(BLOCKS, q)

        @block.vector
        def _(dve):
            dve.nop().then_inc(share_done, 2)
            dve.nop().then_inc(logit_done, 1)
            dve.nop().then_inc(acc_step, 4)
            count_made = [0]

            def then(ins):
                count_made[0] += 1
                ins.then_inc(made, 1)
                dve.wait_ge(made, count_made[0])

            dve.wait_ge(const_in, 16 * CONSTANTS)
            then(dve.memset(ones2[:, :], 1.0))
            then(dve.memset(cell[:, 1, :], 0.0))
            then(dve.tensor_copy(ident16[:, :], ident[:, :]))
            then(dve.tensor_scalar(gbias[:, :], gbias[:, :], UP, None, ALU.mult))
            then(dve.tensor_scalar(gbias[:, 2:4], gbias[:, 2:4], 2.0, None, ALU.mult))
            then(dve.tensor_scalar(rraw[:, :, :], rraw[:, :, :], UP, None, ALU.mult))
            then(dve.tensor_copy(wrh[:, :, :], rraw[:, :, :]))
            then(dve.tensor_tensor(wrl[:, :, :], rraw[:, :, :], wrh[:, :, :], ALU.subtract))
            then(dve.tensor_scalar(eb[:, :], eb[:, :], UP, None, ALU.mult))
            then(dve.tensor_copy(ebh[:, :], eb[:, :]))
            then(dve.tensor_tensor(ebl[:, :], eb[:, :], ebh[:, :], ALU.subtract))
            then(dve.tensor_scalar(ebm[:, :], ebh[:, :], mask[:, 0:1], None, ALU.mult))
            then(dve.scalar_tensor_tensor(out=rows[:, :], in0=ebl[:, :], scalar=mask[:, 1:2], in1=ebm[:, :],
                                          op0=ALU.mult, op1=ALU.add))

            def split_weights(raw_part, hi, lo, came, candidate):
                dve.wait_ge(came, 16)
                then(dve.tensor_scalar(raw_part, raw_part, UP, None, ALU.mult))
                if candidate:
                    g = raw_part[:, :, 2 * P:4 * P]
                    then(dve.tensor_scalar(g, g, 2.0, None, ALU.mult))
                then(dve.tensor_copy(hi, raw_part))
                return dve.tensor_tensor(lo, raw_part, hi, ALU.subtract)

            two = lambda a: a[:, :].rearrange("p (k n) -> p k n", k=KD)
            split_weights(raw[:, :, 0:GK], two(wxh), two(wxl), wx_in, True).then_inc(gates_split, 1)
            split_weights(raw[:, :, GK:2 * GK], whh[:, :, :], whl[:, :, :], wh_in, True).then_inc(gates_split, 1)
            assert count_made[0] == MADE

            def split_x1(jb):
                src = x1[:, :, :, bass.ds(TB * jb, TB)]
                for k in range(KD):
                    dve.tensor_copy(xs_h[:, k, :, :], src[:, k, :, :]).then_inc(xs_hi_done, 1)
                    dve.wait_ge(xs_hi_done, KD * jb + k + 1)
                    ins = dve.tensor_tensor(xs_l[:, k, :, :], src[:, k, :, :], xs_h[:, k, :, :], ALU.subtract)
                ins.then_inc(xs_done, 1)

            def share_view(share, jb, c):
                v = share[:, :].rearrange("p (r t g b) -> p r g b t", r=2, t=TB, g=GC)
                return v[:, bass.ds(jb % 2, 1), bass.ds(c, 1), :, :].rearrange("p r g b t -> p (r g b) t")

            def split_share(jb, c, b, low):
                n = GC * jb + c
                hi, lo = share_view(share_h, jb, c), share_view(share_l, jb, c)
                if not low:
                    dve.wait_ge(share_staged, n + 2)
                    dve.tensor_copy(hi, xstage[:, b, :, :]).then_inc(share_hi_done, 1)
                else:
                    dve.wait_ge(share_hi_done, n + 1)
                    dve.tensor_tensor(lo, xstage[:, b, :, :], hi, ALU.subtract).then_inc(share_done, 1)

            def side(j, q, i, routing, sharing):
                m = 4 * (j - 1) + q
                G = 7
                if routing and i == 1:
                    dve.wait_ge(routed, m + 1)
                    dve.scalar_tensor_tensor(out=logit[:, :], in0=route_ps[:, 0:8], scalar=1.0 / UP,
                                             in1=rbias[:, :], op0=ALU.mult, op1=ALU.add).then_inc(logit_done, 1)
                    dve.wait_ge(logit_done, m + 2)
                    dve.tensor_reduce(top[:, :], logit[:, :], AX.X, ALU.max).then_inc(gate_step, 1)
                    dve.wait_ge(gate_step, G * m + 1)
                    dve.tensor_scalar(zexp[:, :], logit[:, :], top[:, 0:1], None, ALU.subtract).then_inc(zmax_done, 1)
                if routing and i == 2:
                    dve.tensor_scalar(cand[:, :], logit[:, :], top[:, 0:1], None, ALU.is_lt).then_inc(gate_step, 1)
                    dve.wait_ge(gate_step, G * m + 2)
                    dve.scalar_tensor_tensor(out=cand[:, :], in0=cand[:, :], scalar=8.0, in1=count[:, :],
                                             op0=ALU.mult, op1=ALU.add).then_inc(gate_step, 1)
                    dve.wait_ge(gate_step, G * m + 3)
                    dve.tensor_reduce(first_top[:, :], cand[:, :], AX.X, ALU.min).then_inc(gate_step, 1)
                if routing and i == 3:
                    dve.wait_ge(sig_done, 2 * m + 2)
                    dve.reciprocal(inv_n[:, :], sig_n[:, :]).then_inc(gate_step, 1)
                    dve.wait_ge(gate_step, G * m + 5)
                    dve.tensor_tensor(inv_n[:, :], inv_n[:, :], sig_p[:, :], ALU.mult).then_inc(gate_step, 1)
                    dve.wait_ge(gate_step, G * m + 6)
                    dve.tensor_reduce(zsum[:, :], inv_n[:, :], AX.X, ALU.add).then_inc(gate_step, 1)
                if routing and i == 4:
                    dve.wait_ge(gate_step, G * m + 7)
                    dve.reciprocal(gate[:, :], zsum[:, :]).then_inc(pick_done, 1)
                    dve.wait_ge(pick_done, 3 * m + 1)
                    dve.tensor_scalar(gate[:, :], gate[:, :], 1.0 / UP, None, ALU.mult).then_inc(pick_done, 1)
                    dve.wait_ge(pick_done, 3 * m + 2)
                    dve.tensor_scalar(pick[:, :], count[:, :], first_top[:, 0:1], gate[:, 0:1], ALU.is_equal,
                                      ALU.mult).then_inc(pick_done, 1)
                if routing and 7 <= i <= 14:
                    e = i - 7
                    if e == 0:
                        dve.wait_ge(pick_done, 3 * m + 3)
                        dve.wait_ge(acc_init, m + 2)
                    else:
                        dve.wait_ge(acc_step, FFN_EXPERTS * m + e + 4)
                    dve.wait_ge(ffn_full, 4 * m + e // 2 + 1)
                    dve.scalar_tensor_tensor(out=acc[:, :], in0=ffn_ps[(e // 2) % 2][:, (e % 2) * D:(e % 2 + 1) * D],
                                             scalar=pick[:, e:e + 1], in1=acc[:, :], op0=ALU.mult,
                                             op1=ALU.add).then_inc(acc_step, 1)
                if sharing and 3 <= i <= 6:
                    split_share(j + 1, 2 * q + (i - 3) // 2, (i - 3) // 2, (i - 3) % 2 == 1)

            def halves(a):
                return a.rearrange("p (k n) -> p k n", k=KD)

            def body(j, q, routing, sharing):
                for i in range(SUB):
                    T, p, nxt = TB * j + SUB * q + i, i % 2, (i + 1) % 4
                    dve.wait_ge(hist_done, T + 1)
                    dve.wait_ge(f_done, T + 2)
                    dve.tensor_tensor(fc[:, p, :], f[:, p, :], cell[:, 1 - p, :], ALU.mult).then_inc(fc_done, 1)
                    dve.wait_ge(gi_done, T + 2)
                    dve.scalar_tensor_tensor(out=ig[:, p, :], in0=gi[:, p, 0:2 * B], scalar=-0.5,
                                             in1=gi[:, p, 2 * B:4 * B], op0=ALU.add, op1=ALU.mult).then_inc(ig_done, 1)
                    dve.wait_ge(fc_done, T + 1)
                    dve.wait_ge(ig_done, T + 1)
                    dve.tensor_tensor(cell[:, p, :], ig[:, p, :], fc[:, p, :], ALU.add).then_inc(cell_done, 1)
                    dve.wait_ge(o_done, T + 2)
                    dve.wait_ge(tanh_done, T + 1)
                    dve.tensor_tensor(hs[:, nxt, :, 0:B], halves(o[:, p, :]), halves(tc[:, p, :]),
                                      ALU.mult).then_inc(hi_ready, 1)
                    dve.tensor_tensor(h[:, p, :], o[:, p, :], tc[:, p, :], ALU.mult).then_inc(h_ready, 1)
                    dve.wait_ge(hi_ready, T + 2)
                    dve.wait_ge(h_ready, T + 1)
                    dve.tensor_tensor(hs[:, nxt, :, B:2 * B], halves(h[:, p, :]), hs[:, nxt, :, 0:B],
                                      ALU.subtract).then_inc(lo_ready, 1)
                    side(j, q, i, routing, sharing)

            def before_blocks():
                split_x1(0)
                with dve.Fori(0, GC // 2) as c:
                    for b in range(2):
                        split_share(0, 2 * c + b, b, False)
                        split_share(0, 2 * c + b, b, True)
                split_weights(raw[:, :, :], weh[:, :, :], wel[:, :, :], we_in, False).then_inc(experts_split, 1)
                dve.tensor_copy(hs[:, 0, :, 0:B], h0[:, :, :]).then_inc(hi_ready, 1)
                dve.wait_ge(hi_ready, 1)
                dve.tensor_tensor(hs[:, 0, :, B:2 * B], h0[:, :, :], hs[:, 0, :, 0:B], ALU.subtract
                                  ).then_inc(lo_ready, 1)

            before_blocks()
            split_x1(1)
            with dve.Fori(0, 4) as q:
                body(0, q, False, True)
            with dve.Fori(1, BLOCKS - 1) as j:
                split_x1(j + 1)
                with dve.Fori(0, 4) as q:
                    body(j, q, True, True)
            with dve.Fori(0, 4) as q:
                body(BLOCKS - 1, q, True, False)
            after(dve, side)


def embedded_block_kernel(nc, xT, condT, gate_w, gate_b, time_w, time_b, steps, w1, w2, mix_biases, wqkvo, wrel,
                          positions, qbias, b_out, identity, wx, wh, gate_bias, router_w, router_b, expert_w,
                          expert_b, row_mask, count8, out):
    context = nc.dram_tensor("context", [B, P, 2, KD, L], F32, kind="Internal").ap()
    skew = nc.dram_tensor("skew", [HEADS * P * WIN], F32, kind="Internal").ap()
    with ExitStack() as ctx:
        s = Scope(nc, ctx)
        table_i = s.sb("table_i", [P, B * SLOTS], I32)
        table_w = s.sb("table_w", [P, B * SLOTS * len(RANGES)])
        gating(nc, xT, condT, gate_w, gate_b, time_w, time_b, steps, table_i, table_w)
        mixture(nc, xT, w1, w2, mix_biases, table_i, table_w, context)
    with ExitStack() as ctx:
        x1 = Scope(nc, ctx).sb("x1", [P, KD, B, L])
        attention(nc, xT, wqkvo, wrel, positions, qbias, b_out, identity, context, skew, x1)
        recurrence(nc, condT, wx, wh, gate_bias, router_w, router_b, expert_w, expert_b, row_mask, count8,
                   identity, x1, out)


def _lgamma(x):
    import math
    import numpy as np
    f = np.float32
    total = f(0.99999999999980993227684700473478)
    z = x - f(1)
    for i, c in enumerate((676.520368121885098567009190444019, -1259.13921672240287047156078755283,
                           771.3234287776530788486528258894, -176.61502916214059906584551354,
                           12.507343278686904814458936853, -0.13857109526572011689554707,
                           9.984369578019570859563e-6, 1.50563273514931155834e-7)):
        total = total + f(c) / (z + f(i + 1))
    t, log_t = f(7.5) + z, f(math.log(7.5)) + np.log1p(z / f(7.5))
    return f(0.5 * math.log(2 * math.pi)) + (z + f(0.5) - t / log_t) * log_t + np.log(total)


def _positional_features(seq, features):
    import math
    import numpy as np
    f = np.float32
    n = features // 6

    def linspace(a, z):
        i = np.arange(n - 1, dtype=f) / f(n - 1)
        return np.concatenate([f(a) * (f(1) - i) + f(z) * i, [f(z)]]).astype(f)[None]

    distance = np.arange(-seq + 1, seq).astype(f)
    absd = np.abs(distance)[:, None]
    half_life = f(2) ** linspace(3.0, math.log(seq) / math.log(2.0))
    decay = np.exp(-f(math.log(2.0)) / half_life * absd)
    center = (f(2) ** np.arange(1, n + 1).astype(f) - f(1) > absd).astype(f)
    deviation = seq / (2.0 * n)
    mean = linspace(seq / n, float(seq))
    conc, rate = (mean / f(deviation)) ** 2, mean / f(deviation ** 2)
    log_d = np.log(np.maximum(absd, f(1e-30)))
    density = np.exp((conc - f(1)) * log_d - rate * absd - (_lgamma(conc) - conc * np.log(rate))) + f(1e-8)
    emb = np.concatenate([decay, center, density / density.max(-1, keepdims=True)], -1)
    return np.concatenate([emb, np.sign(distance)[:, None] * emb], -1)


def _gate_order(a):
    import numpy as np
    i, f, o, g = (a[..., n * D:(n + 1) * D] for n in range(4))
    return np.concatenate([f, g, i, o], -1)


def _layout(t):
    import numpy as np
    c = {}
    c["xT"] = t["x"].transpose(2, 0, 1)
    c["condT"] = t["cond_1024"].T
    c["gate_w"], c["gate_b"] = t["L0_cond_gate_w"], t["L0_cond_gate_b"]
    c["time_w"], c["time_b"] = t["L0_cond_time_w"], t["L0_cond_time_b"]
    c["steps"] = np.concatenate([np.tile(np.arange(EXPERTS, dtype=np.float32), (B, 1)),
                                 np.eye(B, dtype=np.float32)], 1)
    c["w1"] = np.concatenate([t["L0_cond_ew1"], t["L0_cond_sw1"][None]])
    c["w2"] = np.concatenate([t["L0_cond_ew2"], t["L0_cond_sw2"][None]])
    b1 = np.concatenate([t["L0_cond_eb1"], t["L0_cond_sb1"][None]]).reshape(EXPERTS + 1, KH, P)
    b2 = np.concatenate([t["L0_cond_eb2"], t["L0_cond_sb2"][None]]).reshape(EXPERTS + 1, KD, P)
    c["mix_biases"] = np.concatenate([b1, b2], 1).transpose(0, 2, 1)
    pair = [t[w].reshape(KD, P, PAIRS, 2 * DK).transpose(2, 1, 0, 3).reshape(PAIRS, P, L)
            for w in ("L0_attn_w_qs", "L0_attn_w_ks", "L0_attn_w_vs")]
    pair.append(t["L0_attn_w_out"].reshape(PAIRS, 2, P, D).transpose(0, 2, 1, 3).reshape(PAIRS, P, L))
    c["wqkvo"] = np.stack(pair, 2)
    c["wrel"] = t["L0_attn_w_rel_pos_k"].reshape(2, FP, PAIRS, 2 * DK).transpose(2, 1, 0, 3)
    positions = np.zeros((FEATS, DIST), np.float32)
    positions[:, 0:DIST - 1] = _positional_features(L, FEATS).T
    c["positions"] = positions.reshape(2, FP, 2, L).transpose(1, 0, 2, 3).reshape(FP, 4, L)
    biases = [t[n].reshape(PAIRS, 2, DK) for n in ("L0_attn_rel_embed_bias", "L0_attn_rel_pos_bias")]
    c["qbias"] = np.stack(biases, 1).reshape(PAIRS, 4, DK).transpose(0, 2, 1)
    c["b_out"] = t["L0_attn_b_out"].reshape(KD, P).T
    c["identity"] = np.eye(P, dtype=np.float32)
    c["wx"], c["wh"] = _gate_order(t["L0_cond2_Wx"]), _gate_order(t["L0_cond2_Wh"])
    c["gate_bias"] = _gate_order(t["L0_cond2_b"]).reshape(GC, P).T
    c["router_w"] = t["L0_ffn_router_w"]
    c["router_b"] = np.tile(t["L0_ffn_router_b"][None], (P, 1))
    c["expert_w"] = t["L0_ffn_expert_w"].transpose(1, 0, 2).reshape(D, FFN_EXPERTS * D)
    c["expert_b"] = np.tile(t["L0_ffn_expert_b"].reshape(1, FFN_EXPERTS * D), (2, 1))
    c["row_mask"] = np.eye(2, dtype=np.float32)
    c["count8"] = np.tile(np.arange(FFN_EXPERTS, dtype=np.float32), (P, 1))
    return c


def kernel(**inputs):
    import numpy as np
    import concourse.bacc as bacc
    from concourse.bass_utils import run_bass_kernel_spmd

    nc = bacc.Bacc("TRN2", target_bir_lowering=False, num_devices=1)
    arrays, args = {}, []
    for name, a in _layout({k: np.asarray(v) for k, v in inputs.items()}).items():
        arrays[f"in_{name}_dram"] = np.ascontiguousarray(a)
        args.append(nc.dram_tensor(f"in_{name}_dram", a.shape, F32, kind="ExternalInput").ap())
    args.append(nc.dram_tensor("out_0_dram", (B, L, D), F32, kind="ExternalOutput").ap())
    embedded_block_kernel(nc, *args)
    r = run_bass_kernel_spmd(nc, [arrays], core_ids=[0])
    return r.results[0]["out_0_dram"]
```

```python
from contextlib import ExitStack

import concourse.bass as bass
from concourse import mybir

F32 = mybir.dt.float32
F32R = mybir.dt.float32r
F16 = mybir.dt.float16
I32 = mybir.dt.int32
ALU = mybir.AluOpType
ACT = mybir.ActivationFunctionType
AX = mybir.AxisListType

P = 128
B, L, D = 8, 512, 256
KD = D // P
EXPERTS, TOP_K, HID = 4, 2, 1024
SHARED = EXPERTS
SLOTS = TOP_K + 1
KH = HID // P
THIRD = L // 3
RANGES = [(0, THIRD), (THIRD, 2 * THIRD), (2 * THIRD, L)]


class Scope:

    def __init__(self, nc, ctx):
        self.nc, self.ctx = nc, ctx

    def sb(self, name, shape, dt=F32):
        return self.ctx.enter_context(self.nc.sbuf_tensor(name, shape, dt))

    def ps(self, name):
        return self.ctx.enter_context(self.nc.psum_tensor(name, [P, 512], F32))

    def sem(self, name):
        return self.ctx.enter_context(self.nc.semaphore(name))


def gating(nc, xT, condT, gate_w, gate_b, time_w, time_b, steps, table_i, table_w):
    with ExitStack() as ctx:
        s = Scope(nc, ctx)
        x_all = s.sb("x_all", [P, KD, B, L])
        gw = s.sb("gw", [P, 3 * KD, EXPERTS])
        tw = s.sb("tw", [P, KD, 2 * EXPERTS])
        gb = s.sb("gb", [1, EXPERTS])
        tb = s.sb("tb", [1, 2 * EXPERTS])
        stp = s.sb("stp", [B, EXPERTS + B])
        cond = s.sb("cond", [P, KD, B])
        csig = s.sb("csig", [P, KD, B])
        csilu = s.sb("csilu", [P, KD, B])
        sums = s.sb("sums", [P, 3, KD, B])
        agg = s.sb("agg", [P, 3, KD, B])
        tmp = s.sb("tmp", [P, KD, B])
        ones = s.sb("ones", [8, P])
        g = s.sb("g", [B, 24, EXPERTS])
        one = s.sb("one", [B, 16])
        vals = s.sb("vals", [B, SLOTS * 4])
        spread = s.sb("spread", [B, B, SLOTS * 4])
        logit_ps, mod_ps, table_ps = s.ps("logit_ps"), s.ps("mod_ps"), s.ps("table_ps")
        small_in, x_in = s.sem("small_in"), s.sem("x_in")
        sig_done, vec, aggs_done, logits_done, spread_done, table_done, exp_done = (
            s.sem(n) for n in ("sig_done", "vec", "aggs_done", "logits_done", "spread_done", "table_done", "exp_done"))
        block = ctx.enter_context(nc.Block())

        @block.sync
        def _(sp):
            sp.dma_start(x_all[:, :, :, :], xT.rearrange("(k p) b l -> p k b l", p=P)).then_inc(x_in, 16)
            sp.dma_start(cond[:, :, :], condT.rearrange("(k p) b -> p k b", p=P)).then_inc(small_in, 16)
            sp.dma_start(gw[:, :, :], gate_w.rearrange("(k p) e -> p k e", p=P)).then_inc(small_in, 16)
            sp.dma_start(tw[:, :, :], time_w.rearrange("(k p) e -> p k e", p=P)).then_inc(small_in, 16)
            sp.dma_start(gb[:, :], gate_b.rearrange("(a e) -> a e", a=1)).then_inc(small_in, 16)
            sp.dma_start(tb[:, :], time_b.rearrange("(a e) -> a e", a=1)).then_inc(small_in, 16)
            sp.dma_start(stp[:, :], steps).then_inc(small_in, 16)

        @block.scalar
        def _(act):
            act.wait_ge(small_in, 96)
            act.activation(csig[:, :, :], cond[:, :, :], ACT.Sigmoid).then_inc(sig_done, 1)
            act.wait_ge(vec, 17)
            act.activation(g[:, 5, :], g[:, 4, :], ACT.Exp, bias=one[:, 0:1],
                           accum_out=one[:, 1:2]).then_inc(exp_done, 1)

        @block.tensor
        def _(pe):
            pe.wait_ge(small_in, 96)
            pe.wait_ge(vec, 2)
            for k in range(KD):
                pe.matmul(mod_ps[0:B, 0:2 * EXPERTS], csilu[:, k, :], tw[:, k, :], start=(k == 0), stop=False)
            pe.matmul(mod_ps[0:B, 0:2 * EXPERTS], ones[0:1, 0:B], tb[:, :], start=False, stop=True)
            pe.wait_ge(aggs_done, 1)
            for j in range(3 * KD):
                pe.matmul(logit_ps[0:B, 0:EXPERTS], agg[:, j // KD, j % KD, :], gw[:, j, :],
                          start=(j == 0), stop=False)
            pe.matmul(logit_ps[0:B, 0:EXPERTS], ones[0:1, 0:B], gb[:, :], start=False,
                      stop=True).then_inc(logits_done, 1)
            pe.wait_ge(spread_done, 1)
            pe.matmul(table_ps[:, 0:B * SLOTS * 4], ones[0:B, :], spread[:, :, :].rearrange("p b n -> p (b n)"),
                      start=True, stop=True).then_inc(table_done, 1)

        @block.vector
        def _(dve):
            done = [0]

            def then(ins):
                done[0] += 1
                ins.then_inc(vec, 1)
                dve.wait_ge(vec, done[0])

            then(dve.memset(ones[:, :], 1.0))
            dve.wait_ge(sig_done, 1)
            then(dve.tensor_tensor(csilu[:, :, :], cond[:, :, :], csig[:, :, :], ALU.mult))
            dve.wait_ge(x_in, 16)
            for r, (a, z) in enumerate(RANGES):
                then(dve.tensor_reduce(sums[:, r, :, :], x_all[:, :, :, a:z], AX.X, ALU.add))
            n_pair = L - THIRD
            then(dve.tensor_tensor(tmp[:, :, :], sums[:, 0, :, :], sums[:, 2, :, :], ALU.add))
            then(dve.tensor_scalar(agg[:, 1, :, :], tmp[:, :, :], 1.0 / n_pair, None, ALU.mult))
            then(dve.tensor_tensor(agg[:, 0, :, :], tmp[:, :, :], sums[:, 1, :, :], ALU.add))
            then(dve.tensor_scalar(agg[:, 0, :, :], agg[:, 0, :, :], 1.0 / L, None, ALU.mult))
            then(dve.tensor_tensor(tmp[:, :, :], sums[:, 1, :, :], sums[:, 2, :, :], ALU.add))
            dve.tensor_scalar(agg[:, 2, :, :], tmp[:, :, :], 1.0 / n_pair, None, ALU.mult).then_inc(aggs_done, 1)
            dve.wait_ge(logits_done, 1)
            then(dve.tensor_scalar(g[:, 0, :], mod_ps[0:B, 0:EXPERTS], 1.0, None, ALU.add))
            then(dve.tensor_copy(g[:, 1, :], mod_ps[0:B, EXPERTS:2 * EXPERTS]))
            then(dve.tensor_tensor(g[:, 2, :], logit_ps[0:B, 0:EXPERTS], g[:, 0, :], ALU.mult))
            then(dve.tensor_tensor(g[:, 4, :], g[:, 2, :], g[:, 1, :], ALU.add))
            then(dve.tensor_reduce(one[:, 2:3], g[:, 4, :], AX.X, ALU.max))
            then(dve.tensor_scalar(one[:, 0:1], one[:, 2:3], -1.0, None, ALU.mult))
            then(dve.memset(vals[:, :], 1.0))
            assert done[0] == 17
            dve.wait_ge(exp_done, 1)
            then(dve.reciprocal(one[:, 3:4], one[:, 1:2]))
            then(dve.tensor_scalar(g[:, 6, :], g[:, 5, :], one[:, 3:4], None, ALU.mult))
            for j in range(TOP_K):
                score = g[:, 6 + j, :]
                top, eq, cand, hot = one[:, 4 + j:5 + j], g[:, 8 + 3 * j, :], g[:, 9 + 3 * j, :], g[:, 10 + 3 * j, :]
                then(dve.tensor_reduce(top, score, AX.X, ALU.max))
                then(dve.tensor_scalar(eq, score, top, None, ALU.is_lt))
                then(dve.scalar_tensor_tensor(out=cand, in0=eq, scalar=8.0, in1=stp[:, 0:EXPERTS],
                                              op0=ALU.mult, op1=ALU.add))
                then(dve.tensor_reduce(vals[:, 4 * j + 3:4 * j + 4], cand, AX.X, ALU.min))
                then(dve.tensor_scalar(hot, stp[:, 0:EXPERTS], vals[:, 4 * j + 3:4 * j + 4], None, ALU.is_equal))
                then(dve.scalar_tensor_tensor(out=g[:, 7 + j, :], in0=hot, scalar=-2.0, in1=score,
                                              op0=ALU.mult, op1=ALU.add) if j == 0 else
                     dve.tensor_tensor(one[:, 6:7], one[:, 4:5], one[:, 5:6], ALU.add))
            then(dve.tensor_scalar(one[:, 7:8], one[:, 6:7], 1e-8, None, ALU.add))
            then(dve.reciprocal(one[:, 8:9], one[:, 7:8]))
            for j in range(TOP_K):
                hot, w = g[:, 10 + 3 * j, :], one[:, 9 + j:10 + j]
                then(dve.tensor_tensor(w, one[:, 4 + j:5 + j], one[:, 8:9], ALU.mult))
                then(dve.tensor_scalar(g[:, 16 + j, :], hot, -1.0, 1.0, ALU.mult, ALU.add))
                then(dve.tensor_tensor(vals[:, 4 * j:4 * j + 1], g[:, 16 + j, 2:3], w, ALU.mult))
                then(dve.tensor_tensor(vals[:, 4 * j + 1:4 * j + 2], g[:, 16 + j, 1:2], w, ALU.mult))
                then(dve.tensor_copy(vals[:, 4 * j + 2:4 * j + 3], w))
            then(dve.memset(vals[:, 4 * TOP_K + 3:4 * TOP_K + 4], float(SHARED)))
            for b in range(B):
                then(dve.tensor_scalar(spread[:, b, :], vals[:, :], stp[:, EXPERTS + b:EXPERTS + b + 1], None,
                                       ALU.mult))
            dve.nop().then_inc(spread_done, 1)
            dve.wait_ge(table_done, 1)
            t = table_ps[:, 0:B * SLOTS * 4].rearrange("p (n c) -> p n c", c=4)
            then(dve.tensor_copy(table_w[:, :].rearrange("p (n c) -> p n c", c=3), t[:, :, 0:3]))
            then(dve.tensor_copy(table_i[0:1, :], t[0:1, :, 3]))


def mixture(nc, xT, w1, w2, biases, table_i, table_w, context, ahead):
    GELUS = 4
    with ExitStack() as ctx:
        s = Scope(nc, ctx)
        raw1, raw2 = s.sb("raw1", [P, KD, HID]), s.sb("raw2", [P, KH, D])
        w1h, w1l = s.sb("w1h", [P, KD, HID], F32R), s.sb("w1l", [P, KD, HID], F32R)
        w2h, w2l = s.sb("w2h", [P, KH, D], F32R), s.sb("w2l", [P, KH, D], F32R)
        bias = s.sb("bias", [P, SLOTS, KH + KD])
        weight = s.sb("weight", [P, 3 * SLOTS])
        x_raw = s.sb("x_raw", [P, KD, L])
        x_hi, x_lo = s.sb("x_hi", [P, KD, L], F32R), s.sb("x_lo", [P, KD, L], F32R)
        g = s.sb("gelu", [P, GELUS, L])
        h_hi, h_lo = s.sb("h_hi", [P, KH, L], F32R), s.sb("h_lo", [P, KH, L], F32R)
        y, acc = s.sb("y", [P, KD, L]), s.sb("acc", [P, KD, L])
        split = s.sb("split", [P, 2, KD, L], F32R)
        h_ps = [s.ps(f"h_ps{i}") for i in range(GELUS)]
        y_ps = [s.ps(f"y_ps{i}") for i in range(KD)]
        raw1_in, raw2_in, x_in = s.sem("raw1_in"), s.sem("raw2_in"), s.sem("mix_x_in")
        bias_in = [s.sem(f"bias_in{i}") for i in range(SLOTS)]
        w1_hi_done, w1_done, w2_hi_done, w2_done = (
            s.sem(n) for n in ("w1_hi_done", "w1_done", "w2_hi_done", "w2_done"))
        x_hi_done, x_done = s.sem("x_hi_done"), s.sem("x_done")
        h_full, gelu_done, hi_done, lo_done = (s.sem(n) for n in ("h_full", "gelu_done", "hi_done", "lo_done"))
        y_full, y_out, y_used, acc_done = (s.sem(n) for n in ("y_full", "y_out", "y_used", "acc_done"))
        split_hi_done, split_done, context_out, context_free = (
            s.sem(n) for n in ("split_hi_done", "split_done", "context_out", "context_free"))
        ahead_in, bias_added = s.sem("ahead_in"), s.sem("bias_added")
        block = ctx.enter_context(nc.Block())

        @block.sync
        def _(sp):
            with sp.Fori(0, B) as b:
                sp.wait_ge(x_done, b + 1)
                sp.dma_start(x_raw[:, :, :],
                             xT[:, bass.ds(b, 1), :].rearrange("(k p) b l -> p k (b l)", p=P)).then_inc(x_in, 16)
                for slot in range(SLOTS):
                    k = SLOTS * b + slot
                    e = sp.value_load(table_i[0:1, bass.ds(k, 1)], min_val=0, max_val=SHARED)
                    sp.wait_ge(w1_done, k + 1)
                    sp.dma_start(raw1[:, :, :], w1[bass.ds(e, 1)].rearrange("e (k p) n -> p (e k) n", p=P)
                                 ).then_inc(raw1_in, 16)
                    sp.dma_start(bias[:, slot, :], biases[bass.ds(e, 1)].rearrange("e p n -> p (e n)")
                                 ).then_inc(bias_in[slot], 16)
                    sp.wait_ge(w2_done, k + 1)
                    sp.dma_start(raw2[:, :, :], w2[bass.ds(e, 1)].rearrange("e (k p) n -> p (e k) n", p=P)
                                 ).then_inc(raw2_in, 16)
            sp.wait_ge(context_out, 16 * B)
            sp.wait_ge(ahead_in, 16 * len(ahead.loads))
            sp.wait_ge(bias_added, KD)

        @block.tensor
        def _(pe):
            with pe.Fori(0, B) as b:
                for slot in range(SLOTS):
                    k = SLOTS * b + slot
                    pe.wait_ge(w1_done, k + 2)
                    if slot == 0:
                        pe.wait_ge(x_done, b + 2)
                    for oc in range(KH):
                        pe.wait_ge(gelu_done, KH * k + oc + 1)
                        for n, (w, x) in enumerate(((w1h, x_hi), (w1h, x_lo), (w1l, x_hi))):
                            for c in range(KD):
                                mm = pe.matmul(h_ps[oc % GELUS][:, :], w[:, c, oc * P:(oc + 1) * P], x[:, c, :],
                                               start=(n == 0 and c == 0), stop=(n == 2 and c == KD - 1))
                        mm.then_inc(h_full, 1)
                    pe.wait_ge(w2_done, k + 2)
                    pe.wait_ge(y_out, KD * k + KD)
                    for c in range(KH):
                        pe.wait_ge(lo_done, KH * k + c + 1 + GELUS)
                        for oc in range(KD):
                            for n, (w, h) in enumerate(((w2h, h_hi), (w2h, h_lo), (w2l, h_hi))):
                                mm = pe.matmul(y_ps[oc][:, :], w[:, c, oc * P:(oc + 1) * P], h[:, c, :],
                                               start=(c == 0 and n == 0), stop=(c == KH - 1 and n == 2))
                            if c == KH - 1:
                                mm.then_inc(y_full, 1)

        @block.scalar
        def _(act):
            act.nop().then_inc(gelu_done, GELUS)
            act.nop().then_inc(y_out, KD)
            act.wait_ge(h_full, 1)
            for dst, src in ahead.loads:
                act.dma_start(dst, src).then_inc(ahead_in, 16)
            with act.Fori(0, B) as b:
                for slot in range(SLOTS):
                    k = SLOTS * b + slot
                    act.wait_ge(bias_in[slot], 16 * b + 16)
                    for oc in range(KH):
                        n = KH * k + oc
                        act.wait_ge(h_full, n + 1)
                        act.wait_ge(lo_done, n + 1)
                        act.activation(g[:, oc % GELUS, :], h_ps[oc % GELUS][:, :], ACT.Gelu_apprx_tanh,
                                       bias=bias[:, slot, oc:oc + 1]).then_inc(gelu_done, 1)
                        act.wait_ge(gelu_done, n + 1 + GELUS)
                        act.copy(h_hi[:, oc, :], g[:, oc % GELUS, :]).then_inc(hi_done, 1)
                    act.wait_ge(y_used, k + 1)
                    for oc in range(KD):
                        act.wait_ge(y_full, KD * k + oc + 1)
                        act.activation(y[:, oc, :], y_ps[oc][:, :], ACT.Identity,
                                       bias=bias[:, slot, KH + oc:KH + oc + 1]).then_inc(y_out, 1)

        @block.gpsimd
        def _(pool):
            pool.nop().then_inc(context_free, 1)
            pool.wait_ge(ahead_in, 16 * len(ahead.loads))
            for k in range(KD):
                pool.tensor_scalar(ahead.x1[:, k, :, :], ahead.x1[:, k, :, :], ahead.bo[:, k:k + 1], None, ALU.add
                                   ).then_inc(bias_added, 1)
            with pool.Fori(0, B) as b:
                pool.wait_ge(split_done, b + 1)
                pool.dma_start(context[bass.ds(b, 1)].rearrange("b p s k l -> p (b s k l)"),
                               split[:, :, :, :].rearrange("p s k l -> p (s k l)").bitcast(F32)
                               ).then_inc(context_out, 16)
                pool.wait_ge(context_out, 16 * b + 16)
                pool.nop().then_inc(context_free, 1)

        @block.vector
        def _(dve):
            dve.nop().then_inc(lo_done, GELUS)
            for free in (y_used, w1_done, w2_done, x_done):
                dve.nop().then_inc(free, 1)

            def split_x(b):
                dve.wait_ge(x_in, 16 * b + 16)
                dve.tensor_copy(x_hi[:, :, :], x_raw[:, :, :]).then_inc(x_hi_done, 1)
                dve.wait_ge(x_hi_done, b + 1)
                dve.tensor_tensor(x_lo[:, :, :], x_raw[:, :, :], x_hi[:, :, :].bitcast(F32),
                                  ALU.subtract).then_inc(x_done, 1)

            def split_w(k, raw, hi, lo, came, hi_split, done):
                dve.wait_ge(came, 16 * k + 16)
                dve.tensor_copy(hi[:, :, :], raw[:, :, :]).then_inc(hi_split, 1)
                dve.wait_ge(hi_split, k + 1)
                dve.tensor_tensor(lo[:, :, :], raw[:, :, :], hi[:, :, :].bitcast(F32),
                                  ALU.subtract).then_inc(done, 1)

            def batch(b, last):
                dve.tensor_copy(weight[:, :], table_w[:, bass.ds(9 * b, 9)]).then_inc(acc_done, 1)
                for slot in range(SLOTS):
                    k = SLOTS * b + slot
                    split_w(k, raw2, w2h, w2l, raw2_in, w2_hi_done, w2_done)
                    for oc in range(KH):
                        dve.wait_ge(hi_done, KH * k + oc + 1)
                        dve.tensor_tensor(h_lo[:, oc, :], g[:, oc % GELUS, :], h_hi[:, oc, :].bitcast(F32),
                                          ALU.subtract).then_inc(lo_done, 1)
                    if not last or slot < SLOTS - 1:
                        if slot == SLOTS - 1:
                            split_x(b + 1)
                        split_w(k + 1, raw1, w1h, w1l, raw1_in, w1_hi_done, w1_done)
                    dve.wait_ge(y_out, KD * k + 2 * KD)
                    dve.wait_ge(acc_done, 6 * b + 1 + 2 * slot)
                    dve.wait_ge(y_used, k + 1)
                    if slot < TOP_K:
                        for r, (a, z) in enumerate(RANGES):
                            w = weight[:, 3 * slot + r:3 * slot + r + 1]
                            if slot == 0:
                                ins = dve.tensor_scalar(acc[:, :, a:z], y[:, :, a:z], w, None, ALU.mult)
                            else:
                                ins = dve.scalar_tensor_tensor(out=acc[:, :, a:z], in0=y[:, :, a:z], scalar=w,
                                                               in1=acc[:, :, a:z], op0=ALU.mult, op1=ALU.add)
                            ins.then_inc(y_used if r == 2 else acc_done, 1)
                        continue
                    dve.tensor_tensor(acc[:, :, :], y[:, :, :], acc[:, :, :], ALU.add).then_inc(y_used, 1)
                    dve.wait_ge(y_used, k + 2)
                    dve.wait_ge(context_free, b + 1)
                    dve.tensor_copy(split[:, 0, :, :], acc[:, :, :]).then_inc(split_hi_done, 1)
                    dve.wait_ge(split_hi_done, b + 1)
                    dve.tensor_tensor(split[:, 1, :, :], acc[:, :, :], split[:, 0, :, :].bitcast(F32),
                                      ALU.subtract).then_inc(split_done, 1)
                    dve.wait_ge(split_done, b + 1)
                    dve.nop().then_inc(acc_done, 1)

            split_x(0)
            split_w(0, raw1, w1h, w1l, raw1_in, w1_hi_done, w1_done)
            with dve.Fori(0, B - 1) as b:
                batch(b, False)
            batch(B - 1, True)


HEADS, DK = 8, 128
PAIRS = HEADS // 2
QT = L // P
KT = L // P
FEATS = 192
FP = FEATS // 2
DIST = 2 * L
WIN = L + P
HALF_WIN = WIN // 2
SCALE = float(DK) ** -0.5

REL = ["rel0", "rel1", "rel2", "rel3"]
EVEN = ["q0", "k0", "out0", "out1", "s0.0", "s0.1", "s0.2", "s0.3", "val0", "t0.0", "t0.1", "t0.2", "t0.3"]
ODD = ["q1", "k1", "val1", "s1.0", "s1.1", "s1.2", "s1.3", "v0", "v1", "t1.0", "t1.1", "t1.2", "t1.3"]
RING = [4, 5, 3, 2, 1, 0, 4, 5, 2, 3, 1, 0, 4, 2, 5, 1, 3, 0, 4, 2, 1, 5, 3, 0, 2, 1]
BANK = dict(zip(EVEN + ODD, RING), rel0=4, rel1=5, rel2=3, rel3=0, last0=4, last1=5)


class Step:

    def __init__(self, hp, bb, odd, leave_out=(), before=None):
        self.pair_start = isinstance(bb, int)
        rel = REL if self.pair_start and odd == 0 else []
        names = rel + EVEN + ODD
        self.items = [n for n in names if n not in leave_out]
        self.hp, self.bb, self.odd = hp, bb, odd
        self.g, self.m = B * hp + 2 * bb + odd, B // 2 * hp + bb
        self.b = 2 * bb + odd
        self.before = before if before is not None else EVEN + ODD

    def number(self, base, name):
        return base + self.items.index(name)


def takes_high(name):
    return name[0] != "s" and not name.startswith(("out", "last"))


class AttentionAhead:

    def __init__(self, s, x1, xT, wqkvo, wrel, positions, qbias, b_out, identity):
        self.x1 = x1
        self.raw_w, self.raw_rel = s.sb("raw_w", [P, 4, L]), s.sb("raw_rel", [FP, 2, 2 * DK])
        self.raw_qb = s.sb("raw_qb", [P, 4])
        self.pos = s.sb("pos", [FP, 4, L])
        self.bo = s.sb("bo", [P, KD])
        self.ident = s.sb("ident", [P, P])
        self.loads = ((x1[:, :, :, :], xT.rearrange("(k p) b l -> p k b l", p=P)), (self.bo[:, :], b_out),
                      (self.ident[:, :], identity), (self.pos[:, :, :], positions)) + self.pair(wrel, qbias, wqkvo, 0)

    def pair(self, wrel, qbias, wqkvo, hp):
        return ((self.raw_rel[:, :, :], wrel[bass.ds(hp, 1)].rearrange("h p m n -> p (h m) n")),
                (self.raw_qb[:, :], qbias[bass.ds(hp, 1)].rearrange("h p n -> p (h n)")),
                (self.raw_w[:, :, :], wqkvo[bass.ds(hp, 1)].rearrange("h p m n -> p (h m) n")))


def attention(nc, wqkvo, wrel, qbias, context, skew, ahead, next_loads):
    with ExitStack() as ctx:
        s = Scope(nc, ctx)
        part = s.sb("part", [P, 2, 2, KD, L], F32R)
        x1, raw_w, raw_rel, raw_qb, pos, ident = (
            ahead.x1, ahead.raw_w, ahead.raw_rel, ahead.raw_qb, ahead.pos, ahead.ident)
        wh, wl = s.sb("wh", [P, 4, L], F32R), s.sb("wl", [P, 4, L], F32R)
        rel_h, rel_l = s.sb("rel_h", [P, 2, DIST], F32R), s.sb("rel_l", [P, 2, DIST], F32R)
        qb = s.sb("qb", [P, 4])
        prob = s.sb("prob", [P, 8, L])
        qe_h, qe_l = s.sb("qe_h", [P, 2, L], F32R), s.sb("qe_l", [P, 2, L], F32R)
        qp_h, qp_l = s.sb("qp_h", [P, L], F32R), s.sb("qp_l", [P, L], F32R)
        k_h, k_l = s.sb("k_h", [P, 2, L], F32R), s.sb("k_l", [P, 2, L], F32R)
        v_h, v_l = s.sb("v_h", [P, KT, 2 * DK], F32R), s.sb("v_l", [P, KT, 2 * DK], F32R)
        pt_h, pt_l = s.sb("pt_h", [P, KT, L], F32R), s.sb("pt_l", [P, KT, L], F32R)
        o_h, o_l = s.sb("o_h", [P, 2, L], F32R), s.sb("o_l", [P, 2, L], F32R)
        dist = s.sb("dist", [P, QT, WIN])
        nmax, total, rinv = s.sb("nmax", [P, 8]), s.sb("total", [P, 8]), s.sb("rinv", [P, 8])
        banks = [s.ps(f"bank{i}") for i in range(6)]
        dist_ps = [s.ps(f"dist_ps{i}") for i in range(2)]

        pair_in, next_in = s.sem("pair_in"), s.sem("next_in")
        w_hi_done, w_done, wo_hi_done, wo_done, bias_ready = (
            s.sem(n) for n in ("w_hi_done", "w_done", "wo_hi_done", "wo_done", "bias_ready"))
        part_in = [s.sem(f"part_in{i}") for i in range(2)]
        item_full, high_done, freed = s.sem("item_full"), s.sem("high_done"), s.sem("freed")
        dist_full, dist_left, dist_right = s.sem("dist_full"), s.sem("dist_left"), s.sem("dist_right")
        stored = [s.sem(f"stored{i}") for i in range(QT)]
        skewed = [s.sem(f"skewed{i}") for i in range(8)]
        scores_seen, exp_done, rinv_done, prob_done = (
            s.sem(n) for n in ("scores_seen", "exp_done", "rinv_done", "prob_done"))
        block = ctx.enter_context(nc.Block())

        start = [n for n in EVEN if n not in ("q0", "k0")] + ["val1"]
        step0 = Step(0, 0, 0, leave_out=start, before=[])
        step1 = Step(0, 0, 1, leave_out=("out0", "out1"), before=step0.items)
        after = Step(PAIRS, 0, 0)
        after.items = ["out0", "out1"] + EVEN[4:] + ["val1", "last0", "last1"]

        def bases(keep):
            size = [sum(map(keep, x.items)) for x in (step0, step1)]
            full, rel = sum(map(keep, EVEN + ODD)), sum(map(keep, REL))

            def base(step):
                if step is step0:
                    return 0
                if step is step1:
                    return size[0]
                rest = size[0] + size[1] + full * (step.g - 2) + rel * step.hp
                return rest - rel if step.items[0] in (REL[0], "out0") else rest
            return base

        item_base, high_base = bases(lambda n: True), bases(takes_high)

        def item(step, name):
            return item_base(step) + step.items.index(name)

        def high(step, name):
            return high_base(step) + [n for n in step.items if takes_high(n)].index(name)

        def user_before(step, name):
            i = step.items.index(name)
            order = step.before + step.items[:i]
            for back, other in enumerate(reversed(order)):
                if BANK[other] == BANK[name]:
                    return item(step, name) - 1 - back
            return None

        def steps(eng, step, finish):
            step(step0)
            step(step1)
            with eng.Fori(1, B // 2) as bb:
                step(Step(0, bb, 0))
                step(Step(0, bb, 1))
            with eng.Fori(1, PAIRS) as hp:
                step(Step(hp, 0, 0))
                step(Step(hp, 0, 1))
                with eng.Fori(1, B // 2) as bb:
                    step(Step(hp, bb, 0))
                    step(Step(hp, bb, 1))
            finish(after)

        @block.sync
        def _(sp):
            def load_pair(hp):
                for dst, src in ahead.pair(wrel, qbias, wqkvo, hp):
                    sp.dma_start(dst, src).then_inc(pair_in, 16)

            def load_part(b, odd):
                sp.dma_start(part[:, odd, :, :, :].rearrange("p s k l -> p (s k l)").bitcast(F32),
                             context[bass.ds(b, 1)].rearrange("b p s k l -> p (b s k l)")).then_inc(part_in[odd], 16)

            def skew_unit(at, h):
                n = 2 * at.g + h

                def load(q):
                    sp.wait_ge(stored[q], 16 * n + 16)
                    src = bass.AP(tensor=skew.tensor, offset=(4 * h + q) * P * WIN + P - 1,
                                  ap=[[WIN - 1, P], [1, L]])
                    sp.dma_start(prob[:, 4 * h + q, :], src).then_inc(skewed[4 * h + q], 16)

                for q in range(QT):
                    sp.wait_ge(dist_left, QT * n + q + 1)
                    sp.wait_ge(dist_right, QT * n + q + 1)
                    dst = bass.AP(tensor=skew.tensor, offset=(4 * h + q) * P * WIN, ap=[[WIN, P], [1, WIN]])
                    sp.dma_start(dst, dist[:, q, :]).then_inc(stored[q], 16)
                    if q:
                        load(q - 1)
                load(QT - 1)

            def step(at):
                skew_unit(at, 0)
                skew_unit(at, 1)
                sp.wait_ge(item_full, item(at, "v1") + 1)
                load_part((at.b + 2) % B, at.odd)
                if at.pair_start and at.odd == 1:
                    sp.wait_ge(wo_done, at.hp + 1)
                    load_pair((at.hp + 1) % PAIRS)

            load_part(0, 0)
            load_part(1, 1)
            sp.nop().then_inc(pair_in, 48)
            for dst, src in next_loads:
                sp.dma_start(dst, src).then_inc(next_in, 16)
            steps(sp, step, lambda at: None)
            for i in range(2):
                sp.wait_ge(part_in[i], 16 * (PAIRS * B // 2 + 1))
            sp.wait_ge(pair_in, 48 * (PAIRS + 1))
            sp.wait_ge(next_in, 16 * len(next_loads))

        @block.tensor
        def _(pe):
            def product(out, terms, start=True, stop=True):
                for i, (a, x) in enumerate(terms):
                    mm = pe.matmul(out, a, x, start=start and i == 0, stop=stop and i == len(terms) - 1)
                return mm

            def passes(ah, al, mh, ml):
                return ((ah, mh), (ah, ml), (al, mh))

            def take_bank(at, name):
                free = user_before(at, name)
                if free is not None:
                    pe.wait_ge(freed, free + 1)
                return banks[BANK[name]]

            def distance_keys(at):
                pe.wait_ge(pair_in, 48 * at.hp + 48)
                for h in range(2):
                    for half in range(2):
                        bank = take_bank(at, f"rel{2 * h + half}")
                        terms = [(raw_rel[:, k, h * DK:(h + 1) * DK], pos[:, 2 * k + half, :]) for k in range(2)]
                        product(bank[:, :], terms).then_inc(item_full, 1)

            def w(m, k, a, z):
                return wh[:, m, 2 * DK * k + a:2 * DK * k + z], wl[:, m, 2 * DK * k + a:2 * DK * k + z]

            def project_qk(at, h):
                if h == 0:
                    pe.wait_ge(part_in[at.odd], 16 * at.m + 16)
                for m, name in enumerate((f"q{h}", f"k{h}")):
                    bank = take_bank(at, name)
                    terms = []
                    for k in range(KD):
                        terms += passes(*w(m, k, h * DK, (h + 1) * DK), part[:, at.odd, 0, k, :],
                                        part[:, at.odd, 1, k, :])
                    product(bank[:, :], terms).then_inc(item_full, 1)

            def v_tile(at, t):
                bank = take_bank(at, f"v{t // 2}") if t % 2 == 0 else banks[BANK[f"v{t // 2}"]]
                rows = slice(t * P, (t + 1) * P)
                terms = []
                for k in range(KD):
                    wkh, wkl = w(2, k, 0, 2 * DK)
                    ch, cl = part[:, at.odd, 0, k, rows], part[:, at.odd, 1, k, rows]
                    terms += ((ch, wkh), (ch, wkl), (cl, wkh))
                mm = product(bank[:, (t % 2) * 2 * DK:(t % 2 + 1) * 2 * DK], terms)
                if t % 2:
                    mm.then_inc(item_full, 1)

            def values_part(at, h, k):
                name = f"val{h}"
                bank = take_bank(at, name) if k == 0 else banks[BANK[name]]
                cols = slice(h * DK, (h + 1) * DK)
                mm = product(bank[:, :], passes(v_h[:, k, cols], v_l[:, k, cols], pt_h[:, k, :], pt_l[:, k, :]),
                             start=(k == 0), stop=(k == KT - 1))
                if k == KT - 1:
                    mm.then_inc(item_full, 1)

            def values(at, h):
                for k in range(KT):
                    values_part(at, h, k)

            def scores(at, slot):
                h = 1 - slot
                for q in range(QT):
                    bank = take_bank(at, f"s{slot}.{q}")
                    cols = slice(q * P, (q + 1) * P)
                    product(bank[:, :], passes(qe_h[:, h, cols], qe_l[:, h, cols], k_h[:, h, :], k_l[:, h, :])
                            ).then_inc(item_full, 1)

            def distances(at, h, between):
                n = 2 * at.g + h
                pe.wait_ge(freed, item(at, f"q{h}") + 1)
                for q in range(QT):
                    cols = slice(q * P, (q + 1) * P)
                    for half, left in enumerate((dist_left, dist_right)):
                        if at is not step0 or 2 * n + q > 0:
                            pe.wait_ge(left, QT * n + q)
                        a = L - P - q * P + half * HALF_WIN
                        product(dist_ps[half][:, 0:HALF_WIN],
                                passes(qp_h[:, cols], qp_l[:, cols], rel_h[:, h, a:a + HALF_WIN],
                                       rel_l[:, h, a:a + HALF_WIN])).then_inc(dist_full, 1)
                    between(q)

            def transposes(at, slot):
                h, n = 1 - slot, 2 * at.g + slot - 1
                for q in range(QT):
                    bank = take_bank(at, f"t{slot}.{q}")
                    pe.wait_ge(prob_done, QT * n + q + 1)
                    for k in range(KT):
                        mm = pe.transpose(bank[:, k * P:(k + 1) * P], prob[:, 4 * h + q, k * P:(k + 1) * P],
                                          ident[:, :])
                    mm.then_inc(item_full, 1)

            def project_out(at, names):
                for oc, name in enumerate(names):
                    bank = take_bank(at, name)
                    terms = []
                    for h in range(2):
                        cols = slice(2 * DK * h + oc * P, 2 * DK * h + (oc + 1) * P)
                        terms += passes(wh[:, 3, cols], wl[:, 3, cols], o_h[:, h, :], o_l[:, h, :])
                    product(bank[:, :], terms).then_inc(item_full, 1)

            def split_before(at, name):
                pe.wait_ge(freed, item_base(at) - len(at.before) + at.before.index(name) + 1)

            def step(at):
                if "rel0" in at.items:
                    distance_keys(at)
                    pe.wait_ge(w_done, 2 * at.hp + 2)
                project_qk(at, 0)
                if "out0" in at.items:
                    if not at.pair_start:
                        pe.wait_ge(wo_done, at.hp + 1)
                    split_before(at, "val1")
                    project_out(at, ("out0", "out1"))
                if "s0.0" in at.items:
                    split_before(at, "k1")
                    scores(at, 0)
                    split_before(at, "t1.3")
                    distances(at, 0, lambda q: values_part(at, 0, q))
                    transposes(at, 0)
                else:
                    pe.wait_ge(freed, item(at, "rel3") + 1)
                    distances(at, 0, lambda q: None)
                project_qk(at, 1)
                if "val1" in at.items:
                    pe.wait_ge(freed, item(at, "t0.3") + 1)
                    values(at, 1)
                pe.wait_ge(freed, item(at, "k0") + 1)
                scores(at, 1)
                distances(at, 1, lambda q: v_tile(at, q))
                transposes(at, 1)

            def finish(at):
                split_before(at, "val1")
                project_out(at, ("out0", "out1"))
                scores(at, 0)
                split_before(at, "t1.3")
                values(at, 0)
                transposes(at, 0)
                pe.wait_ge(freed, item(at, "t0.3") + 1)
                values(at, 1)
                pe.wait_ge(freed, item(at, "val1") + 1)
                project_out(at, ("last0", "last1"))

            steps(pe, step, finish)

        @block.scalar
        def _(act):
            def split_weights(hp):
                act.wait_ge(pair_in, 48 * hp + 48)
                act.activation(wh[:, 0, :], raw_w[:, 0, :], ACT.Copy, scale=SCALE).then_inc(w_hi_done, 1)
                act.activation(wh[:, 1:3, :].rearrange("p m n -> p (m n)"),
                               raw_w[:, 1:3, :].rearrange("p m n -> p (m n)"), ACT.Copy).then_inc(w_hi_done, 1)

            def take(at, name, dst, view=lambda a: a):
                act.wait_ge(item_full, item(at, name) + 1)
                act.copy(dst, view(banks[BANK[name]][:, :])).then_inc(high_done, 1)

            def take_qk(at, h):
                act.wait_ge(item_full, item(at, f"q{h}") + 1)
                if "rel0" in at.items and h == 0:
                    act.wait_ge(bias_ready, at.hp + 1)
                bank = banks[BANK[f"q{h}"]]
                act.activation(qe_h[:, h, :], bank[:, :], ACT.Identity, bias=qb[:, h:h + 1])
                act.activation(qp_h[:, :], bank[:, :], ACT.Identity, bias=qb[:, 2 + h:3 + h]).then_inc(high_done, 1)
                take(at, f"k{h}", k_h[:, h, :])

            def exponentials(at, slot, q):
                h, n = 1 - slot, 2 * at.g + slot - 1
                i = 4 * h + q
                act.wait_ge(freed, item(at, f"s{slot}.{q}") + 1)
                act.activation(prob[:, i, :], prob[:, i, :], ACT.Exp, scale=-1.0, bias=nmax[:, i:i + 1],
                               accum_out=total[:, i:i + 1]).then_inc(exp_done, 1)

            def left_half(at, h, q):
                n = 2 * at.g + h
                if at is not step0 or n > 0:
                    act.wait_ge(stored[q], 16 * n)
                act.wait_ge(dist_full, 2 * QT * n + 2 * q + 1)
                act.copy(dist[:, q, 0:HALF_WIN], dist_ps[0][:, 0:HALF_WIN]).then_inc(dist_left, 1)

            def take_v(at, i):
                take(at, f"v{i}", v_h[:, 2 * i:2 * i + 2, :], lambda a: a.rearrange("p (t n) -> p t n", t=2))

            def take_transposed(at, slot):
                for q in range(QT):
                    take(at, f"t{slot}.{q}", pt_h[:, :, q * P:(q + 1) * P],
                         lambda a: a.rearrange("p (k n) -> p k n", k=KT))

            def slot(at, h, has_scores, after_tile):
                for q in range(QT):
                    if has_scores:
                        for e in {0: (0, 1), 1: (2,), 2: (3,), 3: ()}[q]:
                            exponentials(at, h, e)
                    if q == 2:
                        after_tile(0)
                    left_half(at, h, q)
                after_tile(1)

            def step(at):
                if "rel0" in at.items:
                    split_weights(at.hp)
                    for i, name in enumerate(REL):
                        take(at, name, rel_h[:, i // 2, (i % 2) * L:(i % 2 + 1) * L])
                take_qk(at, 0)
                before = "s0.0" in at.items
                slot(at, 0, before, lambda i: None)
                if before:
                    take(at, "val0", o_h[:, 0, :])
                    take_transposed(at, 0)
                take_qk(at, 1)
                if "val1" in at.items:
                    take(at, "val1", o_h[:, 1, :])
                slot(at, 1, True, lambda i: take_v(at, i))
                take_transposed(at, 1)
                if at.pair_start and at.odd == 1:
                    act.copy(wh[:, 3, :], raw_w[:, 3, :]).then_inc(wo_hi_done, 1)

            def finish(at):
                for q in range(QT):
                    exponentials(at, 0, q)
                take(at, "val0", o_h[:, 0, :])
                take_transposed(at, 0)
                take(at, "val1", o_h[:, 1, :])

            steps(act, step, finish)

        @block.gpsimd
        def _(pool):
            with pool.Fori(0, PAIRS * B) as g:
                for h in range(2):
                    for q in range(QT):
                        i = 4 * h + q
                        pool.wait_ge(rinv_done, QT * (2 * g + h) + q + 1)
                        pool.tensor_tensor(prob[:, i, :], prob[:, i, :], rinv[:, i:i + 1].to_broadcast([P, L]),
                                           ALU.mult).then_inc(prob_done, 1)

        @block.vector
        def _(dve):
            def split_weights(hp):
                dve.wait_ge(pair_in, 48 * hp + 48)
                dve.tensor_copy(qb[:, :], raw_qb[:, :]).then_inc(bias_ready, 1)
                dve.wait_ge(w_hi_done, 2 * hp + 1)
                dve.scalar_tensor_tensor(out=wl[:, 0, :], in0=raw_w[:, 0, :], scalar=SCALE,
                                         in1=wh[:, 0, :].bitcast(F32), op0=ALU.mult, op1=ALU.subtract
                                         ).then_inc(w_done, 1)
                dve.wait_ge(w_hi_done, 2 * hp + 2)
                dve.tensor_tensor(wl[:, 1:3, :], raw_w[:, 1:3, :], wh[:, 1:3, :].bitcast(F32), ALU.subtract
                                  ).then_inc(w_done, 1)
                dve.wait_ge(bias_ready, hp + 1)

            def take(at, name, lo, hi, view=lambda a: a):
                dve.wait_ge(high_done, high(at, name) + 1)
                dve.tensor_tensor(lo, view(banks[BANK[name]][:, :]), hi.bitcast(F32), ALU.subtract).then_inc(freed, 1)

            def take_qk(at, h):
                dve.wait_ge(high_done, high(at, f"q{h}") + 1)
                bank = banks[BANK[f"q{h}"]]
                dve.scalar_tensor_tensor(out=qe_l[:, h, :], in0=bank[:, :], scalar=qb[:, h:h + 1],
                                         in1=qe_h[:, h, :].bitcast(F32), op0=ALU.add, op1=ALU.subtract)
                dve.scalar_tensor_tensor(out=qp_l[:, :], in0=bank[:, :], scalar=qb[:, 2 + h:3 + h],
                                         in1=qp_h[:, :].bitcast(F32), op0=ALU.add, op1=ALU.subtract
                                         ).then_inc(freed, 1)
                take(at, f"k{h}", k_l[:, h, :], k_h[:, h, :])

            def logits(at, slot, q):
                h, m = 1 - slot, at.g + slot - 1
                i = 4 * h + q
                dve.wait_ge(skewed[i], 16 * m + 16 if slot == 0 else 16 * at.g + 16)
                dve.wait_ge(item_full, item(at, f"s{slot}.{q}") + 1)
                dve.nop().then_inc(scores_seen, 1)
                dve.tensor_tensor_reduce(out=prob[:, i, :], in0=banks[BANK[f"s{slot}.{q}"]][:, :],
                                         in1=prob[:, i, :], scale=-1.0, scalar=3.0e38, op0=ALU.add, op1=ALU.min,
                                         accum_out=nmax[:, i:i + 1]).then_inc(freed, 1)

            def inverse(at, slot, q):
                h, n = 1 - slot, 2 * at.g + slot - 1
                i = 4 * h + q
                dve.wait_ge(exp_done, QT * n + q + 1)
                dve.reciprocal(rinv[:, i:i + 1], total[:, i:i + 1]).then_inc(rinv_done, 1)

            def right_half(at, h, q):
                n = 2 * at.g + h
                if at is not step0 or n > 0:
                    dve.wait_ge(stored[q], 16 * n)
                dve.wait_ge(dist_full, 2 * QT * n + 2 * q + 2)
                dve.tensor_copy(dist[:, q, HALF_WIN:WIN], dist_ps[1][:, 0:HALF_WIN]).then_inc(dist_right, 1)

            def take_v(at, i):
                take(at, f"v{i}", v_l[:, 2 * i:2 * i + 2, :], v_h[:, 2 * i:2 * i + 2, :],
                     lambda a: a.rearrange("p (t n) -> p t n", t=2))

            def take_transposed(at, slot):
                for q in range(QT):
                    cols = slice(q * P, (q + 1) * P)
                    take(at, f"t{slot}.{q}", pt_l[:, :, cols], pt_h[:, :, cols],
                         lambda a: a.rearrange("p (k n) -> p k n", k=KT))

            def add_out(at, names, b):
                for oc, name in enumerate(names):
                    dve.wait_ge(item_full, item(at, name) + 1)
                    acc = x1[:, oc, bass.ds(b, 1), :].rearrange("p b l -> p (b l)")
                    dve.tensor_tensor(acc, banks[BANK[name]][:, :], acc, ALU.add).then_inc(freed, 1)

            def slot(at, h, has_scores, after_tile):
                if has_scores:
                    logits(at, h, 0)
                    logits(at, h, 1)
                    logits(at, h, 2)
                    inverse(at, h, 0)
                    logits(at, h, 3)
                    inverse(at, h, 1)
                for q in range(QT):
                    right_half(at, h, q)
                    if has_scores and q < 2:
                        inverse(at, h, q + 2)
                    if q == 1:
                        after_tile(0)
                after_tile(1)

            def step(at):
                if "rel0" in at.items:
                    split_weights(at.hp)
                    for i, name in enumerate(REL):
                        cols = slice((i % 2) * L, (i % 2 + 1) * L)
                        take(at, name, rel_l[:, i // 2, cols], rel_h[:, i // 2, cols])
                take_qk(at, 0)
                if "out0" in at.items:
                    add_out(at, ("out0", "out1"), B - 2 + at.odd if at.pair_start else 2 * at.bb + at.odd - 2)
                before = "s0.0" in at.items
                slot(at, 0, before, lambda i: None)
                if before:
                    take(at, "val0", o_l[:, 0, :], o_h[:, 0, :])
                    take_transposed(at, 0)
                take_qk(at, 1)
                if "val1" in at.items:
                    take(at, "val1", o_l[:, 1, :], o_h[:, 1, :])
                slot(at, 1, True, lambda i: take_v(at, i))
                take_transposed(at, 1)
                if at.pair_start and at.odd == 1:
                    dve.wait_ge(wo_hi_done, at.hp + 1)
                    dve.tensor_tensor(wl[:, 3, :], raw_w[:, 3, :], wh[:, 3, :].bitcast(F32), ALU.subtract
                                      ).then_inc(wo_done, 1)

            def finish(at):
                add_out(at, ("out0", "out1"), B - 2)
                for q in range(QT):
                    logits(at, 0, q)
                for q in range(QT):
                    inverse(at, 0, q)
                take(at, "val0", o_l[:, 0, :], o_h[:, 0, :])
                take_transposed(at, 0)
                take(at, "val1", o_l[:, 1, :], o_h[:, 1, :])
                add_out(at, ("last0", "last1"), B - 1)

            steps(dve, step, finish)


GATES = 4
GC = GATES * D // P
FFN_EXPERTS = 8
TB = 64
BLOCKS = L // TB
SUB = TB // 4
UP = 16.0



MADE = 9


class RecurrenceAhead:

    def __init__(self, s, condT, wx, wh, gate_bias, router_w, router_b, row_mask, count8, identity):
        self.raw = s.sb("raw_gates", [P, 2, KD, GC * P])
        self.h0 = s.sb("h0", [P, KD, B])
        self.gbias, self.rbias = s.sb("gbias", [P, GC]), s.sb("rbias", [P, 8])
        self.mask, self.count = s.sb("mask", [2, 2]), s.sb("count", [P, 8])
        self.rraw = s.sb("rraw", [P, KD, 8])
        self.ident = s.sb("ident3", [P, P])
        self.loads = ((self.raw[:, 0, :, :], wx.rearrange("(k p) n -> p k n", p=P)),
                      (self.raw[:, 1, :, :], wh.rearrange("(k p) n -> p k n", p=P)),
                      (self.ident[:, :], identity), (self.h0[:, :, :], condT.rearrange("(k p) b -> p k b", p=P)),
                      (self.gbias[:, :], gate_bias), (self.rbias[:, :], router_b), (self.count[:, :], count8),
                      (self.rraw[:, :, :], router_w.rearrange("(k p) e -> p k e", p=P)),
                      (self.mask[:, :], row_mask))


def recurrence(nc, ahead, expert_w, expert_b, x1, out):
    GK = GC * P
    EK = FFN_EXPERTS * D
    with ExitStack() as ctx:
        s = Scope(nc, ctx)
        raw = s.sb("raw_experts", [P, KD, EK])
        raw_gates, h0, gbias, rbias, mask, count, rraw, ident = (
            ahead.raw, ahead.h0, ahead.gbias, ahead.rbias, ahead.mask, ahead.count, ahead.rraw, ahead.ident)
        wxh, wxl = s.sb("wxh", [P, KD * GK], F16), s.sb("wxl", [P, KD * GK], F16)
        whh, whl = s.sb("whh", [P, KD, GK], F16), s.sb("whl", [P, KD, GK], F16)
        weh, wel = s.sb("weh", [P, KD, EK], F16), s.sb("wel", [P, KD, EK], F16)
        wrh, wrl = s.sb("wrh", [P, KD, 8], F16), s.sb("wrl", [P, KD, 8], F16)
        eb, ebh, ebl = s.sb("eb", [2, EK]), s.sb("ebh", [2, EK], F16), s.sb("ebl", [2, EK], F16)
        ebm, rows = s.sb("ebm", [2, EK], F16), s.sb("rows", [2, EK], F16)
        ones2, factor = s.sb("ones2", [2, P], F16), s.sb("factor", [P, 1])
        ident16 = s.sb("ident16", [P, P], F16)
        xs_h, xs_l = s.sb("xs_h", [P, KD, B, TB], F16), s.sb("xs_l", [P, KD, B, TB], F16)
        share = s.sb("share", [P, 2, 2 * TB * GC * B], F16)
        now = s.sb("now", [P, 4, GC, 2 * B], F16)
        hs = s.sb("hs", [P, 4, KD, 2 * B], F16)
        hist = s.sb("hist", [P, 2 * 2 * KD * B * TB], F16)
        f, gi, o = s.sb("forget", [P, 2, 2 * B]), s.sb("cand_in", [P, 2, 4 * B]), s.sb("out_gate", [P, 2, 2 * B])
        cell, fc, ig = s.sb("cell", [P, 2, 2 * B]), s.sb("fc", [P, 2, 2 * B]), s.sb("ig", [P, 2, 2 * B])
        tc, h = s.sb("tc", [P, 2, 2 * B]), s.sb("hidden", [P, 2, 2 * B])
        xt = s.sb("xt", [P, KD, P])
        acc = s.sb("acc3", [P, D])
        logit, zexp, sig_p, sig_n, inv_n, cand, pick = (
            s.sb(n, [P, 8]) for n in ("logit", "zexp", "sig_p", "sig_n", "inv_n", "cand", "pick"))
        top, ztop, zsum, gate, first_top = (s.sb(n, [P, 1]) for n in ("top", "ztop", "zsum", "gate", "first_top"))
        f_ps, gi_ps, o_ps, share_ps, route_ps, xt_ps = (
            s.ps(n) for n in ("f_ps", "gi_ps", "o_ps", "share_ps", "route_ps", "xt_ps"))
        ffn_ps = [s.ps(f"ffn_ps{i}") for i in range(2)]

        experts_in, experts_step, experts_split = s.sem("experts_in"), s.sem("experts_step"), s.sem("experts_split")
        made, gates_hi_done, gates_split = s.sem("made"), s.sem("gates_hi_done"), s.sem("gates_split")
        hi_ready, h_ready, lo_ready = s.sem("hi_ready"), s.sem("h_ready"), s.sem("lo_ready")
        f_full, gi_full, o_full = s.sem("f_full"), s.sem("gi_full"), s.sem("o_full")
        f_added, gi_added, o_added = s.sem("f_added"), s.sem("gi_added"), s.sem("o_added")
        f_done, gi_done, o_done = s.sem("f_done"), s.sem("gi_done"), s.sem("o_done")
        ig_done, cell_done, tanh_done = (s.sem(n) for n in ("ig_done", "cell_done", "tanh_done"))
        hist_done = s.sem("hist_done")
        xs_hi_done, xs_done = s.sem("xs_hi_done"), s.sem("xs_done")
        pre_f, pre_gi, pre_o = f_ps[:, 64:64 + 2 * B], gi_ps[:, 64:64 + 4 * B], o_ps[:, 64:64 + 2 * B]

        share_full, share_hi_done, share_done, now_done = (
            s.sem(n) for n in ("share_full", "share_hi_done", "share_done", "now_done"))
        routed, xt_done, xt_full, acc_init = (s.sem(n) for n in ("routed", "xt_done", "xt_full", "acc_init"))
        logit_done, zmax_done, sig_done, gate_step, pick_done = (
            s.sem(n) for n in ("logit_done", "zmax_done", "sig_done", "gate_step", "pick_done"))
        ffn_full, acc_step, out_sent = s.sem("ffn_full"), s.sem("acc_step"), s.sem("out_sent")
        block = ctx.enter_context(nc.Block())

        def blocks(eng, body, before_routed=lambda: None, start=lambda j: None):
            start(0)
            with eng.Fori(0, 4) as q:
                body(0, q, False, True)
            before_routed()
            with eng.Fori(1, BLOCKS - 1) as j:
                start(j)
                with eng.Fori(0, 4) as q:
                    body(j, q, True, True)
            with eng.Fori(0, 4) as q:
                body(BLOCKS - 1, q, True, False)

        def after(eng, side):
            with eng.Fori(0, 4) as q:
                for i in range(SUB):
                    side(BLOCKS, q, i, True, False)

        two = lambda a: a[:, :].rearrange("p (k n) -> p k n", k=KD)
        GATE_PARTS = ((0, 2 * P, UP), (2 * P, 4 * P, 2 * UP), (4 * P, GK, UP))

        def share_view(part, jb, c):
            v = share[:, part, :].rearrange("p (r t g b) -> p r g b t", r=2, t=TB, g=GC)
            return v[:, bass.ds(jb % 2, 1), bass.ds(c, 1), :, :].rearrange("p r g b t -> p (r g b) t")

        @block.sync
        def _(sp):
            sp.dma_start(raw[:, :, :], expert_w.rearrange("(k p) n -> p k n", p=P)).then_inc(experts_in, 16)
            sp.dma_start(eb[:, :], expert_b).then_inc(experts_in, 16)
            sp.nop().then_inc(out_sent, 32)
            with sp.Fori(1, BLOCKS + 1) as j:
                with sp.Fori(0, 4) as q:
                    sp.wait_ge(acc_step, FFN_EXPERTS * (4 * (j - 1) + q + 1) + 4)
                    for i in range(2):
                        dst = out[bass.ds(2 * q + i, 1), bass.ds(TB * (j - 1), TB), :]
                        sp.dma_start(dst.rearrange("b t d -> (b t) d"), acc[TB * i:TB * (i + 1), :]
                                     ).then_inc(out_sent, 16)
            sp.wait_ge(out_sent, 32 * 4 * BLOCKS + 32)

        @block.tensor
        def _(pe):
            def low_products(bank, slot, g0, g1):
                for g in range(g0, g1):
                    for k in range(KD):
                        pe.matmul(bank[:, (g - g0) * 2 * B:(g - g0) * 2 * B + B], whl[:, k, g * P:(g + 1) * P],
                                  hs[:, slot, k, 0:B], start=False, stop=False, skip_group_check=True)

            def high_products(bank, slot, g0, g1):
                for g in range(g0, g1):
                    for k in range(KD):
                        mm = pe.matmul(bank[:, (g - g0) * 2 * B:(g - g0 + 1) * 2 * B], whh[:, k, g * P:(g + 1) * P],
                                       hs[:, slot, k, :], start=False, stop=True, skip_group_check=True)
                return mm

            def put_share(T, slot, bank, a, z, done):
                pe.wait_ge(done, T + 1)
                pe.matmul(bank[:, 0:(z - a) * 2 * B], ident16[:, :],
                          now[:, slot, a:z, :].rearrange("p g n -> p (g n)"), start=True, stop=False,
                          skip_group_check=True)

            def share_terms(jb, c, lo, hi):
                if lo == 0:
                    pe.wait_ge(share_done, GC * jb + c + 1)
                    pe.wait_ge(xs_done, jb + 1)
                terms = [(w, x, k) for w, x in ((wxh, xs_h), (wxh, xs_l), (wxl, xs_h)) for k in range(KD)]
                for n in range(lo, hi):
                    w, x, k = terms[n]
                    mm = pe.matmul(share_ps[:, :], w[:, bass.ds(P * c + GK * k, P)],
                                   x[:, k, :, :].rearrange("p b t -> p (b t)"), start=(n == 0), stop=(n == 5))
                if hi == 6:
                    mm.then_inc(share_full, 1)

            def hidden(j, part, k, q):
                return hist[:, bass.ds(2048 * ((j + 1) % 2) + 1024 * part + 512 * k + P * q, P)]

            def route(j, q):
                m = 4 * (j - 1) + q
                pe.wait_ge(hist_done, TB * j + 4)
                pe.wait_ge(logit_done, m + 1)
                n = 0
                for part, w in ((0, wrh), (1, wrh), (0, wrl)):
                    for k in range(KD):
                        mm = pe.matmul(route_ps[:, 0:8], hidden(j, part, k, q), w[:, k, :], start=(n == 0),
                                       stop=(n == 5))
                        n += 1
                mm.then_inc(routed, 1)

            def turn_x1(j, q):
                m = 4 * (j - 1) + q
                pe.wait_ge(xt_done, m + 1)
                pe.wait_ge(acc_init, m + 1)
                for k in range(KD):
                    mm = pe.transpose(xt_ps[:, k * P:(k + 1) * P], xt[:, k, :], ident[:, :])
                mm.then_inc(xt_full, 1)

            def experts(j, q, a, z):
                m = 4 * (j - 1) + q
                for n in range(a, z):
                    e, n = divmod(n, 7)
                    bank = ffn_ps[e % 2]
                    cols = slice(2 * D * e, 2 * D * (e + 1))
                    if n == 0:
                        pe.wait_ge(acc_step, FFN_EXPERTS * m + 2 * e + 2)
                        pe.matmul(bank[:, :], ones2[:, :], rows[:, cols], start=True, stop=False)
                        continue
                    part, w, k = [(part, w, k) for part, w in ((0, weh), (1, weh), (0, wel)) for k in range(KD)][n - 1]
                    mm = pe.matmul(bank[:, :], hidden(j, part, k, q), w[:, k, cols], start=False, stop=(n == 6))
                    if n == 6:
                        mm.then_inc(ffn_full, 1)

            EXPERTS_AT = {2: (0, 3), 3: (3, 6), 4: (6, 9), 5: (9, 12), 8: (12, 15), 9: (15, 18), 10: (18, 21),
                          13: (21, 25), 14: (25, 28)}
            SHARE_AT = {6: (0, 0, 3), 7: (0, 3, 6), 11: (1, 0, 3), 12: (1, 3, 6)}

            def side(j, q, i, routing, sharing):
                if routing and i == 1:
                    route(j, q)
                    turn_x1(j, q)
                if routing and i in EXPERTS_AT:
                    experts(j, q, *EXPERTS_AT[i])
                if sharing and i in SHARE_AT:
                    c, lo, hi = SHARE_AT[i]
                    share_terms(j + 1, 2 * q + c, lo, hi)

            def body(j, q, routing, sharing):
                for i in range(SUB):
                    T, slot = TB * j + SUB * q + i, i % 4
                    pe.wait_ge(now_done, T + 1)
                    side(j, q, i, routing, sharing)
                    put_share(T, slot, f_ps, 0, 2, f_done)
                    put_share(T, slot, gi_ps, 2, 6, gi_done)
                    pe.wait_ge(hi_ready, T + 1)
                    low_products(f_ps, slot, 0, 2)
                    low_products(gi_ps, slot, 2, 6)
                    pe.wait_ge(lo_ready, T + 1)
                    high_products(f_ps, slot, 0, 2).then_inc(f_full, 1)
                    high_products(gi_ps, slot, 2, 6).then_inc(gi_full, 1)
                    put_share(T, slot, o_ps, 6, 8, o_done)
                    low_products(o_ps, slot, 6, 8)
                    high_products(o_ps, slot, 6, 8).then_inc(o_full, 1)

            pe.wait_ge(gates_split, 2)
            with pe.Fori(0, GC) as c:
                share_terms(0, c, 0, 6)
            pe.wait_ge(gates_split, 4)
            pe.wait_ge(made, MADE)
            blocks(pe, body, lambda: pe.wait_ge(experts_split, 4))
            after(pe, side)

        @block.scalar
        def _(act):
            for free in (f_done, gi_done, o_done, acc_init):
                act.nop().then_inc(free, 1)

            def high_x1(jb):
                src = x1[:, :, :, bass.ds(TB * jb, TB)]
                for k in range(KD):
                    act.copy(xs_h[:, k, :, :], src[:, k, :, :]).then_inc(xs_hi_done, 1)

            def high_share(jb, c):
                act.wait_ge(share_full, GC * jb + c + 1)
                act.activation(share_view(0, jb, c), share_ps[:, :].rearrange("p (b t) -> p b t", t=TB),
                               ACT.Identity, bias=gbias[:, bass.ds(c, 1)]).then_inc(share_hi_done, 1)

            def side(j, q, i, routing, sharing):
                m = 4 * (j - 1) + q
                if routing and i == 2:
                    act.wait_ge(zmax_done, m + 1)
                    act.activation(sig_p[:, :], zexp[:, :], ACT.Sigmoid).then_inc(sig_done, 1)
                    act.activation(sig_n[:, :], zexp[:, :], ACT.Sigmoid, scale=-1.0).then_inc(sig_done, 1)
                if routing and i == 3:
                    act.wait_ge(xt_full, m + 1)
                    act.wait_ge(out_sent, 32 * m + 32)
                    act.copy(acc[:, :], xt_ps[:, 0:D]).then_inc(acc_init, 1)
                if sharing and i in (7, 12):
                    high_share(j + 1, 2 * q + i // 12)

            def body(j, q, routing, sharing):
                for i in range(SUB):
                    T, p = TB * j + SUB * q + i, i % 2
                    act.wait_ge(f_added, T + 1)
                    act.activation(f[:, p, :], pre_f, ACT.Sigmoid,
                                   scale=1.0 / UP).then_inc(f_done, 1)
                    act.wait_ge(gi_added, T + 1)
                    act.activation(gi[:, p, :], pre_gi, ACT.Sigmoid,
                                   scale=1.0 / UP).then_inc(gi_done, 1)
                    act.wait_ge(o_added, T + 1)
                    act.activation(o[:, p, :], pre_o, ACT.Sigmoid,
                                   scale=1.0 / UP).then_inc(o_done, 1)
                    act.wait_ge(cell_done, T + 1)
                    act.activation(tc[:, p, :], cell[:, p, :], ACT.Tanh, scale=2.0).then_inc(tanh_done, 1)
                    side(j, q, i, routing, sharing)

            high_x1(0)
            for m, hi in ((0, two(wxh)), (1, whh[:, :, :])):
                for i, (a, z, up) in enumerate(GATE_PARTS):
                    act.activation(hi[:, :, a:z], raw_gates[:, m, :, a:z], ACT.Copy, scale=up).then_inc(gates_hi_done, 1)
                if m == 0:
                    act.wait_ge(made, 2)
                    with act.Fori(0, GC) as c:
                        high_share(0, c)
            act.wait_ge(made, MADE)
            blocks(act, body, start=lambda j: high_x1(j + 1))
            after(act, side)

        @block.gpsimd
        def _(pool):
            pool.nop().then_inc(hist_done, 4)

            def tile_x1(j, q):
                src = x1[:, :, bass.ds(2 * q, 2), bass.ds(TB * (j - 1), TB)]
                pool.tensor_copy(xt[:, :, :].rearrange("p k (b t) -> p k b t", b=2), src).then_inc(xt_done, 1)

            def split_experts(q, i):
                cols = bass.ds(2 * D * q, 2 * D)
                k = 0 if i < 5 else 1
                if i == 1 and not isinstance(q, int):
                    pool.wait_ge(experts_in, 32)
                if i in (1, 5):
                    ins = pool.tensor_tensor(raw[:, k, cols], raw[:, k, cols], factor[:, :].to_broadcast([P, 2 * D]), ALU.mult)
                if i in (2, 6):
                    ins = pool.tensor_copy(weh[:, k, cols], raw[:, k, cols])
                if i in (3, 7):
                    ins = pool.tensor_tensor(wel[:, k, cols], raw[:, k, cols], weh[:, k, cols], ALU.subtract)
                if i == 9:
                    ins = pool.tensor_tensor(eb[:, cols], eb[:, cols], factor[0:2, :].to_broadcast([2, 2 * D]), ALU.mult)
                if i == 10:
                    ins = pool.tensor_copy(ebh[:, cols], eb[:, cols])
                if i == 11:
                    ins = pool.tensor_tensor(ebl[:, cols], eb[:, cols], ebh[:, cols], ALU.subtract)
                if i == 12:
                    ins = pool.tensor_tensor(ebm[:, cols], ebh[:, cols], mask[:, 0:1].to_broadcast([2, 2 * D]), ALU.mult)
                if i == 13:
                    ins = pool.tensor_tensor(ebl[:, cols], ebl[:, cols], mask[:, 1:2].to_broadcast([2, 2 * D]), ALU.mult)
                if i == 14:
                    pool.tensor_tensor(rows[:, cols], ebl[:, cols], ebm[:, cols], ALU.add).then_inc(experts_split, 1)
                elif i in EXPERT_OPS:
                    ins.then_inc(experts_step, 1)
                    pool.wait_ge(experts_step, len(EXPERT_OPS) * q + EXPERT_OPS.index(i) + 1)

            EXPERT_OPS = (1, 2, 3, 5, 6, 7, 9, 10, 11, 12, 13)

            def share_of(t, base, slot):
                src = share[:, :, bass.ds(((base + t) % (2 * TB)) * (GC * B), GC * B)]
                pool.tensor_copy(now[:, slot, :, :].rearrange("p g (s b) -> p s g b", s=2),
                                 src.rearrange("p s (g b) -> p s g b", b=B)).then_inc(now_done, 1)

            def body(j, q, routing, sharing):
                for i in range(SUB):
                    T = TB * j + SUB * q + i
                    if routing and i == 0:
                        tile_x1(j, q)
                    pool.wait_ge(lo_ready, T + 2)
                    rows_t = hist[:, :].rearrange("p (n t) -> p n t", t=TB)
                    dst = rows_t[:, bass.ds(2 * KD * B * (j % 2), 2 * KD * B), bass.ds(SUB * q + i, 1)]
                    pool.tensor_copy(dst.rearrange("p (s k b) t -> p s k (b t)", s=2, k=KD),
                                     hs[:, (i + 1) % 4, :, :].rearrange("p k (s b) -> p s k b", s=2)
                                     ).then_inc(hist_done, 1)
                    if sharing and i == SUB - 3:
                        pool.wait_ge(share_done, GC * (j + 1) + 2 * q + 2 + 1)
                    share_of(SUB * q + i + 3, (j % 2) * TB, (i + 3) % 4)
                    if not routing:
                        split_experts(q, i)

            pool.wait_ge(made, MADE)
            pool.wait_ge(share_done, GC + 1)
            for t in range(3):
                src = share[:, :, t * GC * B:(t + 1) * GC * B]
                pool.tensor_copy(now[:, t, :, :].rearrange("p g (s b) -> p s g b", s=2),
                                 src.rearrange("p s (g b) -> p s g b", b=B)).then_inc(now_done, 1)
            blocks(pool, body)
            with pool.Fori(0, 4) as q:
                pool.wait_ge(xt_full, 4 * (BLOCKS - 1) + q)
                tile_x1(BLOCKS, q)

        @block.vector
        def _(dve):
            dve.nop().then_inc(share_done, 1)
            dve.nop().then_inc(logit_done, 1)
            dve.nop().then_inc(acc_step, 4)
            count_made = [0]

            def then(ins):
                count_made[0] += 1
                ins.then_inc(made, 1)
                dve.wait_ge(made, count_made[0])

            then(dve.tensor_scalar(gbias[:, :], gbias[:, :], UP, None, ALU.mult))
            then(dve.tensor_scalar(gbias[:, 2:4], gbias[:, 2:4], 2.0, None, ALU.mult))

            def low_x1(jb):
                src = x1[:, :, :, bass.ds(TB * jb, TB)]
                for k in range(KD):
                    dve.wait_ge(xs_hi_done, KD * jb + k + 1)
                    ins = dve.tensor_tensor(xs_l[:, k, :, :], src[:, k, :, :], xs_h[:, k, :, :], ALU.subtract)
                ins.then_inc(xs_done, 1)

            low_x1(0)

            def low_gates(m, hi, lo):
                for i, (a, z, up) in enumerate(GATE_PARTS):
                    dve.wait_ge(gates_hi_done, len(GATE_PARTS) * m + i + 1)
                    ins = dve.scalar_tensor_tensor(out=lo[:, :, a:z], in0=raw_gates[:, m, :, a:z], scalar=up,
                                                   in1=hi[:, :, a:z], op0=ALU.mult, op1=ALU.subtract)
                ins.then_inc(gates_split, 2)

            def low_share(jb, c):
                dve.wait_ge(share_hi_done, GC * jb + c + 1)
                dve.scalar_tensor_tensor(out=share_view(1, jb, c),
                                         in0=share_ps[:, :].rearrange("p (b t) -> p b t", t=TB),
                                         scalar=gbias[:, bass.ds(c, 1)], in1=share_view(0, jb, c),
                                         op0=ALU.add, op1=ALU.subtract).then_inc(share_done, 1)

            def side(j, q, i, routing, sharing):
                m = 4 * (j - 1) + q
                G = 7
                if routing and i == 1:
                    dve.wait_ge(routed, m + 1)
                    dve.scalar_tensor_tensor(out=logit[:, :], in0=route_ps[:, 0:8], scalar=1.0 / UP,
                                             in1=rbias[:, :], op0=ALU.mult, op1=ALU.add).then_inc(logit_done, 1)
                    dve.wait_ge(logit_done, m + 2)
                    dve.tensor_reduce(top[:, :], logit[:, :], AX.X, ALU.max).then_inc(gate_step, 1)
                    dve.wait_ge(gate_step, G * m + 1)
                    dve.tensor_scalar(zexp[:, :], logit[:, :], top[:, 0:1], None, ALU.subtract).then_inc(zmax_done, 1)
                if routing and i == 2:
                    dve.tensor_scalar(cand[:, :], logit[:, :], top[:, 0:1], None, ALU.is_lt).then_inc(gate_step, 1)
                    dve.wait_ge(gate_step, G * m + 2)
                    dve.scalar_tensor_tensor(out=cand[:, :], in0=cand[:, :], scalar=8.0, in1=count[:, :],
                                             op0=ALU.mult, op1=ALU.add).then_inc(gate_step, 1)
                    dve.wait_ge(gate_step, G * m + 3)
                    dve.tensor_reduce(first_top[:, :], cand[:, :], AX.X, ALU.min).then_inc(gate_step, 1)
                if routing and i == 3:
                    dve.wait_ge(sig_done, 2 * m + 2)
                    dve.reciprocal(inv_n[:, :], sig_n[:, :]).then_inc(gate_step, 1)
                    dve.wait_ge(gate_step, G * m + 5)
                    dve.tensor_tensor(inv_n[:, :], inv_n[:, :], sig_p[:, :], ALU.mult).then_inc(gate_step, 1)
                    dve.wait_ge(gate_step, G * m + 6)
                    dve.tensor_reduce(zsum[:, :], inv_n[:, :], AX.X, ALU.add).then_inc(gate_step, 1)
                if routing and i == 4:
                    dve.wait_ge(gate_step, G * m + 7)
                    dve.reciprocal(gate[:, :], zsum[:, :]).then_inc(pick_done, 1)
                    dve.wait_ge(pick_done, 3 * m + 1)
                    dve.tensor_scalar(gate[:, :], gate[:, :], 1.0 / UP, None, ALU.mult).then_inc(pick_done, 1)
                    dve.wait_ge(pick_done, 3 * m + 2)
                    dve.tensor_scalar(pick[:, :], count[:, :], first_top[:, 0:1], gate[:, 0:1], ALU.is_equal,
                                      ALU.mult).then_inc(pick_done, 1)
                ADD_AT = {5: 0, 6: 1, 9: 2, 10: 3, 11: 4, 12: 5, 14: 6, 15: 7}
                if routing and i in ADD_AT:
                    e = ADD_AT[i]
                    if e == 0:
                        dve.wait_ge(pick_done, 3 * m + 3)
                        dve.wait_ge(acc_init, m + 2)
                    else:
                        dve.wait_ge(acc_step, FFN_EXPERTS * m + e + 4)
                    dve.wait_ge(ffn_full, 4 * m + e // 2 + 1)
                    dve.scalar_tensor_tensor(out=acc[:, :], in0=ffn_ps[(e // 2) % 2][:, (e % 2) * D:(e % 2 + 1) * D],
                                             scalar=pick[:, e:e + 1], in1=acc[:, :], op0=ALU.mult,
                                             op1=ALU.add).then_inc(acc_step, 1)
                if sharing and i in (8, 13):
                    low_share(j + 1, 2 * q + i // 13)

            def halves(a):
                return a.rearrange("p (k n) -> p k n", k=KD)

            def body(j, q, routing, sharing):
                for i in range(SUB):
                    T, p, nxt = TB * j + SUB * q + i, i % 2, (i + 1) % 4
                    dve.wait_ge(hist_done, T + 1)
                    for bank, n, pre, full, added in ((f_ps, 2, pre_f, f_full, f_added),
                                                      (gi_ps, 4, pre_gi, gi_full, gi_added),
                                                      (o_ps, 2, pre_o, o_full, o_added)):
                        dve.wait_ge(full, T + 1)
                        dve.tensor_reduce(pre.rearrange("p (g b) -> p g b", b=B), bank[:, 0:n * 2 * B].rearrange("p (g s b) -> p g b s", g=n, s=2),
                                          AX.X, ALU.add).then_inc(added, 1)
                    dve.wait_ge(f_done, T + 2)
                    dve.tensor_tensor(fc[:, p, :], f[:, p, :], cell[:, 1 - p, :], ALU.mult)
                    dve.wait_ge(gi_done, T + 2)
                    dve.scalar_tensor_tensor(out=ig[:, p, :], in0=gi[:, p, 0:2 * B], scalar=-0.5,
                                             in1=gi[:, p, 2 * B:4 * B], op0=ALU.add, op1=ALU.mult).then_inc(ig_done, 1)
                    dve.wait_ge(ig_done, T + 1)
                    dve.tensor_tensor(cell[:, p, :], ig[:, p, :], fc[:, p, :], ALU.add).then_inc(cell_done, 1)
                    dve.wait_ge(tanh_done, T + 1)
                    dve.tensor_tensor(hs[:, nxt, :, 0:B], halves(o[:, p, :]), halves(tc[:, p, :]),
                                      ALU.mult).then_inc(hi_ready, 1)
                    dve.tensor_tensor(h[:, p, :], o[:, p, :], tc[:, p, :], ALU.mult).then_inc(h_ready, 1)
                    dve.wait_ge(h_ready, T + 1)
                    dve.tensor_tensor(hs[:, nxt, :, B:2 * B], halves(h[:, p, :]), hs[:, nxt, :, 0:B],
                                      ALU.subtract).then_inc(lo_ready, 1)
                    side(j, q, i, routing, sharing)

            low_gates(0, two(wxh), two(wxl))
            then(dve.memset(ones2[:, :], 1.0))
            then(dve.memset(factor[:, :], UP))
            then(dve.memset(cell[:, 1, :], 0.0))
            then(dve.tensor_copy(ident16[:, :], ident[:, :]))
            with dve.Fori(0, GC) as c:
                low_share(0, c)
            low_gates(1, whh, whl)
            then(dve.tensor_scalar(rraw[:, :, :], rraw[:, :, :], UP, None, ALU.mult))
            then(dve.tensor_copy(wrh[:, :, :], rraw[:, :, :]))
            then(dve.tensor_tensor(wrl[:, :, :], rraw[:, :, :], wrh[:, :, :], ALU.subtract))
            assert count_made[0] == MADE
            dve.tensor_copy(hs[:, 0, :, 0:B], h0[:, :, :]).then_inc(hi_ready, 1)
            dve.wait_ge(hi_ready, 1)
            dve.tensor_tensor(hs[:, 0, :, B:2 * B], h0[:, :, :], hs[:, 0, :, 0:B], ALU.subtract).then_inc(lo_ready, 1)
            blocks(dve, body, start=lambda j: low_x1(j + 1))
            after(dve, side)


def embedded_block_kernel(nc, xT, condT, gate_w, gate_b, time_w, time_b, steps, w1, w2, mix_biases, wqkvo, wrel,
                          positions, qbias, b_out, identity, wx, wh, gate_bias, router_w, router_b, expert_w,
                          expert_b, row_mask, count8, out):
    context = nc.dram_tensor("context", [B, P, 2, KD, L], F32, kind="Internal").ap()
    skew = nc.dram_tensor("skew", [HEADS * P * WIN], F32, kind="Internal").ap()
    with ExitStack() as ctx:
        s = Scope(nc, ctx)
        x1 = s.sb("x1", [P, KD, B, L])
        ahead = RecurrenceAhead(s, condT, wx, wh, gate_bias, router_w, router_b, row_mask, count8, identity)
        with ExitStack() as attention_ctx:
            inputs = AttentionAhead(Scope(nc, attention_ctx), x1, xT, wqkvo, wrel, positions, qbias, b_out, identity)
            with ExitStack() as mixture_ctx:
                m = Scope(nc, mixture_ctx)
                table_i = m.sb("table_i", [P, B * SLOTS], I32)
                table_w = m.sb("table_w", [P, B * SLOTS * len(RANGES)])
                gating(nc, xT, condT, gate_w, gate_b, time_w, time_b, steps, table_i, table_w)
                mixture(nc, xT, w1, w2, mix_biases, table_i, table_w, context, inputs)
            attention(nc, wqkvo, wrel, qbias, context, skew, inputs, ahead.loads)
        recurrence(nc, ahead, expert_w, expert_b, x1, out)


def _lgamma(x):
    import math
    import numpy as np
    f = np.float32
    total = f(0.99999999999980993227684700473478)
    z = x - f(1)
    for i, c in enumerate((676.520368121885098567009190444019, -1259.13921672240287047156078755283,
                           771.3234287776530788486528258894, -176.61502916214059906584551354,
                           12.507343278686904814458936853, -0.13857109526572011689554707,
                           9.984369578019570859563e-6, 1.50563273514931155834e-7)):
        total = total + f(c) / (z + f(i + 1))
    t, log_t = f(7.5) + z, f(math.log(7.5)) + np.log1p(z / f(7.5))
    return f(0.5 * math.log(2 * math.pi)) + (z + f(0.5) - t / log_t) * log_t + np.log(total)


def _positional_features(seq, features):
    import math
    import numpy as np
    f = np.float32
    n = features // 6

    def linspace(a, z):
        i = np.arange(n - 1, dtype=f) / f(n - 1)
        return np.concatenate([f(a) * (f(1) - i) + f(z) * i, [f(z)]]).astype(f)[None]

    distance = np.arange(-seq + 1, seq).astype(f)
    absd = np.abs(distance)[:, None]
    half_life = f(2) ** linspace(3.0, math.log(seq) / math.log(2.0))
    decay = np.exp(-f(math.log(2.0)) / half_life * absd)
    center = (f(2) ** np.arange(1, n + 1).astype(f) - f(1) > absd).astype(f)
    deviation = seq / (2.0 * n)
    mean = linspace(seq / n, float(seq))
    conc, rate = (mean / f(deviation)) ** 2, mean / f(deviation ** 2)
    log_d = np.log(np.maximum(absd, f(1e-30)))
    density = np.exp((conc - f(1)) * log_d - rate * absd - (_lgamma(conc) - conc * np.log(rate))) + f(1e-8)
    emb = np.concatenate([decay, center, density / density.max(-1, keepdims=True)], -1)
    return np.concatenate([emb, np.sign(distance)[:, None] * emb], -1)


def _gate_order(a):
    import numpy as np
    i, f, o, g = (a[..., n * D:(n + 1) * D] for n in range(4))
    return np.concatenate([f, g, i, o], -1)


def _layout(t):
    import numpy as np
    c = {}
    c["xT"] = t["x"].transpose(2, 0, 1)
    c["condT"] = t["cond_1024"].T
    c["gate_w"], c["gate_b"] = t["L0_cond_gate_w"], t["L0_cond_gate_b"]
    c["time_w"], c["time_b"] = t["L0_cond_time_w"], t["L0_cond_time_b"]
    c["steps"] = np.concatenate([np.tile(np.arange(EXPERTS, dtype=np.float32), (B, 1)),
                                 np.eye(B, dtype=np.float32)], 1)
    c["w1"] = np.concatenate([t["L0_cond_ew1"], t["L0_cond_sw1"][None]])
    c["w2"] = np.concatenate([t["L0_cond_ew2"], t["L0_cond_sw2"][None]])
    b1 = np.concatenate([t["L0_cond_eb1"], t["L0_cond_sb1"][None]]).reshape(EXPERTS + 1, KH, P)
    b2 = np.concatenate([t["L0_cond_eb2"], t["L0_cond_sb2"][None]]).reshape(EXPERTS + 1, KD, P)
    c["mix_biases"] = np.concatenate([b1, b2], 1).transpose(0, 2, 1)
    pair = [t[w].reshape(KD, P, PAIRS, 2 * DK).transpose(2, 1, 0, 3).reshape(PAIRS, P, L)
            for w in ("L0_attn_w_qs", "L0_attn_w_ks", "L0_attn_w_vs")]
    pair.append(t["L0_attn_w_out"].reshape(PAIRS, 2, P, D).transpose(0, 2, 1, 3).reshape(PAIRS, P, L))
    c["wqkvo"] = np.stack(pair, 2)
    c["wrel"] = t["L0_attn_w_rel_pos_k"].reshape(2, FP, PAIRS, 2 * DK).transpose(2, 1, 0, 3)
    positions = np.zeros((FEATS, DIST), np.float32)
    positions[:, 0:DIST - 1] = _positional_features(L, FEATS).T
    c["positions"] = positions.reshape(2, FP, 2, L).transpose(1, 0, 2, 3).reshape(FP, 4, L)
    biases = [t[n].reshape(PAIRS, 2, DK) for n in ("L0_attn_rel_embed_bias", "L0_attn_rel_pos_bias")]
    c["qbias"] = np.stack(biases, 1).reshape(PAIRS, 4, DK).transpose(0, 2, 1)
    c["b_out"] = t["L0_attn_b_out"].reshape(KD, P).T
    c["identity"] = np.eye(P, dtype=np.float32)
    c["wx"], c["wh"] = _gate_order(t["L0_cond2_Wx"]), _gate_order(t["L0_cond2_Wh"])
    c["gate_bias"] = _gate_order(t["L0_cond2_b"]).reshape(GC, P).T
    c["router_w"] = t["L0_ffn_router_w"]
    c["router_b"] = np.tile(t["L0_ffn_router_b"][None], (P, 1))
    c["expert_w"] = t["L0_ffn_expert_w"].transpose(1, 0, 2).reshape(D, FFN_EXPERTS * D)
    c["expert_b"] = np.tile(t["L0_ffn_expert_b"].reshape(1, FFN_EXPERTS * D), (2, 1))
    c["row_mask"] = np.eye(2, dtype=np.float32)
    c["count8"] = np.tile(np.arange(FFN_EXPERTS, dtype=np.float32), (P, 1))
    return c


def kernel(**inputs):
    import numpy as np
    import concourse.bacc as bacc
    from concourse.bass_utils import run_bass_kernel_spmd

    nc = bacc.Bacc("TRN2", target_bir_lowering=False, num_devices=1)
    arrays, args = {}, []
    for name, a in _layout({k: np.asarray(v) for k, v in inputs.items()}).items():
        arrays[f"in_{name}_dram"] = np.ascontiguousarray(a)
        args.append(nc.dram_tensor(f"in_{name}_dram", a.shape, F32, kind="ExternalInput").ap())
    args.append(nc.dram_tensor("out_0_dram", (B, L, D), F32, kind="ExternalOutput").ap())
    embedded_block_kernel(nc, *args)
    r = run_bass_kernel_spmd(nc, [arrays], core_ids=[0])
    return r.results[0]["out_0_dram"]
```

```python
from contextlib import ExitStack

import concourse.bass as bass
from concourse import mybir

F32 = mybir.dt.float32
F32R = mybir.dt.float32r
F16 = mybir.dt.float16
I32 = mybir.dt.int32
ALU = mybir.AluOpType
ACT = mybir.ActivationFunctionType
AX = mybir.AxisListType

P = 128
B, L, D = 8, 512, 256
KD = D // P
EXPERTS, TOP_K, HID = 4, 2, 1024
SHARED = EXPERTS
SLOTS = TOP_K + 1
KH = HID // P
THIRD = L // 3
RANGES = [(0, THIRD), (THIRD, 2 * THIRD), (2 * THIRD, L)]


class Scope:

    def __init__(self, nc, ctx):
        self.nc, self.ctx = nc, ctx

    def sb(self, name, shape, dt=F32):
        return self.ctx.enter_context(self.nc.sbuf_tensor(name, shape, dt))

    def ps(self, name):
        return self.ctx.enter_context(self.nc.psum_tensor(name, [P, 512], F32))

    def sem(self, name):
        return self.ctx.enter_context(self.nc.semaphore(name))


def gating(s, xT, condT, gate_w, gate_b, time_w, time_b, steps, table_i, table_w, x_all):
    gw = s.sb("gw", [P, 3 * KD, EXPERTS])
    tw = s.sb("tw", [P, KD, 2 * EXPERTS])
    gb = s.sb("gb", [1, EXPERTS])
    tb = s.sb("tb", [1, 2 * EXPERTS])
    stp = s.sb("stp", [B, EXPERTS + B])
    cond = s.sb("cond", [P, KD, B])
    csig = s.sb("csig", [P, KD, B])
    csilu = s.sb("csilu", [P, KD, B])
    sums = s.sb("sums", [P, 3, KD, B])
    agg = s.sb("agg", [P, 3, KD, B])
    tmp = s.sb("tmp", [P, KD, B])
    ones = s.sb("ones", [8, P])
    g = s.sb("g", [B, 24, EXPERTS])
    one = s.sb("one", [B, 16])
    vals = s.sb("vals", [B, SLOTS * 4])
    spread = s.sb("spread", [B, B, SLOTS * 4])
    gate_ps, table_ps = s.ps("gate_ps"), s.ps("table_ps")
    mod_ps, logit_ps = gate_ps[:, 0:2 * EXPERTS], gate_ps[:, 64:64 + EXPERTS]
    PARTS = 4
    small_in, x_in = s.sem("small_in"), [s.sem(f"x_in{i}") for i in range(PARTS)]
    table_ready = s.sem("table_ready")
    sig_done, vec, aggs_done, logits_done, spread_done, table_done, exp_done = (
        s.sem(n) for n in ("sig_done", "vec", "aggs_done", "logits_done", "spread_done", "table_done", "exp_done"))
    def sync(sp):
        sp.dma_start(cond[:, :, :], condT.rearrange("(k p) b -> p k b", p=P)).then_inc(small_in, 16)
        sp.dma_start(gw[:, :, :], gate_w.rearrange("(k p) e -> p k e", p=P)).then_inc(small_in, 16)
        sp.dma_start(tw[:, :, :], time_w.rearrange("(k p) e -> p k e", p=P)).then_inc(small_in, 16)
        sp.dma_start(gb[:, :], gate_b.rearrange("(a e) -> a e", a=1)).then_inc(small_in, 16)
        sp.dma_start(tb[:, :], time_b.rearrange("(a e) -> a e", a=1)).then_inc(small_in, 16)
        sp.dma_start(stp[:, :], steps).then_inc(small_in, 16)

    def scalar_first(act):
        for i in range(PARTS):
            rows = slice(i * B // PARTS, (i + 1) * B // PARTS)
            act.dma_start(x_all[:, :, rows, :], xT.rearrange("(k p) b l -> p k b l", p=P)[:, :, rows, :]
                          ).then_inc(x_in[i], 16)

    def scalar_sigmoid(act):
        act.wait_ge(small_in, 96)
        act.activation(csig[:, :, :], cond[:, :, :], ACT.Sigmoid).then_inc(sig_done, 1)

    def scalar_exp(act):
        act.wait_ge(vec, 14 + 3 * PARTS)
        act.activation(g[:, 5, :], g[:, 4, :], ACT.Exp, bias=one[:, 0:1],
                       accum_out=one[:, 1:2]).then_inc(exp_done, 1)

    def tensor(pe):
        pe.wait_ge(small_in, 96)
        pe.wait_ge(vec, 2 + 3 * PARTS)
        for k in range(KD):
            pe.matmul(mod_ps[0:B, 0:2 * EXPERTS], csilu[:, k, :], tw[:, k, :], start=(k == 0), stop=False)
        pe.matmul(mod_ps[0:B, 0:2 * EXPERTS], ones[0:1, 0:B], tb[:, :], start=False, stop=True)
        pe.wait_ge(aggs_done, 1)
        for j in range(3 * KD):
            pe.matmul(logit_ps[0:B, 0:EXPERTS], agg[:, j // KD, j % KD, :], gw[:, j, :],
                      start=(j == 0), stop=False)
        pe.matmul(logit_ps[0:B, 0:EXPERTS], ones[0:1, 0:B], gb[:, :], start=False,
                  stop=True).then_inc(logits_done, 1)
        pe.wait_ge(spread_done, 1)
        pe.matmul(table_ps[:, 0:B * SLOTS * 4], ones[0:B, :], spread[:, :, :].rearrange("p b n -> p (b n)"),
                  start=True, stop=True).then_inc(table_done, 1)

    done = [0]

    def then(dve, ins):
        done[0] += 1
        ins.then_inc(vec, 1)
        dve.wait_ge(vec, done[0])

    def vector_sums(dve, i):
        rows = slice(i * B // PARTS, (i + 1) * B // PARTS)
        dve.wait_ge(x_in[i], 16)
        for r, (a, z) in enumerate(RANGES):
            then(dve, dve.tensor_reduce(sums[:, r, :, rows], x_all[:, :, rows, a:z], AX.X, ALU.add))

    def vector(dve):
        then(dve, dve.memset(ones[:, :], 1.0))
        dve.wait_ge(sig_done, 1)
        then(dve, dve.tensor_tensor(csilu[:, :, :], cond[:, :, :], csig[:, :, :], ALU.mult))
        n_pair = L - THIRD
        then(dve, dve.tensor_tensor(tmp[:, :, :], sums[:, 0, :, :], sums[:, 2, :, :], ALU.add))
        then(dve, dve.tensor_scalar(agg[:, 1, :, :], tmp[:, :, :], 1.0 / n_pair, None, ALU.mult))
        then(dve, dve.tensor_tensor(agg[:, 0, :, :], tmp[:, :, :], sums[:, 1, :, :], ALU.add))
        then(dve, dve.tensor_scalar(agg[:, 0, :, :], agg[:, 0, :, :], 1.0 / L, None, ALU.mult))
        then(dve, dve.tensor_tensor(tmp[:, :, :], sums[:, 1, :, :], sums[:, 2, :, :], ALU.add))
        dve.tensor_scalar(agg[:, 2, :, :], tmp[:, :, :], 1.0 / n_pair, None, ALU.mult).then_inc(aggs_done, 1)
        dve.wait_ge(logits_done, 1)
        then(dve, dve.tensor_scalar(g[:, 0, :], mod_ps[0:B, 0:EXPERTS], 1.0, None, ALU.add))
        then(dve, dve.tensor_copy(g[:, 1, :], mod_ps[0:B, EXPERTS:2 * EXPERTS]))
        then(dve, dve.tensor_tensor(g[:, 2, :], logit_ps[0:B, 0:EXPERTS], g[:, 0, :], ALU.mult))
        then(dve, dve.tensor_tensor(g[:, 4, :], g[:, 2, :], g[:, 1, :], ALU.add))
        then(dve, dve.tensor_reduce(one[:, 2:3], g[:, 4, :], AX.X, ALU.max))
        then(dve, dve.tensor_scalar(one[:, 0:1], one[:, 2:3], -1.0, None, ALU.mult))
        then(dve, dve.memset(vals[:, :], 1.0))
        assert done[0] == 14 + 3 * PARTS
        dve.wait_ge(exp_done, 1)
        then(dve, dve.reciprocal(one[:, 3:4], one[:, 1:2]))
        then(dve, dve.tensor_scalar(g[:, 6, :], g[:, 5, :], one[:, 3:4], None, ALU.mult))
        for j in range(TOP_K):
            score = g[:, 6 + j, :]
            top, eq, cand, hot = one[:, 4 + j:5 + j], g[:, 8 + 3 * j, :], g[:, 9 + 3 * j, :], g[:, 10 + 3 * j, :]
            then(dve, dve.tensor_reduce(top, score, AX.X, ALU.max))
            then(dve, dve.tensor_scalar(eq, score, top, None, ALU.is_lt))
            then(dve, dve.scalar_tensor_tensor(out=cand, in0=eq, scalar=8.0, in1=stp[:, 0:EXPERTS],
                                          op0=ALU.mult, op1=ALU.add))
            number = vals[:, 4 * (j + 1) + 3:4 * (j + 1) + 4]
            then(dve, dve.tensor_reduce(number, cand, AX.X, ALU.min))
            then(dve, dve.tensor_scalar(hot, stp[:, 0:EXPERTS], number, None, ALU.is_equal))
            then(dve, dve.scalar_tensor_tensor(out=g[:, 7 + j, :], in0=hot, scalar=-2.0, in1=score,
                                          op0=ALU.mult, op1=ALU.add) if j == 0 else
                 dve.tensor_tensor(one[:, 6:7], one[:, 4:5], one[:, 5:6], ALU.add))
        then(dve, dve.tensor_scalar(one[:, 7:8], one[:, 6:7], 1e-8, None, ALU.add))
        then(dve, dve.reciprocal(one[:, 8:9], one[:, 7:8]))
        for j in range(TOP_K):
            hot, w = g[:, 10 + 3 * j, :], one[:, 9 + j:10 + j]
            then(dve, dve.tensor_tensor(w, one[:, 4 + j:5 + j], one[:, 8:9], ALU.mult))
            then(dve, dve.tensor_scalar(g[:, 16 + j, :], hot, -1.0, 1.0, ALU.mult, ALU.add))
            v = 4 * (j + 1)
            then(dve, dve.tensor_tensor(vals[:, v:v + 1], g[:, 16 + j, 2:3], w, ALU.mult))
            then(dve, dve.tensor_tensor(vals[:, v + 1:v + 2], g[:, 16 + j, 1:2], w, ALU.mult))
            then(dve, dve.tensor_copy(vals[:, v + 2:v + 3], w))
        for b in range(B):
            then(dve, dve.tensor_scalar(spread[:, b, :], vals[:, :], stp[:, EXPERTS + b:EXPERTS + b + 1], None,
                                   ALU.mult))
        dve.nop().then_inc(spread_done, 1)
        dve.wait_ge(table_done, 1)
        t = table_ps[:, 0:B * SLOTS * 4].rearrange("p (n c) -> p n c", c=4)
        then(dve, dve.tensor_copy(table_w[:, :].rearrange("p (n c) -> p n c", c=3), t[:, :, 0:3]))
        then(dve, dve.tensor_copy(table_i[0:1, :], t[0:1, :, 3]))
        dve.nop().then_inc(table_ready, 1)

    return sync, scalar_first, scalar_sigmoid, scalar_exp, tensor, vector_sums, vector, aggs_done, table_ready


def mixture(nc, xT, w1, w2, biases, gating_inputs, context, ahead):
    GELUS = 4
    with ExitStack() as ctx:
        s = Scope(nc, ctx)
        table_i, table_w = s.sb("table_i", [P, B * SLOTS], I32), s.sb("table_w", [P, B * SLOTS * len(RANGES)])
        raw1, raw2 = s.sb("raw1", [P, KD, HID]), s.sb("raw2", [P, KH, D])
        bias = s.sb("bias", [P, SLOTS, KH + KD])
        x_raw = s.sb("x_raw", [P, KD, L])
        w1h, w1l = s.sb("w1h", [P, KD, HID], F32R), s.sb("w1l", [P, KD, HID], F32R)
        w2h, w2l = s.sb("w2h", [P, KH, D], F32R), s.sb("w2l", [P, KH, D], F32R)
        weight = s.sb("weight", [P, 3 * SLOTS])
        x_hi, x_lo = s.sb("x_hi", [P, KD, L], F32R), s.sb("x_lo", [P, KD, L], F32R)
        g = s.sb("gelu", [P, GELUS, L])
        h_hi, h_lo = s.sb("h_hi", [P, KH, L], F32R), s.sb("h_lo", [P, KH, L], F32R)
        y, acc = s.sb("y", [P, KD, L]), s.sb("acc", [P, KD, L])
        split = s.sb("split", [P, 2, KD, L], F32R)
        h_ps = [s.ps(f"h_ps{i}") for i in range(GELUS)]
        y_ps = [s.ps(f"y_ps{i}") for i in range(KD)]
        raw1_in, raw2_in, x_in = s.sem("raw1_in"), s.sem("raw2_in"), s.sem("mix_x_in")
        bias_in = [s.sem(f"bias_in{i}") for i in range(SLOTS)]
        w1_hi_done, w1_done, w2_hi_done, w2_done = (
            s.sem(n) for n in ("w1_hi_done", "w1_done", "w2_hi_done", "w2_done"))
        x_hi_done, x_done = s.sem("x_hi_done"), s.sem("x_done")
        h_full, gelu_done, hi_done, lo_done = (s.sem(n) for n in ("h_full", "gelu_done", "hi_done", "lo_done"))
        y_full, y_out, y_used, acc_done = (s.sem(n) for n in ("y_full", "y_out", "y_used", "acc_done"))
        split_hi_done, split_done, context_out, context_free = (
            s.sem(n) for n in ("split_hi_done", "split_done", "context_out", "context_free"))
        ahead_in, bias_added = s.sem("ahead_in"), s.sem("bias_added")
        (gating_sync, gating_first, gating_sigmoid, gating_exp, gating_tensor, gating_sums, gating_vector,
         sums_used, table_ready) = gating(s, xT, *gating_inputs, table_i, table_w, ahead.x1)
        block = ctx.enter_context(nc.Block())

        @block.sync
        def _(sp):
            def batch(b, begins=False):
                sp.wait_ge(x_done, b + 1)
                sp.dma_start(x_raw[:, :, :],
                             xT[:, bass.ds(b, 1), :].rearrange("(k p) b l -> p k (b l)", p=P)).then_inc(x_in, 16)
                for slot in range(SLOTS):
                    k = SLOTS * b + slot
                    e = SHARED
                    if begins and slot == 1:
                        gating_sync(sp)
                        sp.wait_ge(table_ready, 1)
                    if slot:
                        e = sp.value_load(table_i[0:1, bass.ds(k, 1)], min_val=0, max_val=SHARED)
                    sp.wait_ge(w1_done, k + 1)
                    sp.dma_start(raw1[:, :, :], w1[bass.ds(e, 1)].rearrange("e (k p) n -> p (e k) n", p=P)
                                 ).then_inc(raw1_in, 16)
                    sp.dma_start(bias[:, slot, :], biases[bass.ds(e, 1)].rearrange("e p n -> p (e n)")
                                 ).then_inc(bias_in[slot], 16)
                    sp.wait_ge(w2_done, k + 1)
                    sp.dma_start(raw2[:, :, :], w2[bass.ds(e, 1)].rearrange("e (k p) n -> p (e k) n", p=P)
                                 ).then_inc(raw2_in, 16)

            batch(0, begins=True)
            with sp.Fori(1, B) as b:
                batch(b)
            sp.wait_ge(context_out, 16 * B)
            sp.wait_ge(ahead_in, 16 * len(ahead.loads))
            sp.wait_ge(bias_added, KD)

        @block.tensor
        def _(pe):
            def batch(b, begins=False):
                for slot in range(SLOTS):
                    k = SLOTS * b + slot
                    pe.wait_ge(w1_done, k + 2)
                    if slot == 0:
                        pe.wait_ge(x_done, b + 2)
                    for oc in range(KH):
                        pe.wait_ge(gelu_done, KH * k + oc + 1)
                        for n, (w, x) in enumerate(((w1h, x_hi), (w1h, x_lo), (w1l, x_hi))):
                            for c in range(KD):
                                mm = pe.matmul(h_ps[oc % GELUS][:, :], w[:, c, oc * P:(oc + 1) * P], x[:, c, :],
                                               start=(n == 0 and c == 0), stop=(n == 2 and c == KD - 1))
                        mm.then_inc(h_full, 1)
                    pe.wait_ge(w2_done, k + 2)
                    pe.wait_ge(y_out, KD * k + KD)
                    for c in range(KH):
                        pe.wait_ge(lo_done, KH * k + c + 1 + GELUS)
                        for oc in range(KD):
                            for n, (w, h) in enumerate(((w2h, h_hi), (w2h, h_lo), (w2l, h_hi))):
                                mm = pe.matmul(y_ps[oc][:, :], w[:, c, oc * P:(oc + 1) * P], h[:, c, :],
                                               start=(c == 0 and n == 0), stop=(c == KH - 1 and n == 2))
                            if c == KH - 1:
                                mm.then_inc(y_full, 1)
                    if begins and slot == 0:
                        gating_tensor(pe)

            batch(0, begins=True)
            with pe.Fori(1, B) as b:
                batch(b)

        @block.scalar
        def _(act):
            act.nop().then_inc(gelu_done, GELUS)
            act.nop().then_inc(y_out, KD)
            act.wait_ge(raw1_in, 16)
            gating_first(act)
            act.wait_ge(h_full, 1)
            for dst, src in ahead.loads:
                act.dma_start(dst, src).then_inc(ahead_in, 16)

            def batch(b, begins=False):
                for slot in range(SLOTS):
                    k = SLOTS * b + slot
                    act.wait_ge(bias_in[slot], 16 * b + 16)
                    for oc in range(KH):
                        n = KH * k + oc
                        act.wait_ge(h_full, n + 1)
                        act.wait_ge(lo_done, n + 1)
                        act.activation(g[:, oc % GELUS, :], h_ps[oc % GELUS][:, :], ACT.Gelu_apprx_tanh,
                                       bias=bias[:, slot, oc:oc + 1]).then_inc(gelu_done, 1)
                        act.wait_ge(gelu_done, n + 1 + GELUS)
                        act.copy(h_hi[:, oc, :], g[:, oc % GELUS, :]).then_inc(hi_done, 1)
                    if begins and slot == 0:
                        gating_sigmoid(act)
                    act.wait_ge(y_used, k + 1)
                    for oc in range(KD):
                        act.wait_ge(y_full, KD * k + oc + 1)
                        act.activation(y[:, oc, :], y_ps[oc][:, :], ACT.Identity,
                                       bias=bias[:, slot, KH + oc:KH + oc + 1]).then_inc(y_out, 1)
                    if begins and slot == 0:
                        gating_exp(act)

            batch(0, begins=True)
            with act.Fori(1, B) as b:
                batch(b)

        @block.gpsimd
        def _(pool):
            pool.nop().then_inc(context_free, 1)
            pool.wait_ge(ahead_in, 16 * len(ahead.loads))
            pool.wait_ge(sums_used, 1)
            for k in range(KD):
                pool.tensor_scalar(ahead.x1[:, k, :, :], ahead.x1[:, k, :, :], ahead.bo[:, k:k + 1], None, ALU.add
                                   ).then_inc(bias_added, 1)
            with pool.Fori(0, B) as b:
                pool.wait_ge(split_done, b + 1)
                pool.dma_start(context[bass.ds(b, 1)].rearrange("b p s k l -> p (b s k l)"),
                               split[:, :, :, :].rearrange("p s k l -> p (s k l)").bitcast(F32)
                               ).then_inc(context_out, 16)
                pool.wait_ge(context_out, 16 * b + 16)
                pool.nop().then_inc(context_free, 1)

        @block.vector
        def _(dve):
            dve.nop().then_inc(lo_done, GELUS)
            for free in (y_used, w1_done, w2_done, x_done):
                dve.nop().then_inc(free, 1)

            def split_x(b):
                dve.wait_ge(x_in, 16 * b + 16)
                dve.tensor_copy(x_hi[:, :, :], x_raw[:, :, :]).then_inc(x_hi_done, 1)
                dve.wait_ge(x_hi_done, b + 1)
                dve.tensor_tensor(x_lo[:, :, :], x_raw[:, :, :], x_hi[:, :, :].bitcast(F32),
                                  ALU.subtract).then_inc(x_done, 1)

            def split_w(k, raw, hi, lo, came, hi_split, done):
                dve.wait_ge(came, 16 * k + 16)
                dve.tensor_copy(hi[:, :, :], raw[:, :, :]).then_inc(hi_split, 1)
                dve.wait_ge(hi_split, k + 1)
                dve.tensor_tensor(lo[:, :, :], raw[:, :, :], hi[:, :, :].bitcast(F32),
                                  ALU.subtract).then_inc(done, 1)

            def batch(b, begins=False, last=False):
                for slot in range(SLOTS):
                    k = SLOTS * b + slot
                    split_w(k, raw2, w2h, w2l, raw2_in, w2_hi_done, w2_done)
                    for oc in range(KH):
                        dve.wait_ge(hi_done, KH * k + oc + 1)
                        dve.tensor_tensor(h_lo[:, oc, :], g[:, oc % GELUS, :], h_hi[:, oc, :].bitcast(F32),
                                          ALU.subtract).then_inc(lo_done, 1)
                        if begins and slot == 0 and oc % 2:
                            gating_sums(dve, oc // 2)
                    if begins and slot == 0:
                        gating_vector(dve)
                    if slot == 0:
                        dve.tensor_copy(weight[:, :], table_w[:, bass.ds(9 * b, 9)]).then_inc(acc_done, 1)
                    if not last or slot < SLOTS - 1:
                        if slot == SLOTS - 1:
                            split_x(b + 1)
                        split_w(k + 1, raw1, w1h, w1l, raw1_in, w1_hi_done, w1_done)
                    dve.wait_ge(y_out, KD * k + 2 * KD)
                    dve.wait_ge(y_used, k + 1)
                    if slot == 0:
                        dve.tensor_copy(acc[:, :, :], y[:, :, :]).then_inc(y_used, 1)
                        continue
                    dve.wait_ge(acc_done, 6 * b + 1 + 2 * (slot - 1))
                    for r, (a, z) in enumerate(RANGES):
                        w = weight[:, 3 * slot + r:3 * slot + r + 1]
                        dve.scalar_tensor_tensor(out=acc[:, :, a:z], in0=y[:, :, a:z], scalar=w, in1=acc[:, :, a:z],
                                                 op0=ALU.mult, op1=ALU.add).then_inc(y_used if r == 2 else acc_done, 1)
                    if slot < SLOTS - 1:
                        continue
                    dve.wait_ge(acc_done, 6 * b + 5)
                    dve.wait_ge(y_used, k + 2)
                    dve.wait_ge(context_free, b + 1)
                    dve.tensor_copy(split[:, 0, :, :], acc[:, :, :]).then_inc(split_hi_done, 1)
                    dve.wait_ge(split_hi_done, b + 1)
                    dve.tensor_tensor(split[:, 1, :, :], acc[:, :, :], split[:, 0, :, :].bitcast(F32),
                                      ALU.subtract).then_inc(split_done, 1)
                    dve.wait_ge(split_done, b + 1)
                    dve.nop().then_inc(acc_done, 1)

            split_x(0)
            split_w(0, raw1, w1h, w1l, raw1_in, w1_hi_done, w1_done)
            batch(0, begins=True)
            with dve.Fori(1, B - 1) as b:
                batch(b)
            batch(B - 1, last=True)


HEADS, DK = 8, 128
PAIRS = HEADS // 2
QT = L // P
KT = L // P
FEATS = 192
FP = FEATS // 2
DIST = 2 * L
WIN = L + P
HALF_WIN = WIN // 2
SCALE = float(DK) ** -0.5

REL = ["rel0", "rel1", "rel2", "rel3"]
EVEN = ["q0", "k0", "out0", "out1", "s0.0", "s0.1", "s0.2", "s0.3", "val0", "t0.0", "t0.1", "t0.2", "t0.3"]
ODD = ["q1", "k1", "val1", "s1.0", "s1.1", "s1.2", "s1.3", "v0", "v1", "t1.0", "t1.1", "t1.2", "t1.3"]
RING = [4, 5, 3, 2, 1, 0, 4, 5, 2, 3, 1, 0, 4, 2, 5, 1, 3, 0, 4, 2, 1, 5, 3, 0, 2, 1]
BANK = dict(zip(EVEN + ODD, RING), rel0=4, rel1=5, rel2=3, rel3=0, last0=4, last1=5)


class Step:

    def __init__(self, hp, bb, odd, leave_out=(), before=None):
        self.pair_start = isinstance(bb, int)
        rel = REL if self.pair_start and odd == 0 else []
        names = rel + EVEN + ODD
        self.items = [n for n in names if n not in leave_out]
        self.hp, self.bb, self.odd = hp, bb, odd
        self.g, self.m = B * hp + 2 * bb + odd, B // 2 * hp + bb
        self.b = 2 * bb + odd
        self.before = before if before is not None else EVEN + ODD

    def number(self, base, name):
        return base + self.items.index(name)


def takes_high(name):
    return name[0] != "s" and not name.startswith(("out", "last"))


class AttentionAhead:

    def __init__(self, s, x1, wqkvo, wrel, positions, qbias, b_out, identity):
        self.x1 = x1
        self.raw_w, self.raw_rel = s.sb("raw_w", [P, 4, L]), s.sb("raw_rel", [FP, 2, 2 * DK])
        self.raw_qb = s.sb("raw_qb", [P, 4])
        self.pos = s.sb("pos", [FP, 4, L])
        self.bo = s.sb("bo", [P, KD])
        self.ident = s.sb("ident", [P, P])
        self.loads = ((self.bo[:, :], b_out), (self.ident[:, :], identity), (self.pos[:, :, :], positions),
                      *self.pair(wrel, qbias, wqkvo, 0))

    def pair(self, wrel, qbias, wqkvo, hp):
        return ((self.raw_rel[:, :, :], wrel[bass.ds(hp, 1)].rearrange("h p m n -> p (h m) n")),
                (self.raw_qb[:, :], qbias[bass.ds(hp, 1)].rearrange("h p n -> p (h n)")),
                (self.raw_w[:, :, :], wqkvo[bass.ds(hp, 1)].rearrange("h p m n -> p (h m) n")))


def attention(nc, wqkvo, wrel, qbias, context, skew, ahead, next_loads):
    with ExitStack() as ctx:
        s = Scope(nc, ctx)
        part = s.sb("part", [P, 2, 2, KD, L], F32R)
        x1, raw_w, raw_rel, raw_qb, pos, ident = (
            ahead.x1, ahead.raw_w, ahead.raw_rel, ahead.raw_qb, ahead.pos, ahead.ident)
        wh, wl = s.sb("wh", [P, 4, L], F32R), s.sb("wl", [P, 4, L], F32R)
        rel_h, rel_l = s.sb("rel_h", [P, 2, DIST], F32R), s.sb("rel_l", [P, 2, DIST], F32R)
        qb = s.sb("qb", [P, 4])
        prob = s.sb("prob", [P, 8, L])
        qe_h, qe_l = s.sb("qe_h", [P, 2, L], F32R), s.sb("qe_l", [P, 2, L], F32R)
        qp_h, qp_l = s.sb("qp_h", [P, L], F32R), s.sb("qp_l", [P, L], F32R)
        k_h, k_l = s.sb("k_h", [P, 2, L], F32R), s.sb("k_l", [P, 2, L], F32R)
        v_h, v_l = s.sb("v_h", [P, KT, 2 * DK], F32R), s.sb("v_l", [P, KT, 2 * DK], F32R)
        pt_h, pt_l = s.sb("pt_h", [P, KT, L], F32R), s.sb("pt_l", [P, KT, L], F32R)
        o_h, o_l = s.sb("o_h", [P, 2, L], F32R), s.sb("o_l", [P, 2, L], F32R)
        dist = s.sb("dist", [P, QT, WIN])
        nmax, total, rinv = s.sb("nmax", [P, 8]), s.sb("total", [P, 8]), s.sb("rinv", [P, 8])
        banks = [s.ps(f"bank{i}") for i in range(6)]
        dist_ps = [s.ps(f"dist_ps{i}") for i in range(2)]

        pair_in, next_in = s.sem("pair_in"), s.sem("next_in")
        w_hi_done, w_done, wo_hi_done, wo_done, bias_ready = (
            s.sem(n) for n in ("w_hi_done", "w_done", "wo_hi_done", "wo_done", "bias_ready"))
        part_in = [s.sem(f"part_in{i}") for i in range(2)]
        item_full, high_done, freed = s.sem("item_full"), s.sem("high_done"), s.sem("freed")
        dist_full, dist_left, dist_right = s.sem("dist_full"), s.sem("dist_left"), s.sem("dist_right")
        stored = [s.sem(f"stored{i}") for i in range(QT)]
        skewed = [s.sem(f"skewed{i}") for i in range(8)]
        scores_seen, exp_done, rinv_done, prob_done = (
            s.sem(n) for n in ("scores_seen", "exp_done", "rinv_done", "prob_done"))
        block = ctx.enter_context(nc.Block())

        start = [n for n in EVEN if n not in ("q0", "k0")] + ["val1"]
        step0 = Step(0, 0, 0, leave_out=start, before=[])
        step1 = Step(0, 0, 1, leave_out=("out0", "out1"), before=step0.items)
        after = Step(PAIRS, 0, 0)
        after.items = ["out0", "out1"] + EVEN[4:] + ["val1", "last0", "last1"]

        def bases(keep):
            size = [sum(map(keep, x.items)) for x in (step0, step1)]
            full, rel = sum(map(keep, EVEN + ODD)), sum(map(keep, REL))

            def base(step):
                if step is step0:
                    return 0
                if step is step1:
                    return size[0]
                rest = size[0] + size[1] + full * (step.g - 2) + rel * step.hp
                return rest - rel if step.items[0] in (REL[0], "out0") else rest
            return base

        item_base, high_base = bases(lambda n: True), bases(takes_high)

        def item(step, name):
            return item_base(step) + step.items.index(name)

        def high(step, name):
            return high_base(step) + [n for n in step.items if takes_high(n)].index(name)

        def user_before(step, name):
            i = step.items.index(name)
            order = step.before + step.items[:i]
            for back, other in enumerate(reversed(order)):
                if BANK[other] == BANK[name]:
                    return item(step, name) - 1 - back
            return None

        def steps(eng, step, finish):
            step(step0)
            step(step1)
            with eng.Fori(1, B // 2) as bb:
                step(Step(0, bb, 0))
                step(Step(0, bb, 1))
            with eng.Fori(1, PAIRS) as hp:
                step(Step(hp, 0, 0))
                step(Step(hp, 0, 1))
                with eng.Fori(1, B // 2) as bb:
                    step(Step(hp, bb, 0))
                    step(Step(hp, bb, 1))
            finish(after)

        @block.sync
        def _(sp):
            def load_pair(hp):
                for dst, src in ahead.pair(wrel, qbias, wqkvo, hp):
                    sp.dma_start(dst, src).then_inc(pair_in, 16)

            def load_part(b, odd):
                sp.dma_start(part[:, odd, :, :, :].rearrange("p s k l -> p (s k l)").bitcast(F32),
                             context[bass.ds(b, 1)].rearrange("b p s k l -> p (b s k l)")).then_inc(part_in[odd], 16)

            def skew_unit(at, h):
                n = 2 * at.g + h

                def load(q):
                    sp.wait_ge(stored[q], 16 * n + 16)
                    src = bass.AP(tensor=skew.tensor, offset=(4 * h + q) * P * WIN + P - 1,
                                  ap=[[WIN - 1, P], [1, L]])
                    sp.dma_start(prob[:, 4 * h + q, :], src).then_inc(skewed[4 * h + q], 16)

                for q in range(QT):
                    sp.wait_ge(dist_left, QT * n + q + 1)
                    sp.wait_ge(dist_right, QT * n + q + 1)
                    dst = bass.AP(tensor=skew.tensor, offset=(4 * h + q) * P * WIN, ap=[[WIN, P], [1, WIN]])
                    sp.dma_start(dst, dist[:, q, :]).then_inc(stored[q], 16)
                    if q:
                        load(q - 1)
                load(QT - 1)

            def step(at):
                skew_unit(at, 0)
                skew_unit(at, 1)
                sp.wait_ge(item_full, item(at, "v1") + 1)
                load_part((at.b + 2) % B, at.odd)
                if at.pair_start and at.odd == 1:
                    sp.wait_ge(wo_done, at.hp + 1)
                    load_pair((at.hp + 1) % PAIRS)

            load_part(0, 0)
            load_part(1, 1)
            sp.nop().then_inc(pair_in, 48)
            for dst, src in next_loads:
                sp.dma_start(dst, src).then_inc(next_in, 16)
            steps(sp, step, lambda at: None)
            for i in range(2):
                sp.wait_ge(part_in[i], 16 * (PAIRS * B // 2 + 1))
            sp.wait_ge(pair_in, 48 * (PAIRS + 1))
            sp.wait_ge(next_in, 16 * len(next_loads))

        @block.tensor
        def _(pe):
            def product(out, terms, start=True, stop=True):
                for i, (a, x) in enumerate(terms):
                    mm = pe.matmul(out, a, x, start=start and i == 0, stop=stop and i == len(terms) - 1)
                return mm

            def passes(ah, al, mh, ml):
                return ((ah, mh), (ah, ml), (al, mh))

            def take_bank(at, name):
                free = user_before(at, name)
                if free is not None:
                    pe.wait_ge(freed, free + 1)
                return banks[BANK[name]]

            def distance_keys(at):
                pe.wait_ge(pair_in, 48 * at.hp + 48)
                for h in range(2):
                    for half in range(2):
                        bank = take_bank(at, f"rel{2 * h + half}")
                        terms = [(raw_rel[:, k, h * DK:(h + 1) * DK], pos[:, 2 * k + half, :]) for k in range(2)]
                        product(bank[:, :], terms).then_inc(item_full, 1)

            def w(m, k, a, z):
                return wh[:, m, 2 * DK * k + a:2 * DK * k + z], wl[:, m, 2 * DK * k + a:2 * DK * k + z]

            def project_qk(at, h):
                if h == 0:
                    pe.wait_ge(part_in[at.odd], 16 * at.m + 16)
                for m, name in enumerate((f"q{h}", f"k{h}")):
                    bank = take_bank(at, name)
                    terms = []
                    for k in range(KD):
                        terms += passes(*w(m, k, h * DK, (h + 1) * DK), part[:, at.odd, 0, k, :],
                                        part[:, at.odd, 1, k, :])
                    product(bank[:, :], terms).then_inc(item_full, 1)

            def v_tile(at, t):
                bank = take_bank(at, f"v{t // 2}") if t % 2 == 0 else banks[BANK[f"v{t // 2}"]]
                rows = slice(t * P, (t + 1) * P)
                terms = []
                for k in range(KD):
                    wkh, wkl = w(2, k, 0, 2 * DK)
                    ch, cl = part[:, at.odd, 0, k, rows], part[:, at.odd, 1, k, rows]
                    terms += ((ch, wkh), (ch, wkl), (cl, wkh))
                mm = product(bank[:, (t % 2) * 2 * DK:(t % 2 + 1) * 2 * DK], terms)
                if t % 2:
                    mm.then_inc(item_full, 1)

            def values_part(at, h, k):
                name = f"val{h}"
                bank = take_bank(at, name) if k == 0 else banks[BANK[name]]
                cols = slice(h * DK, (h + 1) * DK)
                mm = product(bank[:, :], passes(v_h[:, k, cols], v_l[:, k, cols], pt_h[:, k, :], pt_l[:, k, :]),
                             start=(k == 0), stop=(k == KT - 1))
                if k == KT - 1:
                    mm.then_inc(item_full, 1)

            def values(at, h):
                for k in range(KT):
                    values_part(at, h, k)

            def scores(at, slot):
                h = 1 - slot
                for q in range(QT):
                    bank = take_bank(at, f"s{slot}.{q}")
                    cols = slice(q * P, (q + 1) * P)
                    product(bank[:, :], passes(qe_h[:, h, cols], qe_l[:, h, cols], k_h[:, h, :], k_l[:, h, :])
                            ).then_inc(item_full, 1)

            def distances(at, h, between):
                n = 2 * at.g + h
                pe.wait_ge(freed, item(at, f"q{h}") + 1)
                for q in range(QT):
                    cols = slice(q * P, (q + 1) * P)
                    for half, left in enumerate((dist_left, dist_right)):
                        if at is not step0 or 2 * n + q > 0:
                            pe.wait_ge(left, QT * n + q)
                        a = L - P - q * P + half * HALF_WIN
                        product(dist_ps[half][:, 0:HALF_WIN],
                                passes(qp_h[:, cols], qp_l[:, cols], rel_h[:, h, a:a + HALF_WIN],
                                       rel_l[:, h, a:a + HALF_WIN])).then_inc(dist_full, 1)
                    between(q)

            def transposes(at, slot):
                h, n = 1 - slot, 2 * at.g + slot - 1
                for q in range(QT):
                    bank = take_bank(at, f"t{slot}.{q}")
                    pe.wait_ge(prob_done, QT * n + q + 1)
                    for k in range(KT):
                        mm = pe.transpose(bank[:, k * P:(k + 1) * P], prob[:, 4 * h + q, k * P:(k + 1) * P],
                                          ident[:, :])
                    mm.then_inc(item_full, 1)

            def project_out(at, names):
                for oc, name in enumerate(names):
                    bank = take_bank(at, name)
                    terms = []
                    for h in range(2):
                        cols = slice(2 * DK * h + oc * P, 2 * DK * h + (oc + 1) * P)
                        terms += passes(wh[:, 3, cols], wl[:, 3, cols], o_h[:, h, :], o_l[:, h, :])
                    product(bank[:, :], terms).then_inc(item_full, 1)

            def split_before(at, name):
                pe.wait_ge(freed, item_base(at) - len(at.before) + at.before.index(name) + 1)

            def step(at):
                if "rel0" in at.items:
                    distance_keys(at)
                    pe.wait_ge(w_done, 2 * at.hp + 2)
                project_qk(at, 0)
                if "out0" in at.items:
                    if not at.pair_start:
                        pe.wait_ge(wo_done, at.hp + 1)
                    split_before(at, "val1")
                    project_out(at, ("out0", "out1"))
                if "s0.0" in at.items:
                    split_before(at, "k1")
                    scores(at, 0)
                    split_before(at, "t1.3")
                    distances(at, 0, lambda q: values_part(at, 0, q))
                    transposes(at, 0)
                else:
                    pe.wait_ge(freed, item(at, "rel3") + 1)
                    distances(at, 0, lambda q: None)
                project_qk(at, 1)
                if "val1" in at.items:
                    pe.wait_ge(freed, item(at, "t0.3") + 1)
                    values(at, 1)
                pe.wait_ge(freed, item(at, "k0") + 1)
                scores(at, 1)
                distances(at, 1, lambda q: v_tile(at, q))
                transposes(at, 1)

            def finish(at):
                split_before(at, "val1")
                project_out(at, ("out0", "out1"))
                scores(at, 0)
                split_before(at, "t1.3")
                values(at, 0)
                transposes(at, 0)
                pe.wait_ge(freed, item(at, "t0.3") + 1)
                values(at, 1)
                pe.wait_ge(freed, item(at, "val1") + 1)
                project_out(at, ("last0", "last1"))

            steps(pe, step, finish)

        @block.scalar
        def _(act):
            def split_weights(hp):
                act.wait_ge(pair_in, 48 * hp + 48)
                act.activation(wh[:, 0, :], raw_w[:, 0, :], ACT.Copy, scale=SCALE).then_inc(w_hi_done, 1)
                act.activation(wh[:, 1:3, :].rearrange("p m n -> p (m n)"),
                               raw_w[:, 1:3, :].rearrange("p m n -> p (m n)"), ACT.Copy).then_inc(w_hi_done, 1)

            def take(at, name, dst, view=lambda a: a):
                act.wait_ge(item_full, item(at, name) + 1)
                act.copy(dst, view(banks[BANK[name]][:, :])).then_inc(high_done, 1)

            def take_qk(at, h):
                act.wait_ge(item_full, item(at, f"q{h}") + 1)
                if "rel0" in at.items and h == 0:
                    act.wait_ge(bias_ready, at.hp + 1)
                bank = banks[BANK[f"q{h}"]]
                act.activation(qe_h[:, h, :], bank[:, :], ACT.Identity, bias=qb[:, h:h + 1])
                act.activation(qp_h[:, :], bank[:, :], ACT.Identity, bias=qb[:, 2 + h:3 + h]).then_inc(high_done, 1)
                take(at, f"k{h}", k_h[:, h, :])

            def exponentials(at, slot, q):
                h, n = 1 - slot, 2 * at.g + slot - 1
                i = 4 * h + q
                act.wait_ge(freed, item(at, f"s{slot}.{q}") + 1)
                act.activation(prob[:, i, :], prob[:, i, :], ACT.Exp, scale=-1.0, bias=nmax[:, i:i + 1],
                               accum_out=total[:, i:i + 1]).then_inc(exp_done, 1)

            def left_half(at, h, q):
                n = 2 * at.g + h
                if at is not step0 or n > 0:
                    act.wait_ge(stored[q], 16 * n)
                act.wait_ge(dist_full, 2 * QT * n + 2 * q + 1)
                act.copy(dist[:, q, 0:HALF_WIN], dist_ps[0][:, 0:HALF_WIN]).then_inc(dist_left, 1)

            def take_v(at, i):
                take(at, f"v{i}", v_h[:, 2 * i:2 * i + 2, :], lambda a: a.rearrange("p (t n) -> p t n", t=2))

            def take_transposed(at, slot):
                for q in range(QT):
                    take(at, f"t{slot}.{q}", pt_h[:, :, q * P:(q + 1) * P],
                         lambda a: a.rearrange("p (k n) -> p k n", k=KT))

            def slot(at, h, has_scores, after_tile):
                for q in range(QT):
                    if has_scores:
                        for e in {0: (0, 1), 1: (2,), 2: (3,), 3: ()}[q]:
                            exponentials(at, h, e)
                    if q == 2:
                        after_tile(0)
                    left_half(at, h, q)
                after_tile(1)

            def step(at):
                if "rel0" in at.items:
                    split_weights(at.hp)
                    for i, name in enumerate(REL):
                        take(at, name, rel_h[:, i // 2, (i % 2) * L:(i % 2 + 1) * L])
                take_qk(at, 0)
                before = "s0.0" in at.items
                slot(at, 0, before, lambda i: None)
                if before:
                    take(at, "val0", o_h[:, 0, :])
                    take_transposed(at, 0)
                take_qk(at, 1)
                if "val1" in at.items:
                    take(at, "val1", o_h[:, 1, :])
                slot(at, 1, True, lambda i: take_v(at, i))
                take_transposed(at, 1)
                if at.pair_start and at.odd == 1:
                    act.copy(wh[:, 3, :], raw_w[:, 3, :]).then_inc(wo_hi_done, 1)

            def finish(at):
                for q in range(QT):
                    exponentials(at, 0, q)
                take(at, "val0", o_h[:, 0, :])
                take_transposed(at, 0)
                take(at, "val1", o_h[:, 1, :])

            steps(act, step, finish)

        @block.gpsimd
        def _(pool):
            with pool.Fori(0, PAIRS * B) as g:
                for h in range(2):
                    for q in range(QT):
                        i = 4 * h + q
                        pool.wait_ge(rinv_done, QT * (2 * g + h) + q + 1)
                        pool.tensor_tensor(prob[:, i, :], prob[:, i, :], rinv[:, i:i + 1].to_broadcast([P, L]),
                                           ALU.mult).then_inc(prob_done, 1)

        @block.vector
        def _(dve):
            def split_weights(hp):
                dve.wait_ge(pair_in, 48 * hp + 48)
                dve.tensor_copy(qb[:, :], raw_qb[:, :]).then_inc(bias_ready, 1)
                dve.wait_ge(w_hi_done, 2 * hp + 1)
                dve.scalar_tensor_tensor(out=wl[:, 0, :], in0=raw_w[:, 0, :], scalar=SCALE,
                                         in1=wh[:, 0, :].bitcast(F32), op0=ALU.mult, op1=ALU.subtract
                                         ).then_inc(w_done, 1)
                dve.wait_ge(w_hi_done, 2 * hp + 2)
                dve.tensor_tensor(wl[:, 1:3, :], raw_w[:, 1:3, :], wh[:, 1:3, :].bitcast(F32), ALU.subtract
                                  ).then_inc(w_done, 1)
                dve.wait_ge(bias_ready, hp + 1)

            def take(at, name, lo, hi, view=lambda a: a):
                dve.wait_ge(high_done, high(at, name) + 1)
                dve.tensor_tensor(lo, view(banks[BANK[name]][:, :]), hi.bitcast(F32), ALU.subtract).then_inc(freed, 1)

            def take_qk(at, h):
                dve.wait_ge(high_done, high(at, f"q{h}") + 1)
                bank = banks[BANK[f"q{h}"]]
                dve.scalar_tensor_tensor(out=qe_l[:, h, :], in0=bank[:, :], scalar=qb[:, h:h + 1],
                                         in1=qe_h[:, h, :].bitcast(F32), op0=ALU.add, op1=ALU.subtract)
                dve.scalar_tensor_tensor(out=qp_l[:, :], in0=bank[:, :], scalar=qb[:, 2 + h:3 + h],
                                         in1=qp_h[:, :].bitcast(F32), op0=ALU.add, op1=ALU.subtract
                                         ).then_inc(freed, 1)
                take(at, f"k{h}", k_l[:, h, :], k_h[:, h, :])

            def logits(at, slot, q):
                h, m = 1 - slot, at.g + slot - 1
                i = 4 * h + q
                dve.wait_ge(skewed[i], 16 * m + 16 if slot == 0 else 16 * at.g + 16)
                dve.wait_ge(item_full, item(at, f"s{slot}.{q}") + 1)
                dve.nop().then_inc(scores_seen, 1)
                dve.tensor_tensor_reduce(out=prob[:, i, :], in0=banks[BANK[f"s{slot}.{q}"]][:, :],
                                         in1=prob[:, i, :], scale=-1.0, scalar=3.0e38, op0=ALU.add, op1=ALU.min,
                                         accum_out=nmax[:, i:i + 1]).then_inc(freed, 1)

            def inverse(at, slot, q):
                h, n = 1 - slot, 2 * at.g + slot - 1
                i = 4 * h + q
                dve.wait_ge(exp_done, QT * n + q + 1)
                dve.reciprocal(rinv[:, i:i + 1], total[:, i:i + 1]).then_inc(rinv_done, 1)

            def right_half(at, h, q):
                n = 2 * at.g + h
                if at is not step0 or n > 0:
                    dve.wait_ge(stored[q], 16 * n)
                dve.wait_ge(dist_full, 2 * QT * n + 2 * q + 2)
                dve.tensor_copy(dist[:, q, HALF_WIN:WIN], dist_ps[1][:, 0:HALF_WIN]).then_inc(dist_right, 1)

            def take_v(at, i):
                take(at, f"v{i}", v_l[:, 2 * i:2 * i + 2, :], v_h[:, 2 * i:2 * i + 2, :],
                     lambda a: a.rearrange("p (t n) -> p t n", t=2))

            def take_transposed(at, slot):
                for q in range(QT):
                    cols = slice(q * P, (q + 1) * P)
                    take(at, f"t{slot}.{q}", pt_l[:, :, cols], pt_h[:, :, cols],
                         lambda a: a.rearrange("p (k n) -> p k n", k=KT))

            def add_out(at, names, b):
                for oc, name in enumerate(names):
                    dve.wait_ge(item_full, item(at, name) + 1)
                    acc = x1[:, oc, bass.ds(b, 1), :].rearrange("p b l -> p (b l)")
                    dve.tensor_tensor(acc, banks[BANK[name]][:, :], acc, ALU.add).then_inc(freed, 1)

            def slot(at, h, has_scores, after_tile):
                if has_scores:
                    logits(at, h, 0)
                    logits(at, h, 1)
                    logits(at, h, 2)
                    inverse(at, h, 0)
                    logits(at, h, 3)
                    inverse(at, h, 1)
                for q in range(QT):
                    right_half(at, h, q)
                    if has_scores and q < 2:
                        inverse(at, h, q + 2)
                    if q == 1:
                        after_tile(0)
                after_tile(1)

            def step(at):
                if "rel0" in at.items:
                    split_weights(at.hp)
                    for i, name in enumerate(REL):
                        cols = slice((i % 2) * L, (i % 2 + 1) * L)
                        take(at, name, rel_l[:, i // 2, cols], rel_h[:, i // 2, cols])
                take_qk(at, 0)
                if "out0" in at.items:
                    add_out(at, ("out0", "out1"), B - 2 + at.odd if at.pair_start else 2 * at.bb + at.odd - 2)
                before = "s0.0" in at.items
                slot(at, 0, before, lambda i: None)
                if before:
                    take(at, "val0", o_l[:, 0, :], o_h[:, 0, :])
                    take_transposed(at, 0)
                take_qk(at, 1)
                if "val1" in at.items:
                    take(at, "val1", o_l[:, 1, :], o_h[:, 1, :])
                slot(at, 1, True, lambda i: take_v(at, i))
                take_transposed(at, 1)
                if at.pair_start and at.odd == 1:
                    dve.wait_ge(wo_hi_done, at.hp + 1)
                    dve.tensor_tensor(wl[:, 3, :], raw_w[:, 3, :], wh[:, 3, :].bitcast(F32), ALU.subtract
                                      ).then_inc(wo_done, 1)

            def finish(at):
                add_out(at, ("out0", "out1"), B - 2)
                for q in range(QT):
                    logits(at, 0, q)
                for q in range(QT):
                    inverse(at, 0, q)
                take(at, "val0", o_l[:, 0, :], o_h[:, 0, :])
                take_transposed(at, 0)
                take(at, "val1", o_l[:, 1, :], o_h[:, 1, :])
                add_out(at, ("last0", "last1"), B - 1)

            steps(dve, step, finish)


GATES = 4
GC = GATES * D // P
FFN_EXPERTS = 8
TB = 64
BLOCKS = L // TB
SUB = TB // 4
UP = 16.0



MADE = 9


class RecurrenceAhead:

    def __init__(self, s, condT, wx, wh, gate_bias, router_w, router_b, row_mask, count8, identity):
        self.raw = s.sb("raw_gates", [P, 2, KD, GC * P])
        self.h0 = s.sb("h0", [P, KD, B])
        self.gbias, self.rbias = s.sb("gbias", [P, GC]), s.sb("rbias", [P, 8])
        self.mask, self.count = s.sb("mask", [2, 2]), s.sb("count", [P, 8])
        self.rraw = s.sb("rraw", [P, KD, 8])
        self.ident = s.sb("ident3", [P, P])
        self.loads = ((self.raw[:, 0, :, :], wx.rearrange("(k p) n -> p k n", p=P)),
                      (self.raw[:, 1, :, :], wh.rearrange("(k p) n -> p k n", p=P)),
                      (self.ident[:, :], identity), (self.h0[:, :, :], condT.rearrange("(k p) b -> p k b", p=P)),
                      (self.gbias[:, :], gate_bias), (self.rbias[:, :], router_b), (self.count[:, :], count8),
                      (self.rraw[:, :, :], router_w.rearrange("(k p) e -> p k e", p=P)),
                      (self.mask[:, :], row_mask))


def recurrence(nc, ahead, expert_w, expert_b, x1, out):
    GK = GC * P
    EK = FFN_EXPERTS * D
    with ExitStack() as ctx:
        s = Scope(nc, ctx)
        raw = s.sb("raw_experts", [P, KD, EK])
        raw_gates, h0, gbias, rbias, mask, count, rraw, ident = (
            ahead.raw, ahead.h0, ahead.gbias, ahead.rbias, ahead.mask, ahead.count, ahead.rraw, ahead.ident)
        wxh, wxl = s.sb("wxh", [P, KD * GK], F16), s.sb("wxl", [P, KD * GK], F16)
        whh, whl = s.sb("whh", [P, KD, GK], F16), s.sb("whl", [P, KD, GK], F16)
        weh, wel = s.sb("weh", [P, KD, EK], F16), s.sb("wel", [P, KD, EK], F16)
        wrh, wrl = s.sb("wrh", [P, KD, 8], F16), s.sb("wrl", [P, KD, 8], F16)
        eb, ebh, ebl = s.sb("eb", [2, EK]), s.sb("ebh", [2, EK], F16), s.sb("ebl", [2, EK], F16)
        ebm, rows = s.sb("ebm", [2, EK], F16), s.sb("rows", [2, EK], F16)
        ones2, factor = s.sb("ones2", [2, P], F16), s.sb("factor", [P, 1])
        ident16 = s.sb("ident16", [P, P], F16)
        xs_h, xs_l = s.sb("xs_h", [P, KD, B, TB], F16), s.sb("xs_l", [P, KD, B, TB], F16)
        share = s.sb("share", [P, 2 * TB * GC * B])
        now = s.sb("now", [P, 4, GC, 2 * B], F16)
        hs = s.sb("hs", [P, 4, KD, 2 * B], F16)
        hist = s.sb("hist", [P, 2 * 2 * KD * B * TB], F16)
        f, gi, o = s.sb("forget", [P, 2, 2 * B]), s.sb("cand_in", [P, 2, 4 * B]), s.sb("out_gate", [P, 2, 2 * B])
        cell, fc, ig = s.sb("cell", [P, 2, 2 * B]), s.sb("fc", [P, 2, 2 * B]), s.sb("ig", [P, 2, 2 * B])
        tc, h = s.sb("tc", [P, 2, 2 * B]), s.sb("hidden", [P, 2, 2 * B])
        xt = s.sb("xt", [P, KD, P])
        acc = s.sb("acc3", [P, D])
        logit, zexp, sig_p, sig_n, inv_n, cand, pick = (
            s.sb(n, [P, 8]) for n in ("logit", "zexp", "sig_p", "sig_n", "inv_n", "cand", "pick"))
        top, zsum, gate, first_top = (s.sb(n, [P, 1]) for n in ("top", "zsum", "gate", "first_top"))
        f_ps, gi_ps, o_ps, share_ps, route_ps, xt_ps = (
            s.ps(n) for n in ("f_ps", "gi_ps", "o_ps", "share_ps", "route_ps", "xt_ps"))
        ffn_ps = [s.ps(f"ffn_ps{i}") for i in range(2)]

        experts_in, experts_step, experts_split = s.sem("experts_in"), s.sem("experts_step"), s.sem("experts_split")
        made, gates_hi_done, gates_split = s.sem("made"), s.sem("gates_hi_done"), s.sem("gates_split")
        hi_ready, h_ready, lo_ready = s.sem("hi_ready"), s.sem("h_ready"), s.sem("lo_ready")
        f_full, gi_full, o_full = s.sem("f_full"), s.sem("gi_full"), s.sem("o_full")
        f_added, gi_added, o_added = s.sem("f_added"), s.sem("gi_added"), s.sem("o_added")
        f_done, gi_done, o_done = s.sem("f_done"), s.sem("gi_done"), s.sem("o_done")
        ig_done, cell_done, tanh_done = (s.sem(n) for n in ("ig_done", "cell_done", "tanh_done"))
        hist_done = s.sem("hist_done")
        xs_hi_done, xs_done = s.sem("xs_hi_done"), s.sem("xs_done")
        pre_f, pre_gi, pre_o = f_ps[:, 64:64 + 2 * B], gi_ps[:, 64:64 + 4 * B], o_ps[:, 64:64 + 2 * B]

        share_full, share_done, now_hi_done, now_hi_seen, now_done = (
            s.sem(n) for n in ("share_full", "share_done", "now_hi_done", "now_hi_seen", "now_done"))
        routed, xt_done, xt_full, acc_init = (s.sem(n) for n in ("routed", "xt_done", "xt_full", "acc_init"))
        logit_done, zmax_done, sig_done, gate_step, pick_done = (
            s.sem(n) for n in ("logit_done", "zmax_done", "sig_done", "gate_step", "pick_done"))
        ffn_full, acc_step, out_sent = s.sem("ffn_full"), s.sem("acc_step"), s.sem("out_sent")
        block = ctx.enter_context(nc.Block())

        def blocks(eng, body, before_routed=lambda: None, start=lambda j: None):
            start(0)
            with eng.Fori(0, 4) as q:
                body(0, q, False, True)
            before_routed()
            with eng.Fori(1, BLOCKS - 1) as j:
                start(j)
                with eng.Fori(0, 4) as q:
                    body(j, q, True, True)
            with eng.Fori(0, 4) as q:
                body(BLOCKS - 1, q, True, False)

        def after(eng, side):
            with eng.Fori(0, 4) as q:
                for i in range(SUB):
                    side(BLOCKS, q, i, True, False)

        two = lambda a: a[:, :].rearrange("p (k n) -> p k n", k=KD)
        GATE_PARTS = ((0, 2 * P, UP), (2 * P, 4 * P, 2 * UP), (4 * P, GK, UP))

        def share_view(jb, c):
            v = share[:, :].rearrange("p (r t g b) -> p r g b t", r=2, t=TB, g=GC)
            return v[:, bass.ds(jb % 2, 1), bass.ds(c, 1), :, :].rearrange("p r g b t -> p (r g b) t")

        @block.sync
        def _(sp):
            sp.dma_start(raw[:, :, :], expert_w.rearrange("(k p) n -> p k n", p=P)).then_inc(experts_in, 16)
            sp.dma_start(eb[:, :], expert_b).then_inc(experts_in, 16)
            sp.nop().then_inc(out_sent, 32)
            with sp.Fori(1, BLOCKS + 1) as j:
                with sp.Fori(0, 4) as q:
                    sp.wait_ge(acc_step, FFN_EXPERTS * (4 * (j - 1) + q + 1) + 4)
                    for i in range(2):
                        dst = out[bass.ds(2 * q + i, 1), bass.ds(TB * (j - 1), TB), :]
                        sp.dma_start(dst.rearrange("b t d -> (b t) d"), acc[TB * i:TB * (i + 1), :]
                                     ).then_inc(out_sent, 16)
            sp.wait_ge(out_sent, 32 * 4 * BLOCKS + 32)

        @block.tensor
        def _(pe):
            def low_products(bank, slot, g0, g1):
                for g in range(g0, g1):
                    for k in range(KD):
                        pe.matmul(bank[:, (g - g0) * 2 * B:(g - g0) * 2 * B + B], whl[:, k, g * P:(g + 1) * P],
                                  hs[:, slot, k, 0:B], start=False, stop=False, skip_group_check=True)

            def high_products(bank, slot, g0, g1):
                for g in range(g0, g1):
                    for k in range(KD):
                        mm = pe.matmul(bank[:, (g - g0) * 2 * B:(g - g0 + 1) * 2 * B], whh[:, k, g * P:(g + 1) * P],
                                       hs[:, slot, k, :], start=False, stop=True, skip_group_check=True)
                return mm

            def put_share(T, slot, bank, a, z, done):
                pe.wait_ge(done, T + 1)
                pe.matmul(bank[:, 0:(z - a) * 2 * B], ident16[:, :],
                          now[:, slot, a:z, :].rearrange("p g n -> p (g n)"), start=True, stop=False,
                          skip_group_check=True)

            def share_terms(jb, c, lo, hi, bank=share_ps, buffers=1):
                if lo == 0:
                    pe.wait_ge(share_done, GC * jb + c + 3 - buffers)
                    pe.wait_ge(xs_done, jb + 1)
                terms = [(w, x, k) for w, x in ((wxh, xs_h), (wxh, xs_l), (wxl, xs_h)) for k in range(KD)]
                for n in range(lo, hi):
                    w, x, k = terms[n]
                    mm = pe.matmul(bank[:, :], w[:, bass.ds(P * c + GK * k, P)],
                                   x[:, k, :, :].rearrange("p b t -> p (b t)"), start=(n == 0), stop=(n == 5))
                if hi == 6:
                    mm.then_inc(share_full, 1)

            def hidden(j, part, k, q):
                return hist[:, bass.ds(2048 * ((j + 1) % 2) + 1024 * part + 512 * k + P * q, P)]

            def route(j, q):
                m = 4 * (j - 1) + q
                pe.wait_ge(hist_done, TB * j + 4)
                pe.wait_ge(logit_done, m + 1)
                n = 0
                for part, w in ((0, wrh), (1, wrh), (0, wrl)):
                    for k in range(KD):
                        mm = pe.matmul(route_ps[:, 0:8], hidden(j, part, k, q), w[:, k, :], start=(n == 0),
                                       stop=(n == 5))
                        n += 1
                mm.then_inc(routed, 1)

            def turn_x1(j, q):
                m = 4 * (j - 1) + q
                pe.wait_ge(xt_done, m + 1)
                pe.wait_ge(acc_init, m + 1)
                for k in range(KD):
                    mm = pe.transpose(xt_ps[:, k * P:(k + 1) * P], xt[:, k, :], ident[:, :])
                mm.then_inc(xt_full, 1)

            def experts(j, q, a, z):
                m = 4 * (j - 1) + q
                for n in range(a, z):
                    e, n = divmod(n, 7)
                    bank = ffn_ps[e % 2]
                    cols = slice(2 * D * e, 2 * D * (e + 1))
                    if n == 0:
                        pe.wait_ge(acc_step, FFN_EXPERTS * m + 2 * e + 2)
                        pe.matmul(bank[:, :], ones2[:, :], rows[:, cols], start=True, stop=False)
                        continue
                    part, w, k = [(part, w, k) for part, w in ((0, weh), (1, weh), (0, wel)) for k in range(KD)][n - 1]
                    mm = pe.matmul(bank[:, :], hidden(j, part, k, q), w[:, k, cols], start=False, stop=(n == 6))
                    if n == 6:
                        mm.then_inc(ffn_full, 1)

            EXPERTS_AT = {2: (0, 2), 3: (2, 5), 4: (5, 8), 5: (8, 11), 8: (11, 14), 9: (14, 17), 10: (17, 21),
                          13: (21, 25), 14: (25, 28)}
            SHARE_AT = {6: (0, 0, 3), 7: (0, 3, 6), 11: (1, 0, 3), 12: (1, 3, 6)}

            def side(j, q, i, routing, sharing):
                if routing and i == 1:
                    route(j, q)
                if routing and i == 2:
                    turn_x1(j, q)
                if routing and i in EXPERTS_AT:
                    experts(j, q, *EXPERTS_AT[i])
                if sharing and i in SHARE_AT:
                    c, lo, hi = SHARE_AT[i]
                    share_terms(j + 1, 2 * q + c, lo, hi)

            def body(j, q, routing, sharing):
                for i in range(SUB):
                    T, slot = TB * j + SUB * q + i, i % 4
                    pe.wait_ge(now_done, T + 1)
                    side(j, q, i, routing, sharing)
                    put_share(T, slot, f_ps, 0, 2, f_done)
                    put_share(T, slot, gi_ps, 2, 6, gi_done)
                    pe.wait_ge(hi_ready, T + 1)
                    low_products(f_ps, slot, 0, 2)
                    low_products(gi_ps, slot, 2, 6)
                    pe.wait_ge(lo_ready, T + 1)
                    high_products(f_ps, slot, 0, 2).then_inc(f_full, 1)
                    high_products(gi_ps, slot, 2, 6).then_inc(gi_full, 1)
                    put_share(T, slot, o_ps, 6, 8, o_done)
                    low_products(o_ps, slot, 6, 8)
                    high_products(o_ps, slot, 6, 8).then_inc(o_full, 1)

            pe.wait_ge(gates_split, 2)
            with pe.Fori(0, GC // 2) as c:
                for i, bank in enumerate((share_ps, ffn_ps[0])):
                    share_terms(0, 2 * c + i, 0, 6, bank, buffers=2)
            pe.wait_ge(gates_split, 4)
            pe.wait_ge(made, MADE)
            blocks(pe, body, lambda: pe.wait_ge(experts_split, 4))
            after(pe, side)

        @block.scalar
        def _(act):
            for free, n in ((f_done, 1), (gi_done, 1), (o_done, 1), (acc_init, 1), (share_done, 2)):
                act.nop().then_inc(free, n)

            def high_x1(jb):
                src = x1[:, :, :, bass.ds(TB * jb, TB)]
                for k in range(KD):
                    act.copy(xs_h[:, k, :, :], src[:, k, :, :]).then_inc(xs_hi_done, 1)

            def take_share(jb, c, bank=share_ps):
                act.wait_ge(share_full, GC * jb + c + 1)
                act.activation(share_view(jb, c), bank[:, :].rearrange("p (b t) -> p b t", t=TB),
                               ACT.Identity, bias=gbias[:, bass.ds(c, 1)]).then_inc(share_done, 1)

            def side(j, q, i, routing, sharing):
                m = 4 * (j - 1) + q
                if routing and i == 2:
                    act.wait_ge(zmax_done, m + 1)
                    act.activation(sig_p[:, :], zexp[:, :], ACT.Sigmoid).then_inc(sig_done, 1)
                    act.activation(sig_n[:, :], zexp[:, :], ACT.Sigmoid, scale=-1.0).then_inc(sig_done, 1)
                if routing and i == 3:
                    act.wait_ge(xt_full, m + 1)
                    act.wait_ge(out_sent, 32 * m + 32)
                    act.copy(acc[:, :], xt_ps[:, 0:D]).then_inc(acc_init, 1)
                if sharing and i in (7, 12):
                    take_share(j + 1, 2 * q + i // 12)

            def body(j, q, routing, sharing):
                for i in range(SUB):
                    T, p = TB * j + SUB * q + i, i % 2
                    act.wait_ge(f_added, T + 1)
                    act.activation(f[:, p, :], pre_f, ACT.Sigmoid,
                                   scale=1.0 / UP).then_inc(f_done, 1)
                    act.wait_ge(gi_added, T + 1)
                    act.activation(gi[:, p, :], pre_gi, ACT.Sigmoid,
                                   scale=1.0 / UP).then_inc(gi_done, 1)
                    act.wait_ge(o_added, T + 1)
                    act.activation(o[:, p, :], pre_o, ACT.Sigmoid,
                                   scale=1.0 / UP).then_inc(o_done, 1)
                    act.wait_ge(cell_done, T + 1)
                    act.activation(tc[:, p, :], cell[:, p, :], ACT.Tanh, scale=2.0).then_inc(tanh_done, 1)
                    side(j, q, i, routing, sharing)

            high_x1(0)
            for m, hi in ((0, two(wxh)), (1, whh[:, :, :])):
                for i, (a, z, up) in enumerate(GATE_PARTS):
                    act.activation(hi[:, :, a:z], raw_gates[:, m, :, a:z], ACT.Copy, scale=up).then_inc(gates_hi_done, 1)
                if m == 0:
                    act.wait_ge(made, 2)
                    with act.Fori(0, GC // 2) as c:
                        for i, bank in enumerate((share_ps, ffn_ps[0])):
                            take_share(0, 2 * c + i, bank)
            act.wait_ge(made, MADE)
            blocks(act, body, start=lambda j: high_x1(j + 1))
            after(act, side)

        @block.gpsimd
        def _(pool):
            pool.nop().then_inc(hist_done, 4)

            def tile_x1(j, q):
                src = x1[:, :, bass.ds(2 * q, 2), bass.ds(TB * (j - 1), TB)]
                pool.tensor_copy(xt[:, :, :].rearrange("p k (b t) -> p k b t", b=2), src).then_inc(xt_done, 1)

            def split_experts(q, i):
                cols = bass.ds(2 * D * q, 2 * D)
                k = 0 if i < 5 else 1
                if i == 1 and not isinstance(q, int):
                    pool.wait_ge(experts_in, 32)
                if i in (1, 5):
                    ins = pool.tensor_tensor(raw[:, k, cols], raw[:, k, cols], factor[:, :].to_broadcast([P, 2 * D]),
                                             ALU.mult)
                if i in (2, 6):
                    ins = pool.tensor_copy(weh[:, k, cols], raw[:, k, cols])
                if i in (3, 7):
                    ins = pool.tensor_tensor(wel[:, k, cols], raw[:, k, cols], weh[:, k, cols], ALU.subtract)
                if i == 9:
                    ins = pool.tensor_tensor(eb[:, cols], eb[:, cols], factor[0:2, :].to_broadcast([2, 2 * D]), ALU.mult)
                if i == 10:
                    ins = pool.tensor_copy(ebh[:, cols], eb[:, cols])
                if i == 11:
                    ins = pool.tensor_tensor(ebl[:, cols], eb[:, cols], ebh[:, cols], ALU.subtract)
                if i == 12:
                    ins = pool.tensor_tensor(ebm[:, cols], ebh[:, cols], mask[:, 0:1].to_broadcast([2, 2 * D]), ALU.mult)
                if i == 13:
                    ins = pool.tensor_tensor(ebl[:, cols], ebl[:, cols], mask[:, 1:2].to_broadcast([2, 2 * D]), ALU.mult)
                if i == 14:
                    pool.tensor_tensor(rows[:, cols], ebl[:, cols], ebm[:, cols], ALU.add).then_inc(experts_split, 1)
                elif i in EXPERT_OPS:
                    ins.then_inc(experts_step, 1)
                    pool.wait_ge(experts_step, len(EXPERT_OPS) * q + EXPERT_OPS.index(i) + 1)

            EXPERT_OPS = (1, 2, 3, 5, 6, 7, 9, 10, 11, 12, 13)

            def split_share(src, slot, T):
                src = src.rearrange("p (g b) -> p g b", b=B)
                pool.tensor_copy(now[:, slot, :, 0:B], src).then_inc(now_hi_done, 1)
                pool.wait_ge(now_hi_done, T + 1)
                pool.nop().then_inc(now_hi_seen, 1)
                pool.tensor_tensor(now[:, slot, :, B:2 * B], src, now[:, slot, :, 0:B], ALU.subtract
                                   ).then_inc(now_done, 1)

            def body(j, q, routing, sharing):
                for i in range(SUB):
                    T = TB * j + SUB * q + i
                    if routing and i == 0:
                        tile_x1(j, q)
                    pool.wait_ge(lo_ready, T + 2)
                    rows_t = hist[:, :].rearrange("p (n t) -> p n t", t=TB)
                    dst = rows_t[:, bass.ds(2 * KD * B * (j % 2), 2 * KD * B), bass.ds(SUB * q + i, 1)]
                    pool.tensor_copy(dst.rearrange("p (s k b) t -> p s k (b t)", s=2, k=KD),
                                     hs[:, (i + 1) % 4, :, :].rearrange("p k (s b) -> p s k b", s=2)
                                     ).then_inc(hist_done, 1)
                    if sharing and i == SUB - 3:
                        pool.wait_ge(share_done, GC * (j + 1) + 2 * q + 2 + 2)
                    column = ((TB * (j % 2) + SUB * q + i + 3) % (2 * TB)) * (GC * B)
                    split_share(share[:, bass.ds(column, GC * B)], (i + 3) % 4, T + 3)
                    if not routing:
                        split_experts(q, i)

            pool.wait_ge(made, MADE)
            pool.wait_ge(share_done, GC + 2)
            for t in range(3):
                split_share(share[:, t * GC * B:(t + 1) * GC * B], t, t)
            blocks(pool, body)
            with pool.Fori(0, 4) as q:
                pool.wait_ge(xt_full, 4 * (BLOCKS - 1) + q)
                tile_x1(BLOCKS, q)

        @block.vector
        def _(dve):
            dve.nop().then_inc(logit_done, 1)
            dve.nop().then_inc(acc_step, 4)
            count_made = [0]

            def then(ins):
                count_made[0] += 1
                ins.then_inc(made, 1)
                dve.wait_ge(made, count_made[0])

            then(dve.tensor_scalar(gbias[:, :], gbias[:, :], UP, None, ALU.mult))
            then(dve.tensor_scalar(gbias[:, 2:4], gbias[:, 2:4], 2.0, None, ALU.mult))

            def low_x1(jb):
                src = x1[:, :, :, bass.ds(TB * jb, TB)]
                for k in range(KD):
                    dve.wait_ge(xs_hi_done, KD * jb + k + 1)
                    ins = dve.tensor_tensor(xs_l[:, k, :, :], src[:, k, :, :], xs_h[:, k, :, :], ALU.subtract)
                ins.then_inc(xs_done, 1)

            low_x1(0)

            def low_gates(m, hi, lo):
                for i, (a, z, up) in enumerate(GATE_PARTS):
                    dve.wait_ge(gates_hi_done, len(GATE_PARTS) * m + i + 1)
                    ins = dve.scalar_tensor_tensor(out=lo[:, :, a:z], in0=raw_gates[:, m, :, a:z], scalar=up,
                                                   in1=hi[:, :, a:z], op0=ALU.mult, op1=ALU.subtract)
                ins.then_inc(gates_split, 2)

            def side(j, q, i, routing, sharing):
                m = 4 * (j - 1) + q
                G = 7
                if routing and i == 1:
                    dve.wait_ge(routed, m + 1)
                    dve.scalar_tensor_tensor(out=logit[:, :], in0=route_ps[:, 0:8], scalar=1.0 / UP,
                                             in1=rbias[:, :], op0=ALU.mult, op1=ALU.add).then_inc(logit_done, 1)
                    dve.wait_ge(logit_done, m + 2)
                    dve.tensor_reduce(top[:, :], logit[:, :], AX.X, ALU.max).then_inc(gate_step, 1)
                    dve.wait_ge(gate_step, G * m + 1)
                    dve.tensor_scalar(zexp[:, :], logit[:, :], top[:, 0:1], None, ALU.subtract).then_inc(zmax_done, 1)
                if routing and i == 2:
                    dve.tensor_scalar(cand[:, :], logit[:, :], top[:, 0:1], None, ALU.is_lt).then_inc(gate_step, 1)
                    dve.wait_ge(gate_step, G * m + 2)
                    dve.scalar_tensor_tensor(out=cand[:, :], in0=cand[:, :], scalar=8.0, in1=count[:, :],
                                             op0=ALU.mult, op1=ALU.add).then_inc(gate_step, 1)
                    dve.wait_ge(gate_step, G * m + 3)
                    dve.tensor_reduce(first_top[:, :], cand[:, :], AX.X, ALU.min).then_inc(gate_step, 1)
                if routing and i == 3:
                    dve.wait_ge(sig_done, 2 * m + 2)
                    dve.reciprocal(inv_n[:, :], sig_n[:, :]).then_inc(gate_step, 1)
                    dve.wait_ge(gate_step, G * m + 5)
                    dve.tensor_tensor(inv_n[:, :], inv_n[:, :], sig_p[:, :], ALU.mult).then_inc(gate_step, 1)
                    dve.wait_ge(gate_step, G * m + 6)
                    dve.tensor_reduce(zsum[:, :], inv_n[:, :], AX.X, ALU.add).then_inc(gate_step, 1)
                if routing and i == 4:
                    dve.wait_ge(gate_step, G * m + 7)
                    dve.reciprocal(gate[:, :], zsum[:, :]).then_inc(pick_done, 1)
                    dve.wait_ge(pick_done, 3 * m + 1)
                    dve.tensor_scalar(gate[:, :], gate[:, :], 1.0 / UP, None, ALU.mult).then_inc(pick_done, 1)
                    dve.wait_ge(pick_done, 3 * m + 2)
                    dve.tensor_scalar(pick[:, :], count[:, :], first_top[:, 0:1], gate[:, 0:1], ALU.is_equal,
                                      ALU.mult).then_inc(pick_done, 1)
                ADD_AT = {5: 0, 6: 1, 9: 2, 10: 3, 11: 4, 12: 5, 14: 6, 15: 7}
                if routing and i in ADD_AT:
                    e = ADD_AT[i]
                    if e == 0:
                        dve.wait_ge(pick_done, 3 * m + 3)
                        dve.wait_ge(acc_init, m + 2)
                    else:
                        dve.wait_ge(acc_step, FFN_EXPERTS * m + e + 4)
                    dve.wait_ge(ffn_full, 4 * m + e // 2 + 1)
                    dve.scalar_tensor_tensor(out=acc[:, :], in0=ffn_ps[(e // 2) % 2][:, (e % 2) * D:(e % 2 + 1) * D],
                                             scalar=pick[:, e:e + 1], in1=acc[:, :], op0=ALU.mult,
                                             op1=ALU.add).then_inc(acc_step, 1)

            def halves(a):
                return a.rearrange("p (k n) -> p k n", k=KD)

            def body(j, q, routing, sharing):
                for i in range(SUB):
                    T, p, nxt = TB * j + SUB * q + i, i % 2, (i + 1) % 4
                    dve.wait_ge(hist_done, T + 1)
                    for bank, n, pre, full, added in ((f_ps, 2, pre_f, f_full, f_added),
                                                      (gi_ps, 4, pre_gi, gi_full, gi_added),
                                                      (o_ps, 2, pre_o, o_full, o_added)):
                        dve.wait_ge(full, T + 1)
                        dve.tensor_reduce(pre.rearrange("p (g b) -> p g b", b=B),
                                          bank[:, 0:n * 2 * B].rearrange("p (g s b) -> p g b s", g=n, s=2),
                                          AX.X, ALU.add).then_inc(added, 1)
                    dve.wait_ge(f_done, T + 2)
                    dve.tensor_tensor(fc[:, p, :], f[:, p, :], cell[:, 1 - p, :], ALU.mult)
                    dve.wait_ge(gi_done, T + 2)
                    dve.scalar_tensor_tensor(out=ig[:, p, :], in0=gi[:, p, 0:2 * B], scalar=-0.5,
                                             in1=gi[:, p, 2 * B:4 * B], op0=ALU.add, op1=ALU.mult).then_inc(ig_done, 1)
                    dve.wait_ge(ig_done, T + 1)
                    dve.tensor_tensor(cell[:, p, :], ig[:, p, :], fc[:, p, :], ALU.add).then_inc(cell_done, 1)
                    dve.wait_ge(tanh_done, T + 1)
                    dve.tensor_tensor(hs[:, nxt, :, 0:B], halves(o[:, p, :]), halves(tc[:, p, :]),
                                      ALU.mult).then_inc(hi_ready, 1)
                    dve.tensor_tensor(h[:, p, :], o[:, p, :], tc[:, p, :], ALU.mult).then_inc(h_ready, 1)
                    dve.wait_ge(h_ready, T + 1)
                    dve.tensor_tensor(hs[:, nxt, :, B:2 * B], halves(h[:, p, :]), hs[:, nxt, :, 0:B],
                                      ALU.subtract).then_inc(lo_ready, 1)
                    side(j, q, i, routing, sharing)

            low_gates(0, two(wxh), two(wxl))
            then(dve.memset(ones2[:, :], 1.0))
            then(dve.memset(factor[:, :], UP))
            then(dve.memset(cell[:, 1, :], 0.0))
            then(dve.tensor_copy(ident16[:, :], ident[:, :]))
            low_gates(1, whh, whl)
            then(dve.tensor_scalar(rraw[:, :, :], rraw[:, :, :], UP, None, ALU.mult))
            then(dve.tensor_copy(wrh[:, :, :], rraw[:, :, :]))
            then(dve.tensor_tensor(wrl[:, :, :], rraw[:, :, :], wrh[:, :, :], ALU.subtract))
            assert count_made[0] == MADE
            dve.tensor_copy(hs[:, 0, :, 0:B], h0[:, :, :]).then_inc(hi_ready, 1)
            dve.wait_ge(hi_ready, 1)
            dve.tensor_tensor(hs[:, 0, :, B:2 * B], h0[:, :, :], hs[:, 0, :, 0:B], ALU.subtract).then_inc(lo_ready, 1)
            blocks(dve, body, start=lambda j: low_x1(j + 1))
            after(dve, side)


def embedded_block_kernel(nc, xT, condT, gate_w, gate_b, time_w, time_b, steps, w1, w2, mix_biases, wqkvo, wrel,
                          positions, qbias, b_out, identity, wx, wh, gate_bias, router_w, router_b, expert_w,
                          expert_b, row_mask, count8, out):
    context = nc.dram_tensor("context", [B, P, 2, KD, L], F32, kind="Internal").ap()
    skew = nc.dram_tensor("skew", [HEADS * P * WIN], F32, kind="Internal").ap()
    with ExitStack() as ctx:
        s = Scope(nc, ctx)
        x1 = s.sb("x1", [P, KD, B, L])
        ahead = RecurrenceAhead(s, condT, wx, wh, gate_bias, router_w, router_b, row_mask, count8, identity)
        with ExitStack() as attention_ctx:
            inputs = AttentionAhead(Scope(nc, attention_ctx), x1, wqkvo, wrel, positions, qbias, b_out, identity)
            gating_inputs = (condT, gate_w, gate_b, time_w, time_b, steps)
            mixture(nc, xT, w1, w2, mix_biases, gating_inputs, context, inputs)
            attention(nc, wqkvo, wrel, qbias, context, skew, inputs, ahead.loads)
        recurrence(nc, ahead, expert_w, expert_b, x1, out)


def _lgamma(x):
    import math
    import numpy as np
    f = np.float32
    total = f(0.99999999999980993227684700473478)
    z = x - f(1)
    for i, c in enumerate((676.520368121885098567009190444019, -1259.13921672240287047156078755283,
                           771.3234287776530788486528258894, -176.61502916214059906584551354,
                           12.507343278686904814458936853, -0.13857109526572011689554707,
                           9.984369578019570859563e-6, 1.50563273514931155834e-7)):
        total = total + f(c) / (z + f(i + 1))
    t, log_t = f(7.5) + z, f(math.log(7.5)) + np.log1p(z / f(7.5))
    return f(0.5 * math.log(2 * math.pi)) + (z + f(0.5) - t / log_t) * log_t + np.log(total)


def _positional_features(seq, features):
    import math
    import numpy as np
    f = np.float32
    n = features // 6

    def linspace(a, z):
        i = np.arange(n - 1, dtype=f) / f(n - 1)
        return np.concatenate([f(a) * (f(1) - i) + f(z) * i, [f(z)]]).astype(f)[None]

    distance = np.arange(-seq + 1, seq).astype(f)
    absd = np.abs(distance)[:, None]
    half_life = f(2) ** linspace(3.0, math.log(seq) / math.log(2.0))
    decay = np.exp(-f(math.log(2.0)) / half_life * absd)
    center = (f(2) ** np.arange(1, n + 1).astype(f) - f(1) > absd).astype(f)
    deviation = seq / (2.0 * n)
    mean = linspace(seq / n, float(seq))
    conc, rate = (mean / f(deviation)) ** 2, mean / f(deviation ** 2)
    log_d = np.log(np.maximum(absd, f(1e-30)))
    density = np.exp((conc - f(1)) * log_d - rate * absd - (_lgamma(conc) - conc * np.log(rate))) + f(1e-8)
    emb = np.concatenate([decay, center, density / density.max(-1, keepdims=True)], -1)
    return np.concatenate([emb, np.sign(distance)[:, None] * emb], -1)


def _gate_order(a):
    import numpy as np
    i, f, o, g = (a[..., n * D:(n + 1) * D] for n in range(4))
    return np.concatenate([f, g, i, o], -1)


def _layout(t):
    import numpy as np
    c = {}
    c["xT"] = t["x"].transpose(2, 0, 1)
    c["condT"] = t["cond_1024"].T
    c["gate_w"], c["gate_b"] = t["L0_cond_gate_w"], t["L0_cond_gate_b"]
    c["time_w"], c["time_b"] = t["L0_cond_time_w"], t["L0_cond_time_b"]
    c["steps"] = np.concatenate([np.tile(np.arange(EXPERTS, dtype=np.float32), (B, 1)),
                                 np.eye(B, dtype=np.float32)], 1)
    c["w1"] = np.concatenate([t["L0_cond_ew1"], t["L0_cond_sw1"][None]])
    c["w2"] = np.concatenate([t["L0_cond_ew2"], t["L0_cond_sw2"][None]])
    b1 = np.concatenate([t["L0_cond_eb1"], t["L0_cond_sb1"][None]]).reshape(EXPERTS + 1, KH, P)
    b2 = np.concatenate([t["L0_cond_eb2"], t["L0_cond_sb2"][None]]).reshape(EXPERTS + 1, KD, P)
    c["mix_biases"] = np.concatenate([b1, b2], 1).transpose(0, 2, 1)
    pair = [t[w].reshape(KD, P, PAIRS, 2 * DK).transpose(2, 1, 0, 3).reshape(PAIRS, P, L)
            for w in ("L0_attn_w_qs", "L0_attn_w_ks", "L0_attn_w_vs")]
    pair.append(t["L0_attn_w_out"].reshape(PAIRS, 2, P, D).transpose(0, 2, 1, 3).reshape(PAIRS, P, L))
    c["wqkvo"] = np.stack(pair, 2)
    c["wrel"] = t["L0_attn_w_rel_pos_k"].reshape(2, FP, PAIRS, 2 * DK).transpose(2, 1, 0, 3)
    positions = np.zeros((FEATS, DIST), np.float32)
    positions[:, 0:DIST - 1] = _positional_features(L, FEATS).T
    c["positions"] = positions.reshape(2, FP, 2, L).transpose(1, 0, 2, 3).reshape(FP, 4, L)
    biases = [t[n].reshape(PAIRS, 2, DK) for n in ("L0_attn_rel_embed_bias", "L0_attn_rel_pos_bias")]
    c["qbias"] = np.stack(biases, 1).reshape(PAIRS, 4, DK).transpose(0, 2, 1)
    c["b_out"] = t["L0_attn_b_out"].reshape(KD, P).T
    c["identity"] = np.eye(P, dtype=np.float32)
    c["wx"], c["wh"] = _gate_order(t["L0_cond2_Wx"]), _gate_order(t["L0_cond2_Wh"])
    c["gate_bias"] = _gate_order(t["L0_cond2_b"]).reshape(GC, P).T
    c["router_w"] = t["L0_ffn_router_w"]
    c["router_b"] = np.tile(t["L0_ffn_router_b"][None], (P, 1))
    c["expert_w"] = t["L0_ffn_expert_w"].transpose(1, 0, 2).reshape(D, FFN_EXPERTS * D)
    c["expert_b"] = np.tile(t["L0_ffn_expert_b"].reshape(1, FFN_EXPERTS * D), (2, 1))
    c["row_mask"] = np.eye(2, dtype=np.float32)
    c["count8"] = np.tile(np.arange(FFN_EXPERTS, dtype=np.float32), (P, 1))
    return c


def kernel(**inputs):
    import numpy as np
    import concourse.bacc as bacc
    from concourse.bass_utils import run_bass_kernel_spmd

    nc = bacc.Bacc("TRN2", target_bir_lowering=False, num_devices=1)
    arrays, args = {}, []
    for name, a in _layout({k: np.asarray(v) for k, v in inputs.items()}).items():
        arrays[f"in_{name}_dram"] = np.ascontiguousarray(a)
        args.append(nc.dram_tensor(f"in_{name}_dram", a.shape, F32, kind="ExternalInput").ap())
    args.append(nc.dram_tensor("out_0_dram", (B, L, D), F32, kind="ExternalOutput").ap())
    embedded_block_kernel(nc, *args)
    r = run_bass_kernel_spmd(nc, [arrays], core_ids=[0])
    return r.results[0]["out_0_dram"]
```
